# Optimizing a Trainium2 kernel written in Bass

```python
import numpy as np
import jax
import jax.numpy as jnp

def _softmax(x, axis=-1):
    return jax.nn.softmax(x, axis=axis)

def _gelu(x):
    return jax.nn.gelu(x, approximate=True)

def _silu(x):
    return jax.nn.silu(x)

def _sigmoid(x):
    return jax.nn.sigmoid(x)

def _layernorm(x, axis=-1, eps=1e-05):
    m = jnp.mean(x, axis=axis, keepdims=True)
    v = jnp.var(x, axis=axis, keepdims=True)
    return (x - m) / jnp.sqrt(v + eps)

def _scatter_add(tgt, idx, src, axis=0):
    return tgt.at[idx].add(src)

def _segment_sum(src, seg, n):
    return jax.ops.segment_sum(src, seg, n)
kernel_name = 'mk_vit_tower_d2_tok_img768_r4_566277'

def setup_inputs(seed: int=0):
    np.random.seed(seed)
    _w = jnp.asarray

    def _rec_inputs():
        import jax
        import jax.numpy as jnp
        _rk = jax.random.key(seed)
        x = -0.00016672 + 0.999947 * jax.random.normal(jax.random.fold_in(_rk, 1), (32, 3, 96, 96), jnp.float32)
        return x
    x = _rec_inputs()

    def _L0_tok_setup():
        import jax, jax.numpy as jnp
        import numpy as np
        PATCH = 16

        def _patchify(x, p):
            B, C, H, W = x.shape
            Hp, Wp = (H // p, W // p)
            xu = x.reshape(B, C, Hp, p, Wp, p).transpose(0, 1, 2, 4, 3, 5)
            num_patches = Hp * Wp
            return xu.reshape(B, num_patches, -1)
        key = jax.random.key(seed)
        k1, k2, k3 = jax.random.split(key, 3)
        B, C, H = (64, 3, 96)
        hidden = 192
        d = C * PATCH * PATCH
        x = jax.random.normal(k1, (B, C, H, H), dtype=jnp.float32)
        W = jax.random.normal(k2, (hidden, d), dtype=jnp.float32) * 0.02
        b = jax.random.normal(k3, (hidden,), dtype=jnp.float32) * 0.02
        return {'x': x, 'W': W, 'b': b}
    _L0_tok_all = _L0_tok_setup()
    _L0_tok_in = {k: v for k, v in _L0_tok_all.items() if k in ('W', 'b')}
    del _L0_tok_all

    def _L0_attn_setup():
        import jax, jax.numpy as jnp
        import numpy as np
        B, S, D, U = (4, 512, 192, 192)
        key = jax.random.key(seed)
        kx, kq, kk, kv = jax.random.split(key, 4)
        return {'x': jax.random.normal(kx, (B, S, D), dtype=jnp.float32), 'W_q': jax.random.normal(kq, (D, U), dtype=jnp.float32) * 0.05, 'W_k': jax.random.normal(kk, (D, U), dtype=jnp.float32) * 0.05, 'W_v': jax.random.normal(kv, (D, U), dtype=jnp.float32) * 0.05}
    _L0_attn_all = _L0_attn_setup()
    _L0_attn_in = {k: v for k, v in _L0_attn_all.items() if k in ('W_q', 'W_k', 'W_v')}
    del _L0_attn_all

    def _L0_ffn_setup():
        import jax, jax.numpy as jnp
        import numpy as np
        D = 192
        I = 768
        E = 8
        K = 2
        LIMIT = 10.0
        VOCAB = 8192

        def _expert(xf, W1, W2, W3):
            gate = jnp.minimum(xf @ W1, LIMIT)
            up = jnp.clip(xf @ W3, -LIMIT, LIMIT)
            return jax.nn.silu(gate) * up @ W2
        key = jax.random.key(seed)
        ks = jax.random.split(key, 10)
        s = 0.02
        return {'x': jax.random.normal(ks[0], (1, 512, D), dtype=jnp.float32), 'input_ids': jax.random.randint(ks[1], (1, 512), 0, VOCAB, dtype=jnp.int64), 'gate_w': jax.random.normal(ks[2], (D, E), dtype=jnp.float32) * s, 'gate_bias': jnp.zeros((E,), dtype=jnp.float32), 'w1': jax.random.normal(ks[3], (E, D, I), dtype=jnp.float32) * s, 'w2': jax.random.normal(ks[4], (E, I, D), dtype=jnp.float32) * s, 'w3': jax.random.normal(ks[5], (E, D, I), dtype=jnp.float32) * s, 'w1s': jax.random.normal(ks[6], (D, I), dtype=jnp.float32) * s, 'w2s': jax.random.normal(ks[7], (I, D), dtype=jnp.float32) * s, 'w3s': jax.random.normal(ks[8], (D, I), dtype=jnp.float32) * s}
    _L0_ffn_all = _L0_ffn_setup()
    _L0_ffn_in = {k: v for k, v in _L0_ffn_all.items() if k in ('input_ids', 'gate_w', 'gate_bias', 'w1', 'w2', 'w3', 'w1s', 'w2s', 'w3s')}
    del _L0_ffn_all

    def _L1_attn_setup():
        import jax, jax.numpy as jnp
        import numpy as np

        def _rotate_half(x):
            a, b = jnp.split(x, 2, axis=-1)
            return jnp.concatenate([-b, a], axis=-1)

        def _rope_tables(L, d, dtype):
            inv = 1.0 / 10000.0 ** (jnp.arange(0, d, 2, dtype=jnp.float32) / d)
            ang = jnp.arange(L, dtype=jnp.float32)[:, None] * inv[None, :]
            cos = jnp.repeat(jnp.cos(ang), 2, axis=-1)[None, :, None, :].astype(dtype)
            sin = jnp.repeat(jnp.sin(ang), 2, axis=-1)[None, :, None, :].astype(dtype)
            return (cos, sin)

        def _forward(X, Wq, Wk, Wv, Wu, Wg, Wo, prior_mu, prior_log_tau):
            B, L, D = X.shape
            h = prior_mu.shape[2]
            d = D // h
            eps = 1e-12
            q = (X @ Wq.T).reshape(B, L, h, d)
            k = (X @ Wk.T).reshape(B, L, h, d)
            v = (X @ Wv.T).reshape(B, L, h, d)
            u = (X @ Wu.T).reshape(B, L, h, d)
            gate = (X @ Wg.T).reshape(B, L, h, 3)
            t = jnp.arange(1, L + 1, dtype=X.dtype).reshape(1, L, 1, 1)
            log_tau = jnp.exp(jnp.clip(prior_log_tau, -50.0, 30.0))
            u_sum = jnp.cumsum(u, axis=1)
            bar_u = (log_tau * prior_mu + u_sum) / (log_tau + t)
            s_i = -jnp.sum(u * bar_u, axis=-1, keepdims=True) / np.float32(np.sqrt(d))
            cos, sin = _rope_tables(L, d, X.dtype)
            q = q * cos + _rotate_half(q) * sin
            k = k * cos + _rotate_half(k) * sin
            q = q / jnp.maximum(jnp.linalg.norm(q, axis=-1, keepdims=True), eps)
            k = k / jnp.maximum(jnp.linalg.norm(k, axis=-1, keepdims=True), eps)
            s_max = jax.lax.stop_gradient(jnp.max(s_i, axis=1, keepdims=True))
            exp_s = jnp.exp(s_i - s_max)
            E_t = jnp.cumsum(exp_s, axis=1)
            P_t = jnp.cumsum(s_i, axis=1)
            kv = jnp.einsum('blhd,blhe->blhde', k, v)
            F_t = jnp.cumsum(exp_s[..., None] * kv, axis=1)
            G_t = jnp.cumsum(s_i[..., None] * kv, axis=1)
            H_t = jnp.cumsum(kv, axis=1)
            sig1 = jax.nn.sigmoid(gate[..., 0:1])
            sigh = jax.nn.sigmoid(gate[..., 1:2])
            alpha = sigh / (E_t + eps)
            beta = (sig1 - sigh) / t
            gamma = -((beta * P_t + sigh) / t)
            M = alpha[..., None] * F_t + beta[..., None] * G_t + gamma[..., None] * H_t
            out = jnp.einsum('blhd,blhde->blhe', q, M)
            mu = jnp.mean(out, axis=-1, keepdims=True)
            var = jnp.mean(jnp.square(out - mu), axis=-1, keepdims=True)
            out = (out - mu) / jnp.sqrt(var + 1e-05)
            return out.reshape(B, L, D) @ Wo.T
        key = jax.random.key(seed)
        ks = jax.random.split(key, 7)
        B, L, D, h = (1, 256, 192, 12)
        d = D // h
        s = 0.02
        return {'X': jax.random.normal(ks[0], (B, L, D), jnp.float32), 'Wq': jax.random.normal(ks[1], (D, D), jnp.float32) * s, 'Wk': jax.random.normal(ks[2], (D, D), jnp.float32) * s, 'Wv': jax.random.normal(ks[3], (D, D), jnp.float32) * s, 'Wu': jax.random.normal(ks[4], (D, D), jnp.float32) * s, 'Wg': jax.random.normal(ks[5], (3 * h, D), jnp.float32) * s, 'Wo': jax.random.normal(ks[6], (D, D), jnp.float32) * s, 'prior_mu': jnp.zeros((1, 1, h, d), jnp.float32), 'prior_log_tau': jnp.zeros((1, 1, h, 1), jnp.float32)}
    _L1_attn_all = _L1_attn_setup()
    _L1_attn_in = {k: v for k, v in _L1_attn_all.items() if k in ('Wq', 'Wk', 'Wv', 'Wu', 'Wg', 'Wo', 'prior_mu', 'prior_log_tau')}
    del _L1_attn_all

    def _L1_ffn_setup():
        import jax, jax.numpy as jnp
        import numpy as np
        B, S, H, I = (4, 512, 192, 384)
        E, K = (3, 2)
        INIT = 0.02

        def _expert(x, gw, uw, dw):
            return jax.nn.silu(x @ gw) * (x @ uw) @ dw
        key = jax.random.key(seed)
        ks = jax.random.split(key, 8)
        f32 = jnp.float32
        return {'x': jax.random.normal(ks[0], (B, S, H), f32), 'shared_gate': jax.random.normal(ks[1], (H, I), f32) * INIT, 'shared_up': jax.random.normal(ks[2], (H, I), f32) * INIT, 'shared_down': jax.random.normal(ks[3], (I, H), f32) * INIT, 'routed_gate': jax.random.normal(ks[4], (E, H, I), f32) * INIT, 'routed_up': jax.random.normal(ks[5], (E, H, I), f32) * INIT, 'routed_down': jax.random.normal(ks[6], (E, I, H), f32) * INIT, 'router_w': jax.random.normal(ks[7], (H, E), f32) * INIT, 'routing_bias': jnp.zeros((E,), f32)}
    _L1_ffn_all = _L1_ffn_setup()
    _L1_ffn_in = {k: v for k, v in _L1_ffn_all.items() if k in ('shared_gate', 'shared_up', 'shared_down', 'routed_gate', 'routed_up', 'routed_down', 'router_w', 'routing_bias')}
    del _L1_ffn_all
    return {'x': x, 'L0_tok_W': _L0_tok_in['W'], 'L0_tok_b': _L0_tok_in['b'], 'L0_attn_W_q': _L0_attn_in['W_q'], 'L0_attn_W_k': _L0_attn_in['W_k'], 'L0_attn_W_v': _L0_attn_in['W_v'], 'L0_ffn_input_ids': _L0_ffn_in['input_ids'], 'L0_ffn_gate_w': _L0_ffn_in['gate_w'], 'L0_ffn_gate_bias': _L0_ffn_in['gate_bias'], 'L0_ffn_w1': _L0_ffn_in['w1'], 'L0_ffn_w2': _L0_ffn_in['w2'], 'L0_ffn_w3': _L0_ffn_in['w3'], 'L0_ffn_w1s': _L0_ffn_in['w1s'], 'L0_ffn_w2s': _L0_ffn_in['w2s'], 'L0_ffn_w3s': _L0_ffn_in['w3s'], 'L1_attn_Wq': _L1_attn_in['Wq'], 'L1_attn_Wk': _L1_attn_in['Wk'], 'L1_attn_Wv': _L1_attn_in['Wv'], 'L1_attn_Wu': _L1_attn_in['Wu'], 'L1_attn_Wg': _L1_attn_in['Wg'], 'L1_attn_Wo': _L1_attn_in['Wo'], 'L1_attn_prior_mu': _L1_attn_in['prior_mu'], 'L1_attn_prior_log_tau': _L1_attn_in['prior_log_tau'], 'L1_ffn_shared_gate': _L1_ffn_in['shared_gate'], 'L1_ffn_shared_up': _L1_ffn_in['shared_up'], 'L1_ffn_shared_down': _L1_ffn_in['shared_down'], 'L1_ffn_routed_gate': _L1_ffn_in['routed_gate'], 'L1_ffn_routed_up': _L1_ffn_in['routed_up'], 'L1_ffn_routed_down': _L1_ffn_in['routed_down'], 'L1_ffn_router_w': _L1_ffn_in['router_w'], 'L1_ffn_routing_bias': _L1_ffn_in['routing_bias']}

def reference(x, L0_tok_W, L0_tok_b, L0_attn_W_q, L0_attn_W_k, L0_attn_W_v, L0_ffn_input_ids, L0_ffn_gate_w, L0_ffn_gate_bias, L0_ffn_w1, L0_ffn_w2, L0_ffn_w3, L0_ffn_w1s, L0_ffn_w2s, L0_ffn_w3s, L1_attn_Wq, L1_attn_Wk, L1_attn_Wv, L1_attn_Wu, L1_attn_Wg, L1_attn_Wo, L1_attn_prior_mu, L1_attn_prior_log_tau, L1_ffn_shared_gate, L1_ffn_shared_up, L1_ffn_shared_down, L1_ffn_routed_gate, L1_ffn_routed_up, L1_ffn_routed_down, L1_ffn_router_w, L1_ffn_routing_bias):
    import jax
    import jax.numpy as jnp

    def _L0_tok_ref(x, W, b):
        import jax, jax.numpy as jnp
        import numpy as np
        PATCH = 16

        def _patchify(x, p):
            B, C, H, W = x.shape
            Hp, Wp = (H // p, W // p)
            xu = x.reshape(B, C, Hp, p, Wp, p).transpose(0, 1, 2, 4, 3, 5)
            num_patches = Hp * Wp
            return xu.reshape(B, num_patches, -1)
        patches = _patchify(x, PATCH)
        return jnp.einsum('bnd,hd->bnh', patches, W) + b

    def _L0_attn_ref(x, W_q, W_k, W_v):
        import jax, jax.numpy as jnp
        import numpy as np
        B, S, D, U = (4, 512, 192, 192)
        q = jnp.einsum('bsd,du->bsu', x, W_q)
        k = jnp.einsum('bsd,du->bsu', x, W_k)
        v = jnp.einsum('bsd,du->bsu', x, W_v)
        scale = 1.0 / jnp.sqrt(jnp.asarray(U, dtype=x.dtype))
        scores = jnp.einsum('bqu,bku->bqk', q, k) * scale
        attn = jax.nn.softmax(scores, axis=-1)
        return jnp.einsum('bqk,bku->bqu', attn, v)

    def _L0_ffn_ref(x, input_ids, gate_w, gate_bias, w1, w2, w3, w1s, w2s, w3s):
        import jax, jax.numpy as jnp
        import numpy as np
        D = 192
        I = 768
        E = 8
        K = 2
        LIMIT = 10.0
        VOCAB = 8192

        def _expert(xf, W1, W2, W3):
            gate = jnp.minimum(xf @ W1, LIMIT)
            up = jnp.clip(xf @ W3, -LIMIT, LIMIT)
            return jax.nn.silu(gate) * up @ W2
        B, T, _ = x.shape
        flat = x.reshape(-1, D)
        N = flat.shape[0]
        scores = jnp.sqrt(jax.nn.softplus(flat @ gate_w))
        routed_scores = scores + gate_bias
        _, indices = jax.lax.top_k(routed_scores, K)
        weights = jnp.take_along_axis(scores, indices, axis=1)
        weights = weights / jnp.clip(weights.sum(axis=-1, keepdims=True), 1e-06)
        combine = jnp.zeros((N, E), dtype=weights.dtype)
        combine = combine.at[jnp.arange(N)[:, None], indices].add(weights)
        y = _expert(flat, w1s, w2s, w3s)
        gate_h = jnp.minimum(jnp.einsum('td,edi->eti', flat, w1), LIMIT)
        up_h = jnp.clip(jnp.einsum('td,edi->eti', flat, w3), -LIMIT, LIMIT)
        h = jax.nn.silu(gate_h) * up_h
        out_e = jnp.einsum('eti,eid->etd', h, w2)
        routed = jnp.einsum('etd,te->td', out_e, combine)
        return (y + routed).reshape(B, T, D)

    def _L1_attn_ref(X, Wq, Wk, Wv, Wu, Wg, Wo, prior_mu, prior_log_tau):
        import jax, jax.numpy as jnp
        import numpy as np

        def _rotate_half(x):
            a, b = jnp.split(x, 2, axis=-1)
            return jnp.concatenate([-b, a], axis=-1)

        def _rope_tables(L, d, dtype):
            inv = 1.0 / 10000.0 ** (jnp.arange(0, d, 2, dtype=jnp.float32) / d)
            ang = jnp.arange(L, dtype=jnp.float32)[:, None] * inv[None, :]
            cos = jnp.repeat(jnp.cos(ang), 2, axis=-1)[None, :, None, :].astype(dtype)
            sin = jnp.repeat(jnp.sin(ang), 2, axis=-1)[None, :, None, :].astype(dtype)
            return (cos, sin)

        def _forward(X, Wq, Wk, Wv, Wu, Wg, Wo, prior_mu, prior_log_tau):
            B, L, D = X.shape
            h = prior_mu.shape[2]
            d = D // h
            eps = 1e-12
            q = (X @ Wq.T).reshape(B, L, h, d)
            k = (X @ Wk.T).reshape(B, L, h, d)
            v = (X @ Wv.T).reshape(B, L, h, d)
            u = (X @ Wu.T).reshape(B, L, h, d)
            gate = (X @ Wg.T).reshape(B, L, h, 3)
            t = jnp.arange(1, L + 1, dtype=X.dtype).reshape(1, L, 1, 1)
            log_tau = jnp.exp(jnp.clip(prior_log_tau, -50.0, 30.0))
            u_sum = jnp.cumsum(u, axis=1)
            bar_u = (log_tau * prior_mu + u_sum) / (log_tau + t)
            s_i = -jnp.sum(u * bar_u, axis=-1, keepdims=True) / np.float32(np.sqrt(d))
            cos, sin = _rope_tables(L, d, X.dtype)
            q = q * cos + _rotate_half(q) * sin
            k = k * cos + _rotate_half(k) * sin
            q = q / jnp.maximum(jnp.linalg.norm(q, axis=-1, keepdims=True), eps)
            k = k / jnp.maximum(jnp.linalg.norm(k, axis=-1, keepdims=True), eps)
            s_max = jax.lax.stop_gradient(jnp.max(s_i, axis=1, keepdims=True))
            exp_s = jnp.exp(s_i - s_max)
            E_t = jnp.cumsum(exp_s, axis=1)
            P_t = jnp.cumsum(s_i, axis=1)
            kv = jnp.einsum('blhd,blhe->blhde', k, v)
            F_t = jnp.cumsum(exp_s[..., None] * kv, axis=1)
            G_t = jnp.cumsum(s_i[..., None] * kv, axis=1)
            H_t = jnp.cumsum(kv, axis=1)
            sig1 = jax.nn.sigmoid(gate[..., 0:1])
            sigh = jax.nn.sigmoid(gate[..., 1:2])
            alpha = sigh / (E_t + eps)
            beta = (sig1 - sigh) / t
            gamma = -((beta * P_t + sigh) / t)
            M = alpha[..., None] * F_t + beta[..., None] * G_t + gamma[..., None] * H_t
            out = jnp.einsum('blhd,blhde->blhe', q, M)
            mu = jnp.mean(out, axis=-1, keepdims=True)
            var = jnp.mean(jnp.square(out - mu), axis=-1, keepdims=True)
            out = (out - mu) / jnp.sqrt(var + 1e-05)
            return out.reshape(B, L, D) @ Wo.T
        return _forward(X, Wq, Wk, Wv, Wu, Wg, Wo, prior_mu, prior_log_tau)

    def _L1_ffn_ref(x, shared_gate, shared_up, shared_down, routed_gate, routed_up, routed_down, router_w, routing_bias):
        import jax, jax.numpy as jnp
        import numpy as np
        B, S, H, I = (4, 512, 192, 384)
        E, K = (3, 2)
        INIT = 0.02

        def _expert(x, gw, uw, dw):
            return jax.nn.silu(x @ gw) * (x @ uw) @ dw
        shared_out = _expert(x, shared_gate, shared_up, shared_down)
        routing_probs = jax.nn.sigmoid(x @ router_w + routing_bias)
        scores, indices = jax.lax.top_k(routing_probs, K)
        scores = scores / scores.sum(axis=-1, keepdims=True)
        combine_w = (jax.nn.one_hot(indices, E, dtype=x.dtype) * scores[..., None]).sum(axis=-2)
        g = jnp.einsum('bsh,ehi->ebsi', x, routed_gate)
        u = jnp.einsum('bsh,ehi->ebsi', x, routed_up)
        h = jax.nn.silu(g) * u
        out_e = jnp.einsum('ebsi,eih->ebsh', h, routed_down)
        combined = jnp.einsum('ebsh,bse->bsh', out_e, combine_w)
        return shared_out + combined
    h = _L0_tok_ref(x, L0_tok_W, L0_tok_b)
    h = h + _L0_attn_ref(_layernorm(h, axis=-1), L0_attn_W_q, L0_attn_W_k, L0_attn_W_v)
    h = h + _L0_ffn_ref(_layernorm(h, axis=-1), L0_ffn_input_ids, L0_ffn_gate_w, L0_ffn_gate_bias, L0_ffn_w1, L0_ffn_w2, L0_ffn_w3, L0_ffn_w1s, L0_ffn_w2s, L0_ffn_w3s)
    h = h + _L1_attn_ref(_layernorm(h, axis=-1), L1_attn_Wq, L1_attn_Wk, L1_attn_Wv, L1_attn_Wu, L1_attn_Wg, L1_attn_Wo, L1_attn_prior_mu, L1_attn_prior_log_tau)
    h = h + _L1_ffn_ref(_layernorm(h, axis=-1), L1_ffn_shared_gate, L1_ffn_shared_up, L1_ffn_shared_down, L1_ffn_routed_gate, L1_ffn_routed_up, L1_ffn_routed_down, L1_ffn_router_w, L1_ffn_routing_bias)
    return h

_drawn_inputs = setup_inputs


def setup_inputs(seed=0):
    import zlib

    import numpy as np

    out = dict(_drawn_inputs(seed))
    spreads = {'L0_ffn_gate_bias': (0.0, 0.294),
     'L1_attn_prior_mu': (0.0, 0.749),
     'L1_attn_prior_log_tau': (0.0, 0.8),
     'L1_ffn_routing_bias': (0.0, 0.8)}
    factors = {'L0_ffn_gate_w': 3.033,
     'L1_attn_Wg': 6.741,
     'L1_ffn_routed_gate': 3.017,
     'L1_ffn_routed_up': 2.982,
     'L1_ffn_routed_down': 2.984,
     'L1_ffn_router_w': 5.299}
    for name, (base, spread) in spreads.items():
        noise = np.random.default_rng([zlib.crc32(name.encode()), seed]).standard_normal(out[name].shape)
        drawn = base * np.exp(spread * noise) if base else spread * noise
        out[name] = jnp.asarray(drawn.astype(out[name].dtype))
    for name, factor in factors.items():
        out[name] = (out[name] * factor).astype(out[name].dtype)
    return out
```

```python
from contextlib import ExitStack

import concourse.bass as bass
from concourse import mybir

F32 = mybir.dt.float32
F32R = mybir.dt.float32r
ALU = mybir.AluOpType
ACT = mybir.ActivationFunctionType
AX = mybir.AxisListType

IMAGES, CHANNELS, SIDE, PATCH = 32, 3, 96, 16
SEQ = (SIDE // PATCH) ** 2
TOK = IMAGES * SEQ
D = 192
P = 128
TILES = TOK // P
CH = 3
CHW = TOK // CH
PATCH_K = CHANNELS * PATCH * PATCH // P
GI = 3
GW = GI * SEQ
GROUPS = -(-IMAGES // GI)
XW = GROUPS * GW
BATCHES = [(0, 4), (4, 8), (8, GROUPS)]
HALF = D // 2
HEADS = 12
HD = D // HEADS
QKVG = 4 * D + 2 * HEADS
L1H = QKVG // 2 // 2 * 2
SLOT = 64
E0, F0 = 8, 768
E1, F1 = 3, 384
E1P = 4
LIMIT = 10.0
SILU_LIMIT = 9.999546021312976
NWA = 3 * D + E0 + E1P
EPS = 1e-5

C_ID = 0
C_MASK = C_ID + P
C_TRI = C_MASK + GW
C_COS = C_TRI + GW
C_SIN = C_COS + HD
C_T = C_SIN + HD
C_RT = C_T + 1
C_NRT = C_RT + 1
C_LOW = C_NRT + 1
NCONST = C_LOW + E0 * E0
R_TOKB = 0
R_GB = R_TOKB + D
R_RB = R_GB + E0
R_MU = R_RB + E1P
R_TAU = R_MU + D
NROWS = R_TAU + HEADS


class Moe:

    def __init__(self, experts, width, clip):
        self.works = experts + 1
        self.width = width
        self.clip = clip
        self.fc = width // P
        self.cols = 4 * width + self.fc * D
        self.pieces = 4 + 2


MOE0, MOE1 = Moe(E0, F0, True), Moe(E1, F1, False)


class Steps:

    def __init__(self, eng, sem):
        self.eng, self.sem, self.n = eng, sem, 0

    def step(self, ins):
        ins.then_inc(self.sem, 1)
        self.n += 1
        return self.n

    def settle(self, n=None):
        self.eng.wait_ge(self.sem, self.n if n is None else n)

    def link(self, ins):
        self.step(ins)
        self.settle()


def tower(nc, patches, tokw, consts, rows, wa, l1w, wo, moe0w, moe1w, out):
    with ExitStack() as ctx:
        def sb(name, shape, dt=F32, scope=ctx):
            return scope.enter_context(nc.sbuf_tensor(name, shape, dt))

        def sem(name):
            return ctx.enter_context(nc.semaphore(name))

        bank = [ctx.enter_context(nc.psum_tensor(f"bank{i}", [P, 512], F32)) for i in range(8)]

        H = sb("H", [P, TILES, D])
        Y = sb("Y", [P, TILES, 256])
        X01h = sb("X01h", [P, XW], F32R)
        X01l = sb("X01l", [P, XW], F32R)
        X2h = sb("X2h", [P, XW], F32R)
        X2l = sb("X2l", [64, XW], F32R)
        const = sb("const", [P, NCONST])
        row = sb("row", [P, NROWS])
        WAh = sb("WAh", [P, NWA], F32R)
        WAl = sb("WAl", [P, NWA], F32R)
        WA2 = sb("WA2", [P, NWA], F32R)
        L1h = sb("L1h", [P, QKVG], F32R)
        L1l = sb("L1l", [P, QKVG], F32R)
        L12 = sb("L12", [P, QKVG], F32R)
        wo_sb = sb("wo_sb", [HALF, 2, D])
        stat = sb("stat", [P, TILES, 6])
        mv = sb("mv", [P, TILES, 2])
        ve = sb("ve", [P, TILES])
        sd = sb("sd", [P, TILES])
        rstd = sb("rstd", [P, TILES])
        comb = sb("comb", [P, TILES, E0])
        comb1 = sb("comb1", [P, TILES, E1])

        ident = const[:, C_ID:C_ID + P]
        amask = const[0:GW, C_MASK:C_MASK + GW]
        tri = const[0:GW, C_TRI:C_TRI + GW]

        tau = sb("tau", [GW, HEADS])
        tmu = sb("tmu", [GW, D])
        tden = sb("tden", [GW, HEADS])
        sT = sb("sT", [HEADS, XW])
        smax = sb("smax", [HEADS, GROUPS * GI])
        rt = [sb(f"rt{i}", [P, TILES * E0]) for i in range(6)]
        rk = [sb(f"rk{i}", [P, TILES * E0 * E0]) for i in range(2)]
        rsum = [sb(f"rsum{i}", [P, TILES]) for i in range(2)]

        r1a, r1b = ExitStack(), ExitStack()
        W0 = []
        with r1a:
            for b in range(2):
                W0.append(dict(
                    stage=sb(f"stage{b}", [P, MOE0.cols], F32, r1a),
                    h=sb(f"w0h{b}", [P, 2, F0], F32R, r1a), l=sb(f"w0l{b}", [P, 2, F0], F32R, r1a),
                    t=sb(f"w0t{b}", [P, 2, F0], F32R, r1a),
                    dh=sb(f"d0h{b}", [P, MOE0.fc, D], F32R, r1a), dl=sb(f"d0l{b}", [P, MOE0.fc, D], F32R, r1a)))
            with ExitStack() as s:
                patch = sb("patch", [P, PATCH_K * TOK], F32, s)
                tokw_sb = sb("tokw_sb", [P, PATCH_K, D], F32, s)
            with ExitStack() as s:
                qT = sb("qT", [HALF, 2, XW], F32, s)
                kT = sb("kT", [HALF, 2, XW], F32, s)
                V = sb("V", [GW, GROUPS, D], F32, s)
                Pm = sb("Pm", [GW, GROUPS, GW], F32, s)
                PT = sb("PT", [GW, GROUPS, GW], F32, s)
                oT = sb("oT", [HALF, 2, XW], F32, s)
                mx = sb("mx", [GW, GROUPS], F32, s)
                rs = sb("rs", [GW, GROUPS], F32, s)
                rr = sb("rr", [GW, GROUPS], F32, s)
            with ExitStack() as s:
                A0 = moe_buffers(sb, s, MOE0, "a0")
        with r1b:
            QK = sb("QK", [GW, GROUPS, QKVG], F32, r1b)
            rotA = sb("rotA", [GW, 4, 2 * D], F32, r1b)
            rotB = sb("rotB", [GW, 4, 2 * D], F32, r1b)
            qw = sb("qw", [GW, 4, HEADS, SLOT], F32, r1b)
            kw = sb("kw", [GW, 4, HEADS, SLOT], F32, r1b)
            AT = sb("AT", [GW, HEADS, GW], F32, r1b)
            ES = sb("ES", [GW, GROUPS, 2 * HEADS], F32, r1b)
            SG = sb("SG", [GW, GROUPS, 2 * HEADS], F32, r1b)
            CO = sb("CO", [GW, 3, GROUPS, HEADS], F32, r1b)
            fill = (2 * (MOE0.cols + 6 * F0 + 2 * MOE0.fc * D) - GROUPS * QKVG - 16 * D - 8 * HEADS * SLOT
                    - HEADS * GW - 7 * GROUPS * HEADS)
            sb("fill", [P, fill], F32, r1b)
            W1 = []
            for b in range(2):
                W1.append(dict(
                    stage=sb(f"stage1{b}", [P, MOE1.cols], F32, r1b),
                    h=sb(f"w1h{b}", [P, 2, F1], F32R, r1b), l=sb(f"w1l{b}", [P, 2, F1], F32R, r1b),
                    t=sb(f"w1t{b}", [P, 2, F1], F32R, r1b),
                    dh=sb(f"d1h{b}", [P, MOE1.fc, D], F32R, r1b), dl=sb(f"d1l{b}", [P, MOE1.fc, D], F32R, r1b)))
            CK = sb("CK", [GW, 2, 4, HEADS], F32, r1b)
            CQ = sb("CQ", [GW, 3, 4, HEADS], F32, r1b)
            nrm = sb("nrm", [GW, 4, 2 * HEADS], F32, r1b)
            rn = sb("rn", [GW, 4, 2 * HEADS], F32, r1b)
            qkT = sb("qkT", [P, 12, GW], F32, r1b)
        with ExitStack() as s:
            A1 = moe_buffers(sb, s, MOE1, "a1")
        ld_patch = [sem(f"ld_patch{j}") for j in range(5)]
        ld_tokw, ld_const, ld_row, ld_wo = sem("ld_tokw"), sem("ld_const"), sem("ld_row"), sem("ld_wo")
        ld_stage = [sem(f"ld_stage{b}") for b in range(2)]
        ld_stage1 = [sem(f"ld_stage1{b}") for b in range(2)]
        pads = sem("pads")
        split_hi, split_lo = sem("split_hi"), sem("split_lo")
        tok_done, tok_h = sem("tok_done"), sem("tok_h")
        dve_step, act_step, pool_step = sem("dve_step"), sem("act_step"), sem("pool_step")
        ln_var, ln_sd, ln_y, ln_xt, ln_hi, ln_lo = (sem("ln_" + s) for s in ("var", "sd", "y", "xt", "hi", "lo"))
        proj_done = sem("proj_done")
        proj_out = [sem("proj_act"), sem("proj_dve")]
        a0_s, a0_shift, a0_exp, a0_p, a0_pt, a0_ptc, a0_o, a0_back, a0_h = (
            sem("a0_" + s) for s in ("s", "shift", "exp", "p", "pt", "ptc", "o", "back", "h"))
        a0_oc = [sem("a0_oc_act"), sem("a0_oc_dve")]
        rt_z, rt_neg, rt_e, rt_u, rt_ln, rt_sp, rt_sc = (
            sem("rt_" + s) for s in ("z", "neg", "e", "u", "ln", "sp", "sc"))
        rt1_z, rt1_b, rt1_p = sem("rt1_z"), sem("rt1_b"), sem("rt1_p")
        moe_sems = []
        for m in range(2):
            moe_sems.append({k: sem(f"moe{m}_{k}") for k in (
                "w_hi", "w_lo", "gu_ready", "silu_ready", "clip_ready", "h_ready", "hh_ready", "hl_ready",
                "down_ready", "acc_done")})
        l1_proj = sem("l1_proj")
        l1_out = [sem("l1_out_act"), sem("l1_out_dve")]
        (l1_us, l1_s, l1_st, l1_sh, l1_ex, l1_et, l1_es, l1_cum, l1_sig, l1_tau, l1_co) = (
            sem("l1_" + s) for s in ("us", "s", "st", "sh", "ex", "et", "es", "cum", "sig", "tau", "co"))
        (l1_rope, l1_sw, l1_sq, l1_n2, l1_nr, l1_cq, l1_qw, l1_kw, l1_T, l1_Tca, l1_Tcd, l1_A, l1_Am,
         l1_O, l1_Oc, l1_cen, l1_csq, l1_var, l1_std, l1_on, l1_oT, l1_oTc, l1_f, l1_h) = (
            sem("l1_" + s) for s in ("rope", "sw", "sq", "n2", "nr", "cq", "qw", "kw", "T", "Tca", "Tcd",
                                     "A", "Am", "O", "Oc", "cen", "csq", "var", "std", "on", "oT", "oTc", "f", "h"))
        pad_w = sem("pad_w")
        stored = sem("stored")

        def terms(weights, wcols, xcols):
            wh, wl, w2 = weights
            return [(X01h[:, xcols], wh[wcols]), (X01h[:, xcols], wl[wcols]), (X01l[:, xcols], wh[wcols]),
                    (X2h[:, xcols], w2[wcols]), (X2l[:, xcols], w2[(slice(0, 64),) + wcols[1:]])]

        def wcols2(a, b):
            return (slice(0, P), slice(a, b))

        OT = Y[0:HALF].rearrange("p a b -> p (a b)").rearrange("p (h n) -> p h n", h=2)
        W1b = Y[0:GW].rearrange("p a b -> p (a b)")[:, 0:GROUPS * D].rearrange("p (g d) -> p g d", d=D)

        block = ctx.enter_context(nc.Block())
        PBLK = [(2 * j, min(2 * j + 2, TILES)) for j in range(5)]

        @block.sync
        def _(sp):
            sp.dma_start(tokw_sb[:], tokw).then_inc(ld_tokw, 16)
            for j, (t0, t1) in enumerate(PBLK):
                a, b = t0 * P * PATCH_K, t1 * P * PATCH_K
                sp.dma_start(patch[:, a:b], patches[:, a:b]).then_inc(ld_patch[j], 16)
                if j == 0:
                    sp.dma_start(row[:], rows).then_inc(ld_row, 16)
                    sp.dma_start(const[:], consts).then_inc(ld_const, 16)
            sp.dma_start(W0[0]["stage"][:, 0:2 * NWA], wa).then_inc(ld_stage[0], 16)
            sp.dma_start(W0[1]["stage"][:, 0:2 * QKVG], l1w).then_inc(ld_stage[1], 16)
            sp.dma_start(wo_sb[:], wo).then_inc(ld_wo, 16)
            for n in range(MOE0.works):
                if n < 2:
                    sp.wait_ge(split_lo, 2 * (n + 1))
                else:
                    sp.wait_ge(moe_sems[0]["w_lo"], MOE0.pieces * (n - 1))
                sp.dma_start(W0[n % 2]["stage"][:], moe0w[n]).then_inc(ld_stage[n % 2], 16)
            sp.wait_ge(moe_sems[0]["acc_done"], MOE0.works * TILES)
            for n in range(MOE1.works):
                if n >= 2:
                    sp.wait_ge(moe_sems[1]["w_lo"], MOE1.pieces * (n - 1))
                sp.dma_start(W1[n % 2]["stage"][:], moe1w[n]).then_inc(ld_stage1[n % 2], 16)
            last = (MOE1.works - 1) * TILES
            for c in range(CH):
                sp.wait_ge(moe_sems[1]["acc_done"], last + 3 * (c + 1))
                sp.dma_start(out.rearrange("(t p) d -> p t d", p=P)[:, 3 * c:3 * c + 3, :],
                             H[:, 3 * c:3 * c + 3, :]).then_inc(stored, 16)
            sp.wait_ge(stored, 16 * CH)

        def moe_pe(pe, m, W, A, S, n, odd, first):
            M, (g0, g1), (u0, u1), (d0, d1) = m, (0, 1), (2, 3), (4, 5)
            FC = M.fc

            def gate_up(c):
                if c == 0:
                    pe.wait_ge(S["w_lo"], n * M.pieces + M.pieces)
                for fc in range(FC):
                    par = ((3 * odd + c) * FC + fc) % 2
                    if not (first and c == 0 and fc < 2):
                        pe.wait_ge(S["h_ready"], n * (3 * FC) + (c * FC + fc - 1))
                    for mat, bk in ((0, (g0, g1)[par]), (1, (u0, u1)[par])):
                        w = W[odd]
                        ts = terms((w["h"][:], w["l"][:], w["t"][:]),
                                   (slice(0, P), mat, slice(fc * P, fc * P + P)), slice(c * CHW, c * CHW + CHW))
                        for i, (x, wt) in enumerate(ts):
                            last = nc.tensor.matmul(bank[bk][:, 0:CHW], wt, x, start=(i == 0), stop=(i == 4))
                    last.then_inc(S["gu_ready"], 1)

            def down(nn, o, c):
                q = (o * 3 + c) % 2
                pe.wait_ge(S["hl_ready"], nn * (3 * FC) + (c + 1) * FC)
                for t in range(3):
                    dpar = (q + t) % 2
                    if not (first and c == 0 and t < 2 and nn is n):
                        pe.wait_ge(S["acc_done"], nn * 9 + (3 * c + t - 1))
                    w = W[o]
                    cols = slice(t * P, t * P + P)
                    k = 0
                    for fc in range(FC):
                        hh, hl = A["hh"][q][:, fc, cols], A["hl"][q][:, fc, cols]
                        for lhs, rhs in ((hh, w["dh"]), (hh, w["dl"]), (hl, w["dh"])):
                            last = nc.tensor.matmul(bank[(d0, d1)[dpar]][:, 0:D], lhs, rhs[:, fc, :],
                                                    start=(k == 0), stop=(k == 3 * FC - 1))
                            k += 1
                    last.then_inc(S["down_ready"], 1)

            gate_up(0)
            if not first:
                down(n - 1, 1 - odd, 2)
            gate_up(1)
            down(n, odd, 0)
            gate_up(2)
            down(n, odd, 1)
            return down

        def split_hi_piece(m, W, odd, i):
            w, F = W[odd], m.width
            if i < 4:
                mat, two = i // 2, i % 2
                src = w["stage"][:, (2 * mat + two) * F:(2 * mat + two + 1) * F]
                return src, (w["t"] if two else w["h"])[:, mat, :]
            half = m.fc // 2 if m.fc % 2 == 0 else m.fc - 1
            a, b = (0, half) if i == 4 else (half, m.fc)
            src = w["stage"][:, 4 * F + a * D:4 * F + b * D].rearrange("p (f d) -> p f d", d=D)
            return src, w["dh"][:, a:b, :]

        def split_lo_piece(m, W, odd, i):
            w, F = W[odd], m.width
            src, hi = split_hi_piece(m, W, odd, i)
            if i < 4:
                mat, two = i // 2, i % 2
                if two:
                    t = w["t"][64:P, mat, :]
                    return src[64:P], t, t
                return src, hi, w["l"][:, mat, :]
            half = m.fc // 2 if m.fc % 2 == 0 else m.fc - 1
            a, b = (0, half) if i == 4 else (half, m.fc)
            return src, hi, w["dl"][:, a:b, :]

        def moe_weights_act(act, m, W, S, L, n, odd, i, used, n_pairs):
            if i == 0:
                act.wait_ge(L[odd], n_pairs)
                if used is not None:
                    act.wait_ge(S["down_ready"], used)
            src, hi = split_hi_piece(m, W, odd, i)
            nc.scalar.activation(hi, src, ACT.Copy).then_inc(S["w_hi"], 1)

        def moe_weights_pool(pool, m, W, S, n, odd):
            for i in range(m.pieces):
                if i or not isinstance(n, int) or n:
                    pool.wait_ge(S["w_lo"], n * m.pieces + i)
                pool.wait_ge(S["w_hi"], n * m.pieces + (i + 1))
                src, hi, dst = split_lo_piece(m, W, odd, i)
                nc.gpsimd.tensor_tensor(dst, src, hi.bitcast(F32), ALU.subtract).then_inc(S["w_lo"], 1)

        def moe_act(act, m, W, A, S, L, n, odd, first, last, n_pairs):
            FC = m.fc
            for c in range(CH):
                for fc in range(FC):
                    par = ((3 * odd + c) * FC + fc) % 2
                    k1 = c * FC + fc + 1
                    act.wait_ge(S["gu_ready"], n * (3 * FC) + k1)
                    if not (first and k1 <= 2):
                        act.wait_ge(S["h_ready"], n * (3 * FC) + (k1 - 2))
                    nc.scalar.activation(A["s"][par][:], bank[par][:, 0:CHW], ACT.Silu).then_inc(S["silu_ready"], 1)
                    if not (first and k1 == 1):
                        moe_high(act, m, A, S, n, odd, c * FC + fc - 1)
                    i = (c - 1) * FC + fc
                    if not last and 0 <= i < m.pieces:
                        used = n * 9 if not first else None
                        moe_weights_act(act, m, W, S, L, n + 1, 1 - odd, i, used, n_pairs)

        def moe_high(act, m, A, S, n, odd, k):
            FC = m.fc
            kk = (3 * odd * FC + k) % (6 * FC)
            q, fc, par = (kk // FC) % 2, kk % FC, kk % 2
            act.wait_ge(S["h_ready"], n * (3 * FC) + (k + 1))
            nc.scalar.activation(A["hh"][q][:, fc, :], A["hf"][par][:], ACT.Copy).then_inc(S["hh_ready"], 1)

        def moe_low(dve, m, A, S, n, odd, k):
            FC = m.fc
            kk = (3 * odd * FC + k) % (6 * FC)
            q, fc, par = (kk // FC) % 2, kk % FC, kk % 2
            dve.wait_ge(S["hh_ready"], n * (3 * FC) + (k + 1))
            nc.vector.tensor_tensor(A["hl"][q][:, fc, :], A["hf"][par][:], A["hh"][q][:, fc, :].bitcast(F32),
                                    ALU.subtract).then_inc(S["hl_ready"], 1)

        def moe_acc(dve, m, S, n, odd, c, weight):
            q = (3 * odd + c) % 2
            for t in range(3):
                tile = 3 * c + t
                dve.wait_ge(S["down_ready"], n * 9 + (tile + 1))
                if weight is None:
                    nc.vector.tensor_tensor(H[:, tile, :], bank[4 + (q + t) % 2][:, 0:D], H[:, tile, :],
                                            ALU.add).then_inc(S["acc_done"], 1)
                else:
                    dve.wait_ge(S["acc_done"], n * 9 + (tile - 8))
                    nc.vector.scalar_tensor_tensor(
                        out=H[:, tile, :], in0=bank[4 + (q + t) % 2][:, 0:D], scalar=weight(tile),
                        in1=H[:, tile, :], op0=ALU.mult, op1=ALU.add).then_inc(S["acc_done"], 1)

        def moe_dve(dve, m, A, S, n, odd, first, weight, before):
            FC = m.fc
            for c in range(CH):
                for fc in range(FC):
                    par = ((3 * odd + c) * FC + fc) % 2
                    k1 = c * FC + fc + 1
                    dve.wait_ge(S["gu_ready"], n * (3 * FC) + k1)
                    if m.clip:
                        nc.vector.tensor_scalar(A["t"][par][:], bank[2 + par][:, 0:CHW], LIMIT, -LIMIT, ALU.min,
                                                ALU.max).then_inc(S["clip_ready"], 1)
                    if not (first and k1 == 1):
                        moe_low(dve, m, A, S, n, odd, k1 - 2)
                    dve.wait_ge(S["silu_ready"], n * (3 * FC) + k1)
                    if m.clip:
                        dve.wait_ge(S["clip_ready"], n * (3 * FC) + k1)
                        ins = nc.vector.scalar_tensor_tensor(out=A["hf"][par][:], in0=A["s"][par][:],
                                                             scalar=SILU_LIMIT, in1=A["t"][par][:], op0=ALU.min,
                                                             op1=ALU.mult)
                    else:
                        ins = nc.vector.tensor_tensor(A["hf"][par][:], bank[2 + par][:, 0:CHW], A["s"][par][:],
                                                      ALU.mult)
                    ins.then_inc(S["h_ready"], 1)
                if c == 0 and not first:
                    moe_acc(dve, m, S, n - 1, 1 - odd, 2, before)
                elif c > 0:
                    moe_acc(dve, m, S, n, odd, c - 1, weight)

        @block.tensor
        def _(pe):
            pe.wait_ge(ld_tokw, 16)
            for j, (t0, t1) in enumerate(PBLK):
                pe.wait_ge(ld_patch[j], 16)
                n = (t1 - t0) * P
                pb = patch[:, t0 * P * PATCH_K:t1 * P * PATCH_K].rearrange("p (k n) -> p k n", n=n)
                for t in range(t1 - t0):
                    for k in range(PATCH_K):
                        last = nc.tensor.matmul(bank[j][:, t * D:(t + 1) * D], pb[:, k, t * P:(t + 1) * P],
                                                tokw_sb[:, k, :], start=(k == 0), stop=(k == PATCH_K - 1))
                last.then_inc(tok_done, 1)

            def transposes(k):
                if k == 0:
                    pe.wait_ge(ld_const, 16)
                for c in range(CH):
                    pe.wait_ge(ln_y, 3 * k + c + 1)
                    for half in range(2):
                        for t in range(3):
                            last = nc.tensor.transpose(bank[2 * c + half][:, t * P:(t + 1) * P],
                                                       Y[:, 3 * c + t, half * P:(half + 1) * P], ident)
                    last.then_inc(ln_xt, 1)

            transposes(0)
            pe.wait_ge(ln_lo, 6)
            pe.wait_ge(split_lo, 2)
            pe.wait_ge(pads, 4)
            wa3 = (WAh, WAl, WA2)
            jobs = [("t", mat * D + half * HALF, c) for mat in range(2) for half in range(2) for c in range(3)]
            jobs += [("v", g, 0) for g in range(0, GROUPS, 2)]
            for j, (kind, a, c) in enumerate(jobs):
                if j >= 8:
                    pe.wait_ge(proj_out[j % 2], (j - 8) // 2 + 1)
                if kind == "t":
                    w3 = XW // 3
                    for i, (x, w) in enumerate(terms(wa3, wcols2(a, a + HALF), slice(c * w3, (c + 1) * w3))):
                        last = nc.tensor.matmul(bank[j % 8][0:HALF, 0:w3], w, x, start=(i == 0), stop=(i == 4))
                else:
                    for g in range(a, min(a + 2, GROUPS)):
                        for i, (x, w) in enumerate(terms(wa3, wcols2(2 * D, 3 * D), slice(g * GW, (g + 1) * GW))):
                            last = nc.tensor.matmul(bank[j % 8][0:GW, (g - a) * D:(g - a + 1) * D], x, w,
                                                    start=(i == 0), stop=(i == 4))
                last.then_inc(proj_done, 1)
            pe.wait_ge(proj_out[0], 7)
            pe.wait_ge(proj_out[1], 6)
            for b, (g0, g1) in enumerate(BATCHES):
                for g in range(g0, g1):
                    cols = slice(g * GW, (g + 1) * GW)
                    for half in range(2):
                        last = nc.tensor.matmul(bank[2 + b][0:GW, (g - g0) * GW:(g - g0 + 1) * GW],
                                                qT[:, half, cols], kT[:, half, cols], start=(half == 0),
                                                stop=(half == 1))
                last.then_inc(a0_s, 1)
            pe.wait_ge(proj_out[0], 9)
            pe.wait_ge(proj_out[1], 9)
            for b, (g0, g1) in enumerate(BATCHES):
                pe.wait_ge(a0_p, b + 1)
                for g in range(g0, g1):
                    last = nc.tensor.transpose(bank[5 + b][0:GW, (g - g0) * GW:(g - g0 + 1) * GW], Pm[:, g, :],
                                               ident[0:GW, 0:GW])
                last.then_inc(a0_pt, 1)
            for b, (g0, g1) in enumerate(BATCHES):
                pe.wait_ge(a0_ptc, b + 1)
                for half in range(2):
                    for g in range(g0, g1):
                        last = nc.tensor.matmul(bank[2 * b + half][0:HALF, (g - g0) * GW:(g - g0 + 1) * GW],
                                                V[:, g, half * HALF:(half + 1) * HALF], PT[:, g, :],
                                                start=True, stop=True)
                    last.then_inc(a0_o, 1)
            pe.wait_ge(a0_oc[0], 3)
            pe.wait_ge(a0_oc[1], 3)
            for j, (t0, t1) in enumerate(PBLK):
                for t in range(t0, t1):
                    for half in range(2):
                        last = nc.tensor.transpose(
                            bank[(6 + j) % 8][:, (t - t0) * D + half * HALF:(t - t0) * D + (half + 1) * HALF],
                            oT[:, half, t * P:(t + 1) * P], ident[0:HALF, 0:HALF])
                last.then_inc(a0_back, 1)

            def router(col, width, z):
                for t in range(TILES):
                    for i, (x, w) in enumerate(terms(wa3, wcols2(col, col + width), slice(t * P, (t + 1) * P))):
                        last = nc.tensor.matmul(bank[6][:, t * width:(t + 1) * width], x, w, start=(i == 0),
                                                stop=(i == 4))
                last.then_inc(z, 1)

            transposes(1)
            pe.wait_ge(ln_lo, 12)
            router(3 * D, E0, rt_z)
            M, S = MOE0, moe_sems[0]
            moe_pe(pe, M, W0, A0, S, 0, 0, True)
            with pe.Fori(0, E0 // 2, 1) as i:
                for u in range(2):
                    moe_pe(pe, M, W0, A0, S, i * 2 + (1 + u), (1 + u) % 2, False)
            tail_down(pe, nc, M, W0, A0, S, bank)

            transposes(2)
            pe.wait_ge(ln_lo, 18)
            pe.wait_ge(split_lo, 4)
            l13 = (L1h, L1l, L12)
            for g in range(GROUPS):
                if g >= 4:
                    pe.wait_ge(l1_out[0], g - 3)
                    pe.wait_ge(l1_out[1], g - 3)
                for half in range(2):
                    for i, (x, w) in enumerate(terms(l13, wcols2(half * L1H, (half + 1) * L1H),
                                                     slice(g * GW, (g + 1) * GW))):
                        last = nc.tensor.matmul(bank[(2 * g + half) % 8][0:GW, 0:L1H], x, w, start=(i == 0),
                                                stop=(i == 4))
                last.then_inc(l1_proj, 1)
            pe.wait_ge(l1_out[0], GROUPS)
            pe.wait_ge(l1_out[1], GROUPS)
            for j in range(6):
                for g in range(2 * j, min(2 * j + 2, GROUPS)):
                    last = nc.tensor.matmul(bank[(6 + j) % 8][0:GW, (g % 2) * D:(g % 2 + 1) * D], tri,
                                            QK[:, g, 2 * D:3 * D], start=True, stop=True)
                last.then_inc(l1_us, 1)
            pe.wait_ge(l1_s, 1)
            for b, (g0, g1) in enumerate(BATCHES):
                for g in range(g0, g1):
                    last = nc.tensor.transpose(bank[4 + b][0:HEADS, (g - g0) * GW:(g - g0 + 1) * GW],
                                               ES[:, g, HEADS:2 * HEADS], ident[0:GW, 0:GW])
                last.then_inc(l1_st, 1)
            pe.wait_ge(l1_ex, 1)
            for g in range(GROUPS):
                last = nc.tensor.transpose(bank[7][0:GW, g * HEADS:(g + 1) * HEADS], sT[:, g * GW:(g + 1) * GW],
                                           ident[0:HEADS, 0:HEADS])
            last.then_inc(l1_et, 1)
            pe.wait_ge(l1_es, 1)
            for g in range(GROUPS):
                last = nc.tensor.matmul(bank[0][0:GW, g * 2 * HEADS:(g + 1) * 2 * HEADS], tri, ES[:, g, :],
                                        start=True, stop=True)
            last.then_inc(l1_cum, 1)
            for b, (g0, g1) in enumerate(BATCHES):
                pe.wait_ge(l1_qw, b + 1)
                pe.wait_ge(l1_kw, b + 1)
                for g in range(g0, g1):
                    if g:
                        pe.wait_ge(l1_Tca, 2 * g)
                        pe.wait_ge(l1_Tcd, g)
                    for i in range(12):
                        last = nc.tensor.transpose(
                            bank[i // 4][:, (i % 4) * GW:(i % 4 + 1) * GW],
                            (qw, kw)[i // 6][:, g - g0, 2 * (i % 6):2 * (i % 6) + 2, :].rearrange("p a b -> p (a b)"),
                            ident[0:GW, 0:GW])
                        if i % 4 == 3:
                            last.then_inc(l1_T, 1)
                    pe.wait_ge(l1_Tca, 2 * g + 2)
                    pe.wait_ge(l1_Tcd, g + 1)
                    for k in range(2):
                        if g:
                            pe.wait_ge(l1_Am, 4 * (g - 1) + 2 * k + 2)
                        for h in range(6 * k, 6 * k + 6):
                            o, i = SLOT * (h % 2), h % 6 // 2
                            last = nc.tensor.matmul(bank[3 + 2 * k + h % 2][0:GW, i * GW:(i + 1) * GW],
                                                    qkT[o:o + 3 * HD, 6 + h // 2, :], qkT[o:o + 3 * HD, h // 2, :],
                                                    start=True, stop=True)
                            if h % 6 >= 4:
                                last.then_inc(l1_A, 1)
                    if g:
                        pe.wait_ge(l1_Oc, g)
                    for h in range(HEADS):
                        if h % 6 == 0:
                            pe.wait_ge(l1_Am, 4 * g + h // 3 + 2)
                        last = nc.tensor.matmul(bank[7][0:GW, h * HD:(h + 1) * HD], AT[:, h, :],
                                                QK[:, g, 3 * D + h * HD:3 * D + (h + 1) * HD], start=True,
                                                stop=True)
                    last.then_inc(l1_O, 1)
            for g in range(GROUPS):
                if g == 0:
                    pe.wait_ge(l1_on, 1)
                if g >= 2:
                    pe.wait_ge(l1_oTc, g - 1)
                for half in range(2):
                    last = nc.tensor.transpose(bank[g % 2][0:HALF, half * GW:(half + 1) * GW],
                                               QK[:, g, 2 * D + half * HALF:2 * D + (half + 1) * HALF],
                                               ident[0:GW, 0:GW])
                last.then_inc(l1_oT, 1)
            pe.wait_ge(l1_oTc, GROUPS)
            pe.wait_ge(ld_wo, 16)
            for j, (t0, t1) in enumerate(PBLK):
                for t in range(t0, t1):
                    for half in range(2):
                        last = nc.tensor.matmul(bank[2 + j][:, (t - t0) * D:(t - t0 + 1) * D],
                                                OT[:, half, t * P:(t + 1) * P], wo_sb[:, half, :],
                                                start=(half == 0), stop=(half == 1))
                last.then_inc(l1_f, 1)

            transposes(3)
            pe.wait_ge(ln_lo, 24)
            router(3 * D + E0, E1P, rt1_z)
            M, S = MOE1, moe_sems[1]
            for n in range(M.works):
                moe_pe(pe, M, W1, A1, S, n, n % 2, n == 0)
            tail_down(pe, nc, M, W1, A1, S, bank)

        @block.scalar
        def _(act):
            def norm_act(k):
                act.wait_ge(ln_var, k + 1)
                nc.scalar.activation(sd[:], ve[:], ACT.Sqrt).then_inc(ln_sd, 1)
                for c in range(CH):
                    act.wait_ge(ln_xt, 3 * k + c + 1)
                    cols = slice(c * CHW, (c + 1) * CHW)
                    nc.scalar.activation(X01h[:, cols], bank[2 * c][:, 0:CHW], ACT.Copy).then_inc(ln_hi, 1)
                    nc.scalar.activation(X2h[:, cols], bank[2 * c + 1][:, 0:CHW], ACT.Copy).then_inc(ln_hi, 1)

            for s, (wh, w2, n) in enumerate(((WAh, WA2, NWA), (L1h, L12, QKVG))):
                act.wait_ge(ld_stage[s], 16)
                nc.scalar.activation(wh[:], W0[s]["stage"][:, 0:n], ACT.Copy).then_inc(split_hi, 1)
                nc.scalar.activation(w2[:], W0[s]["stage"][:, n:2 * n], ACT.Copy).then_inc(split_hi, 1)
            norm_act(0)
            for j in range(0, 18, 2):
                act.wait_ge(proj_done, j + 1)
                if j < 12:
                    half, c = (j // 3) % 2, j % 3
                    dst = (qT if j < 6 else kT)[:, half, c * (XW // 3):(c + 1) * (XW // 3)]
                    src = bank[j % 8][0:HALF, 0:XW // 3]
                else:
                    g = 2 * (j - 12)
                    n = min(2, GROUPS - g)
                    dst = V[:, g:g + n, :]
                    src = bank[j % 8][0:GW, 0:n * D].rearrange("p (g d) -> p g d", d=D)
                nc.scalar.activation(dst, src, ACT.Copy).then_inc(proj_out[0], 1)
            for b, (g0, g1) in enumerate(BATCHES):
                act.wait_ge(a0_shift, b + 1)
                nc.scalar.activation(Pm[:, g0:g1, :], Pm[:, g0:g1, :], ACT.Exp,
                                     scale=float(D) ** -0.5).then_inc(a0_exp, 1)
            for b, (g0, g1) in enumerate(BATCHES):
                act.wait_ge(a0_pt, b + 1)
                nc.scalar.activation(PT[:, g0:g1, :], bank[5 + b][0:GW, 0:(g1 - g0) * GW].rearrange(
                    "p (g q) -> p g q", q=GW), ACT.Copy).then_inc(a0_ptc, 1)
            for b, (g0, g1) in enumerate(BATCHES):
                act.wait_ge(a0_o, 2 * b + 1)
                nc.scalar.activation(oT[:, 0, g0 * GW:g1 * GW], bank[2 * b][0:HALF, 0:(g1 - g0) * GW],
                                     ACT.Copy).then_inc(a0_oc[0], 1)
            S0, S1 = moe_sems
            for i in range(MOE0.pieces):
                moe_weights_act(act, MOE0, W0, S0, ld_stage, 0, 0, i, None, 32)
            norm_act(1)
            act.wait_ge(rt_neg, 1)
            nc.scalar.activation(rt[1][:], rt[1][:], ACT.Exp).then_inc(rt_e, 1)
            act.wait_ge(rt_u, 1)
            nc.scalar.activation(rt[3][:], rt[2][:], ACT.Ln).then_inc(rt_ln, 1)
            act.wait_ge(rt_sp, 1)
            nc.scalar.activation(rt[4][:], rt[3][:], ACT.Sqrt).then_inc(rt_sc, 1)
            moe_act(act, MOE0, W0, A0, S0, ld_stage, 0, 0, True, False, 32)
            with act.Fori(0, E0 // 2 - 1, 1) as i:
                for u in range(2):
                    moe_act(act, MOE0, W0, A0, S0, ld_stage, i * 2 + (1 + u), (1 + u) % 2, False, False,
                            i * 16 + 48)
            for n in (E0 - 1, E0):
                moe_act(act, MOE0, W0, A0, S0, ld_stage, n, n % 2, False, n == E0, 16 * ((n + 1) // 2 + 2))
            moe_high(act, MOE0, A0, S0, E0, E0 % 2, 3 * MOE0.fc - 1)
            norm_act(2)

            act.wait_ge(ld_row, 16)
            act.wait_ge(l1_tau, 1)
            nc.scalar.activation(tau[:], tau[:], ACT.Exp).then_inc(l1_tau, 1)
            for g in range(GROUPS):
                act.wait_ge(l1_proj, g + 1)
                nc.scalar.activation(QK[:, g, 0:L1H], bank[(2 * g) % 8][0:GW, 0:L1H], ACT.Copy).then_inc(l1_out[0], 1)
            for n in range(2):
                for i in range(MOE1.pieces):
                    moe_weights_act(act, MOE1, W1, S1, ld_stage1, n, n, i, None, 16)
            act.wait_ge(l1_sh, 3)
            nc.scalar.activation(sT[:], sT[:], ACT.Exp).then_inc(l1_ex, 1)
            act.wait_ge(l1_out[1], GROUPS)
            nc.scalar.activation(SG[:], QK[:, :, 4 * D:QKVG], ACT.Sigmoid).then_inc(l1_sig, 1)
            for b, (g0, g1) in enumerate(BATCHES):
                n = g1 - g0
                act.wait_ge(l1_rope, b + 1)
                nc.scalar.activation(rotA[:, 0:n, :], QK[:, g0:g1, 0:2 * D], ACT.Square).then_inc(l1_sq, 1)
                act.wait_ge(l1_n2, b + 1)
                nc.scalar.activation(nrm[:, 0:n, :], nrm[:, 0:n, :], ACT.Sqrt).then_inc(l1_nr, 1)
                for g in range(g0, g1):
                    for i in range(2):
                        act.wait_ge(l1_T, 3 * g + i + 1)
                        if g:
                            act.wait_ge(l1_A, 4 * g)
                        nc.scalar.activation(qkT[:, 4 * i:4 * i + 4, :], bank[i][:, 0:4 * GW].rearrange(
                            "p (h q) -> p h q", q=GW), ACT.Copy).then_inc(l1_Tca, 1)
                    act.wait_ge(l1_O, g + 1)
                    nc.scalar.activation(QK[:, g, 2 * D:3 * D], bank[7][0:GW, 0:D], ACT.Copy).then_inc(l1_Oc, 1)
            act.wait_ge(l1_cen, 1)
            nc.scalar.activation(W1b, QK[:, :, 2 * D:3 * D], ACT.Square).then_inc(l1_csq, 1)
            act.wait_ge(l1_var, 1)
            nc.scalar.activation(CO[:, 1], CO[:, 0], ACT.Sqrt).then_inc(l1_std, 1)
            for g in range(GROUPS):
                act.wait_ge(l1_oT, g + 1)
                w = min(GW, TOK - g * GW)
                src = bank[g % 2][0:HALF, 0:2 * GW].rearrange("p (h q) -> p h q", h=2)[:, :, 0:w]
                nc.scalar.activation(OT[:, :, g * GW:g * GW + w], src, ACT.Copy).then_inc(l1_oTc, 1)
            norm_act(3)
            act.wait_ge(rt1_b, 1)
            nc.scalar.activation(rt[4][:, 0:TILES * E1], rt[0][:, 0:TILES * E1], ACT.Sigmoid).then_inc(rt1_p, 1)
            for n in range(MOE1.works):
                moe_act(act, MOE1, W1, A1, S1, ld_stage1, n, n % 2, n == 0, n in (0, E1), 32)
            moe_high(act, MOE1, A1, S1, E1, E1 % 2, 3 * MOE1.fc - 1)

        @block.gpsimd
        def _(pool):
            for x in (X01h, X01l, X2h, X2l):
                nc.gpsimd.memset(x[:, TOK:XW].bitcast(F32), 0.0).then_inc(pads, 1)
            for s, (st, wh, wl, w2, n) in enumerate(((0, WAh, WAl, WA2, NWA), (1, L1h, L1l, L12, QKVG))):
                stage = W0[st]["stage"]
                pool.wait_ge(split_hi, 2 * s + 1)
                pool.wait_ge(*((split_lo, 2 * s) if s else (pads, 4)))
                nc.gpsimd.tensor_tensor(wl[:], stage[:, 0:n], wh[:].bitcast(F32), ALU.subtract).then_inc(split_lo, 1)
                pool.wait_ge(split_hi, 2 * s + 2)
                pool.wait_ge(split_lo, 2 * s + 1)
                nc.gpsimd.tensor_tensor(w2[64:P, :], stage[64:P, n:2 * n], w2[64:P, :].bitcast(F32),
                                        ALU.subtract).then_inc(split_lo, 1)
            S0, S1 = moe_sems
            pool.wait_ge(split_lo, 4)
            moe_weights_pool(pool, MOE0, W0, S0, 0, 0)
            with pool.Fori(0, E0 // 2, 1) as i:
                for u in range(2):
                    moe_weights_pool(pool, MOE0, W0, S0, i * 2 + (1 + u), (1 + u) % 2)
            pool.wait_ge(l1_out[1], GROUPS)
            nc.gpsimd.memset(qw[:], 0.0).then_inc(pad_w, 1)
            nc.gpsimd.memset(kw[:], 0.0).then_inc(pad_w, 1)
            pool.wait_ge(pad_w, 2)
            for n in range(2):
                moe_weights_pool(pool, MOE1, W1, S1, n, n)
            for b, (g0, g1) in enumerate(BATCHES):
                n = g1 - g0
                pool.wait_ge(l1_cq, b + 1)
                if b:
                    pool.wait_ge(l1_T, 3 * g0)
                else:
                    pool.wait_ge(pad_w, 2)
                for j in range(3):
                    f = CK[:, j, 0:n, :] if j < 2 else rn[:, 0:n, HEADS:2 * HEADS]
                    last = nc.gpsimd.tensor_tensor(
                        kw[:, 0:n, :, j * HD:(j + 1) * HD],
                        QK[:, g0:g1, D:2 * D].rearrange("p g (h d) -> p g h d", d=HD),
                        f.unsqueeze(3).to_broadcast([GW, n, HEADS, HD]), ALU.mult)
                    last.then_inc(l1_kw if j == 2 else pool_step, 1)
            for n in range(2, MOE1.works):
                moe_weights_pool(pool, MOE1, W1, S1, n, n % 2)

        @block.vector
        def _(dve):
            own = Steps(dve, dve_step)

            def norm(k, ready):
                for t in range(TILES):
                    ready(t)
                    own.step(nc.vector.bn_stats(stat[:, t, :], H[:, t, :]))
                own.settle()
                for t in range(TILES):
                    own.step(nc.vector.bn_aggr(mv[:, t, :], stat[:, t, :]))
                own.settle()
                nc.vector.tensor_scalar(ve[:], mv[:, :, 1], EPS, None, ALU.add).then_inc(ln_var, 1)
                dve.wait_ge(ln_sd, k + 1)
                own.link(nc.vector.reciprocal(rstd[:], sd[:]))
                for c in range(CH):
                    for t in range(3 * c, 3 * c + 3):
                        own.step(nc.vector.tensor_scalar(Y[:, t, 0:D], H[:, t, :], mv[:, t, 0:1], rstd[:, t:t + 1],
                                                         ALU.subtract, ALU.mult))
                    own.settle()
                    nc.vector.tensor_copy(Y[:, 3 * c:3 * c + 3, D:256], Y[:, 3 * c:3 * c + 3, P:D]).then_inc(ln_y, 1)
                for c in range(CH):
                    cols = slice(c * CHW, (c + 1) * CHW)
                    dve.wait_ge(ln_hi, 6 * k + 2 * c + 1)
                    nc.vector.tensor_tensor(X01l[:, cols], bank[2 * c][:, 0:CHW], X01h[:, cols].bitcast(F32),
                                            ALU.subtract).then_inc(ln_lo, 1)
                    dve.wait_ge(ln_hi, 6 * k + 2 * c + 2)
                    nc.vector.tensor_tensor(X2l[:, cols], bank[2 * c + 1][0:64, 0:CHW],
                                            X2h[0:64, cols].bitcast(F32), ALU.subtract).then_inc(ln_lo, 1)

            def rank(sc, keys, E, comb_out, clip):
                shape = [P, TILES, E, E]
                r = keys.rearrange("p (t e) -> p t e", e=E)
                other, mine = r.unsqueeze(2).to_broadcast(shape), r.unsqueeze(3).to_broadcast(shape)
                k0 = rk[0][:, 0:TILES * E * E].rearrange("p (t e j) -> p t e j", e=E, j=E)
                k1 = rk[1][:, 0:TILES * E * E].rearrange("p (t e j) -> p t e j", e=E, j=E)
                low = const[:, C_LOW:C_LOW + E0 * E0].rearrange("p (e j) -> p e j", j=E0)[:, 0:E, 0:E]
                own.step(nc.vector.tensor_tensor(k0, other, mine, ALU.is_gt))
                own.link(nc.vector.tensor_tensor(k1, other, mine, ALU.is_equal))
                own.link(nc.vector.tensor_tensor(k1, k1, low.unsqueeze(1).to_broadcast(shape), ALU.mult))
                own.link(nc.vector.tensor_tensor(k0, k0, k1, ALU.add))
                rnk = rt[5][:, 0:TILES * E]
                own.link(nc.vector.tensor_reduce(rnk.rearrange("p (t e) -> p t e", e=E), k0, AX.X, ALU.add))
                own.link(nc.vector.scalar_tensor_tensor(out=rnk, in0=rnk, scalar=1.5, in1=sc, op0=ALU.is_lt,
                                                        op1=ALU.mult))
                own.link(nc.vector.tensor_reduce(rsum[0][:], rnk.rearrange("p (t e) -> p t e", e=E), AX.X, ALU.add))
                if clip:
                    own.link(nc.vector.tensor_scalar(rsum[0][:], rsum[0][:], 1e-6, None, ALU.max))
                own.link(nc.vector.reciprocal(rsum[1][:], rsum[0][:]))
                own.link(nc.vector.tensor_tensor(comb_out, rnk.rearrange("p (t e) -> p t e", e=E),
                                                 rsum[1][:].unsqueeze(2).to_broadcast([P, TILES, E]), ALU.mult))

            def tiles2(t0, t1):
                return H[:, t0:t1, :]

            def pair(b, t0, t1):
                return bank[b][:, 0:(t1 - t0) * D].rearrange("p (t d) -> p t d", d=D)

            dve.wait_ge(ld_row, 16)
            bias = row[:, R_TOKB:R_TOKB + D].unsqueeze(1)
            for j, (t0, t1) in enumerate(PBLK):
                dve.wait_ge(tok_done, j + 1)
                nc.vector.tensor_tensor(tiles2(t0, t1), pair(j, t0, t1), bias.to_broadcast([P, t1 - t0, D]),
                                        ALU.add).then_inc(tok_h, 1)
            norm(0, lambda t: dve.wait_ge(tok_h, t // 2 + 1))

            dve.wait_ge(ld_const, 16)
            for j in range(1, 18, 2):
                dve.wait_ge(proj_done, j + 1)
                if j < 12:
                    half, c = (j // 3) % 2, j % 3
                    dst = (qT if j < 6 else kT)[:, half, c * (XW // 3):(c + 1) * (XW // 3)]
                    src = bank[j % 8][0:HALF, 0:XW // 3]
                else:
                    g = 2 * (j - 12)
                    n = min(2, GROUPS - g)
                    dst = V[:, g:g + n, :]
                    src = bank[j % 8][0:GW, 0:n * D].rearrange("p (g d) -> p g d", d=D)
                nc.vector.tensor_copy(dst, src).then_inc(proj_out[1], 1)
            for b, (g0, g1) in enumerate(BATCHES):
                n = g1 - g0
                dve.wait_ge(a0_s, b + 1)
                pm = Pm[:, g0:g1, :]
                own.link(nc.vector.tensor_tensor(
                    pm, bank[2 + b][0:GW, 0:n * GW].rearrange("p (g q) -> p g q", q=GW),
                    amask.unsqueeze(1).to_broadcast([GW, n, GW]), ALU.add))
                own.link(nc.vector.tensor_reduce(mx[:, g0:g1], pm, AX.X, ALU.max))
                nc.vector.tensor_tensor(pm, pm, mx[:, g0:g1].unsqueeze(2).to_broadcast([GW, n, GW]),
                                        ALU.subtract).then_inc(a0_shift, 1)
            for b, (g0, g1) in enumerate(BATCHES):
                n = g1 - g0
                dve.wait_ge(a0_exp, b + 1)
                pm = Pm[:, g0:g1, :]
                own.link(nc.vector.tensor_reduce(rs[:, g0:g1], pm, AX.X, ALU.add))
                own.link(nc.vector.reciprocal(rr[:, g0:g1], rs[:, g0:g1]))
                nc.vector.tensor_tensor(pm, pm, rr[:, g0:g1].unsqueeze(2).to_broadcast([GW, n, GW]),
                                        ALU.mult).then_inc(a0_p, 1)
            for b, (g0, g1) in enumerate(BATCHES):
                dve.wait_ge(a0_o, 2 * b + 2)
                nc.vector.tensor_copy(oT[:, 1, g0 * GW:g1 * GW],
                                      bank[2 * b + 1][0:HALF, 0:(g1 - g0) * GW]).then_inc(a0_oc[1], 1)
            for j, (t0, t1) in enumerate(PBLK):
                dve.wait_ge(a0_back, j + 1)
                nc.vector.tensor_tensor(tiles2(t0, t1), pair((6 + j) % 8, t0, t1), tiles2(t0, t1),
                                        ALU.add).then_inc(a0_h, 1)
            norm(1, lambda t: dve.wait_ge(a0_h, t // 2 + 1))

            z, e, u, l, sc = (rt[i][:] for i in range(5))
            dve.wait_ge(rt_z, 1)
            own.link(nc.vector.tensor_copy(z, bank[6][:, 0:TILES * E0]))
            nc.vector.scalar_tensor_tensor(out=e, in0=z, scalar=-1.0, in1=z, op0=ALU.mult,
                                           op1=ALU.min).then_inc(rt_neg, 1)
            dve.wait_ge(rt_e, 1)
            nc.vector.tensor_scalar(u, e, 1.0, None, ALU.add).then_inc(rt_u, 1)
            dve.wait_ge(rt_u, 1)
            own.step(nc.vector.scalar_tensor_tensor(out=e, in0=u, scalar=1.0, in1=e, op0=ALU.subtract,
                                                    op1=ALU.subtract))
            own.link(nc.vector.reciprocal(sc, u))
            own.link(nc.vector.tensor_tensor(e, e, sc, ALU.mult))
            dve.wait_ge(rt_ln, 1)
            own.link(nc.vector.tensor_tensor(l, l, e, ALU.subtract))
            nc.vector.scalar_tensor_tensor(out=l, in0=z, scalar=0.0, in1=l, op0=ALU.max,
                                           op1=ALU.add).then_inc(rt_sp, 1)
            dve.wait_ge(rt_sc, 1)
            own.link(nc.vector.tensor_tensor(
                u.rearrange("p (t e) -> p t e", e=E0), sc.rearrange("p (t e) -> p t e", e=E0),
                row[:, R_GB:R_GB + E0].unsqueeze(1).to_broadcast([P, TILES, E0]), ALU.add))
            rank(sc, u, E0, comb[:], True)

            S0, S1 = moe_sems

            def weight0(e):
                return lambda tile: comb[:, tile, bass.ds(e, 1)] if not isinstance(e, int) else comb[:, tile, e:e + 1]

            moe_dve(dve, MOE0, A0, S0, 0, 0, True, None, None)
            moe_dve(dve, MOE0, A0, S0, 1, 1, False, weight0(0), None)
            moe_dve(dve, MOE0, A0, S0, 2, 0, False, weight0(1), weight0(0))
            with dve.Fori(0, E0 // 2 - 1, 1) as i:
                for u_ in range(2):
                    moe_dve(dve, MOE0, A0, S0, i * 2 + (3 + u_), (3 + u_) % 2, False, weight0(i * 2 + (2 + u_)),
                            weight0(i * 2 + (1 + u_)))
            moe_low(dve, MOE0, A0, S0, E0, E0 % 2, 3 * MOE0.fc - 1)
            moe_acc(dve, MOE0, S0, E0, E0 % 2, 2, weight0(E0 - 1))
            base0 = E0 * 9
            norm(2, lambda t: dve.wait_ge(S0["acc_done"], base0 + t + 1))

            gw = lambda ap: ap.rearrange("p g (h d) -> p g h d", d=HD)
            t_, rt_, nrt_ = (const[0:GW, c:c + 1] for c in (C_T, C_RT, C_NRT))
            nc.vector.tensor_scalar(tau[:], row[0:GW, R_TAU:R_TAU + HEADS], -50.0, 30.0, ALU.max,
                                    ALU.min).then_inc(l1_tau, 1)
            for g in range(GROUPS):
                dve.wait_ge(l1_proj, g + 1)
                nc.vector.tensor_copy(QK[:, g, L1H:QKVG], bank[(2 * g + 1) % 8][0:GW, 0:L1H]).then_inc(l1_out[1], 1)
            dve.wait_ge(l1_tau, 2)
            own.step(nc.vector.tensor_tensor(tmu[:].rearrange("p (h d) -> p h d", d=HD),
                                             row[0:GW, R_MU:R_MU + D].rearrange("p (h d) -> p h d", d=HD),
                                             tau[:].unsqueeze(2).to_broadcast([GW, HEADS, HD]), ALU.mult))
            own.link(nc.vector.tensor_scalar(tden[:], tau[:], t_, None, ALU.add))
            own.link(nc.vector.reciprocal(tau[:], tden[:]))
            own.link(nc.vector.tensor_scalar(tden[:], tau[:], -1.0 / float(HD) ** 0.5, None, ALU.mult))
            for j in range(6):
                g0, g1 = 2 * j, min(2 * j + 2, GROUPS)
                dve.wait_ge(l1_us, j + 1)
                own.step(nc.vector.tensor_tensor(
                    W1b[:, g0:g1, :], bank[(6 + j) % 8][0:GW, 0:(g1 - g0) * D].rearrange("p (g d) -> p g d", d=D),
                    tmu[:].unsqueeze(1).to_broadcast([GW, g1 - g0, D]), ALU.add))
            own.settle()
            own.link(nc.vector.tensor_tensor(W1b, W1b, QK[:, :, 2 * D:3 * D], ALU.mult))
            own.link(nc.vector.tensor_reduce(CO[:, 0], gw(W1b), AX.X, ALU.add))
            nc.vector.tensor_tensor(ES[:, :, HEADS:2 * HEADS], CO[:, 0],
                                    tden[:].unsqueeze(1).to_broadcast([GW, GROUPS, HEADS]), ALU.mult).then_inc(l1_s, 1)
            for b, (g0, g1) in enumerate(BATCHES):
                n = (g1 - g0) * GI
                dve.wait_ge(l1_st, b + 1)
                src = bank[4 + b][0:HEADS, 0:n * SEQ].rearrange("p (i s) -> p i s", s=SEQ)
                m = smax[:, g0 * GI:g1 * GI]
                own.link(nc.vector.tensor_reduce(m, src, AX.X, ALU.max))
                nc.vector.tensor_tensor(sT[:, g0 * GW:g1 * GW].rearrange("p (i s) -> p i s", s=SEQ), src,
                                        m.unsqueeze(2).to_broadcast([HEADS, n, SEQ]), ALU.subtract).then_inc(l1_sh, 1)
            dve.wait_ge(l1_et, 1)
            nc.vector.tensor_copy(ES[:, :, 0:HEADS], bank[7][0:GW, 0:GROUPS * HEADS].rearrange(
                "p (g h) -> p g h", h=HEADS)).then_inc(l1_es, 1)
            dve.wait_ge(l1_cum, 1)
            dve.wait_ge(l1_sig, 1)
            cum = bank[0][0:GW, 0:GROUPS * 2 * HEADS].rearrange("p (g h) -> p g h", h=2 * HEADS)
            al, be, ga = CO[:, 0], CO[:, 1], CO[:, 2]
            s1, sh = SG[:, :, 0:HEADS], SG[:, :, HEADS:2 * HEADS]
            dve.wait_ge(l1_s, 1)
            own.link(nc.vector.tensor_scalar(ga, cum[:, :, 0:HEADS], 1e-12, None, ALU.add))
            own.link(nc.vector.reciprocal(al, ga))
            own.step(nc.vector.tensor_tensor(al, al, sh, ALU.mult))
            own.link(nc.vector.tensor_tensor(be, s1, sh, ALU.subtract))
            own.link(nc.vector.tensor_scalar(be, be, rt_, None, ALU.mult))
            own.link(nc.vector.tensor_tensor(ga, cum[:, :, HEADS:2 * HEADS], be, ALU.mult))
            own.link(nc.vector.tensor_tensor(ga, ga, sh, ALU.add))
            own.link(nc.vector.tensor_scalar(ga, ga, nrt_, None, ALU.mult))
            dve.wait_ge(l1_es, 1)
            for b, (g0, g1) in enumerate(BATCHES):
                n = g1 - g0
                src = QK[:, g0:g1, 0:2 * D].rearrange("p g (h d) -> p g h d", d=HD)
                A4 = rotA[:, 0:n, :].rearrange("p g (h d) -> p g h d", d=HD)
                B4 = rotB[:, 0:n, :].rearrange("p g (h d) -> p g h d", d=HD)
                hh = HD // 2

                def table(c, m):
                    return const[0:GW, c:c + m].unsqueeze(1).unsqueeze(1).to_broadcast([GW, n, 2 * HEADS, m])

                own.step(nc.vector.tensor_tensor(A4, src, table(C_COS, HD), ALU.mult))
                own.step(nc.vector.tensor_tensor(B4[:, :, :, 0:hh], src[:, :, :, hh:HD], table(C_SIN, hh), ALU.mult))
                own.link(nc.vector.tensor_tensor(B4[:, :, :, hh:HD], src[:, :, :, 0:hh], table(C_SIN + hh, hh),
                                                 ALU.mult))
                nc.vector.tensor_tensor(QK[:, g0:g1, 0:2 * D], rotA[:, 0:n, :], rotB[:, 0:n, :],
                                        ALU.add).then_inc(l1_rope, 1)
                dve.wait_ge(l1_sq, b + 1)
                nc.vector.tensor_reduce(nrm[:, 0:n, :], A4, AX.X, ALU.add).then_inc(l1_n2, 1)
                dve.wait_ge(l1_nr, b + 1)
                own.link(nc.vector.tensor_scalar(nrm[:, 0:n, :], nrm[:, 0:n, :], 1e-12, None, ALU.max))
                if b:
                    dve.wait_ge(l1_kw, b)
                own.link(nc.vector.reciprocal(rn[:, 0:n, :], nrm[:, 0:n, :]))
                own.step(nc.vector.tensor_tensor(CK[:, 0, 0:n, :], ES[:, g0:g1, 0:HEADS],
                                                 rn[:, 0:n, HEADS:2 * HEADS], ALU.mult))
                nc.vector.tensor_tensor(CK[:, 1, 0:n, :], ES[:, g0:g1, HEADS:2 * HEADS],
                                        rn[:, 0:n, HEADS:2 * HEADS], ALU.mult).then_inc(l1_cq, 1)
                for j in range(3):
                    own.step(nc.vector.tensor_tensor(CQ[:, j, 0:n, :], CO[:, j, g0:g1, :], rn[:, 0:n, 0:HEADS],
                                                     ALU.mult))
                own.settle()
                if b:
                    dve.wait_ge(l1_T, 3 * g0)
                else:
                    dve.wait_ge(pad_w, 2)
                for j in range(3):
                    nc.vector.tensor_tensor(
                        qw[:, 0:n, :, j * HD:(j + 1) * HD], gw(QK[:, g0:g1, 0:D]),
                        CQ[:, j, 0:n, :].unsqueeze(3).to_broadcast([GW, n, HEADS, HD]),
                        ALU.mult).then_inc(l1_qw if j == 2 else dve_step, 1)
                    own.n += j < 2
                for g in range(g0, g1):
                    dve.wait_ge(l1_T, 3 * g + 3)
                    if g:
                        dve.wait_ge(l1_A, 4 * g)
                    nc.vector.tensor_copy(qkT[:, 8:12, :], bank[2][:, 0:4 * GW].rearrange(
                        "p (h q) -> p h q", q=GW)).then_inc(l1_Tcd, 1)
                    for k in range(4):
                        dve.wait_ge(l1_A, 4 * g + k + 1)
                        if g:
                            dve.wait_ge(l1_O, g)
                        h0 = 6 * (k // 2) + k % 2
                        nc.vector.tensor_tensor(
                            AT[:, h0:h0 + 5:2, :], bank[3 + k][0:GW, 0:3 * GW].rearrange("p (h q) -> p h q", q=GW),
                            tri.unsqueeze(1).to_broadcast([GW, 3, GW]), ALU.mult).then_inc(l1_Am, 1)
            O = gw(QK[:, :, 2 * D:3 * D])
            dve.wait_ge(l1_Oc, GROUPS)
            bc = [GW, GROUPS, HEADS, HD]
            own.link(nc.vector.tensor_reduce(CO[:, 0], O, AX.X, ALU.add))
            own.link(nc.vector.tensor_scalar(CO[:, 1], CO[:, 0], 1.0 / HD, None, ALU.mult))
            nc.vector.tensor_tensor(O, O, CO[:, 1].unsqueeze(3).to_broadcast(bc), ALU.subtract).then_inc(l1_cen, 1)
            dve.wait_ge(l1_csq, 1)
            own.link(nc.vector.tensor_reduce(CO[:, 2], gw(W1b), AX.X, ALU.add))
            nc.vector.tensor_scalar(CO[:, 0], CO[:, 2], 1.0 / HD, EPS, ALU.mult, ALU.add).then_inc(l1_var, 1)
            dve.wait_ge(l1_std, 1)
            own.link(nc.vector.reciprocal(CO[:, 2], CO[:, 1]))
            dve.wait_ge(l1_cen, 1)
            nc.vector.tensor_tensor(O, O, CO[:, 2].unsqueeze(3).to_broadcast(bc), ALU.mult).then_inc(l1_on, 1)
            for j, (t0, t1) in enumerate(PBLK):
                dve.wait_ge(l1_f, j + 1)
                nc.vector.tensor_tensor(tiles2(t0, t1), pair(2 + j, t0, t1), tiles2(t0, t1),
                                        ALU.add).then_inc(l1_h, 1)
            norm(3, lambda t: dve.wait_ge(l1_h, t // 2 + 1))

            dve.wait_ge(rt1_z, 1)
            n1 = TILES * E1
            z3 = rt[0][:, 0:n1]
            nc.vector.tensor_tensor(
                z3.rearrange("p (t e) -> p t e", e=E1),
                bank[6][:, 0:TILES * E1P].rearrange("p (t e) -> p t e", e=E1P)[:, :, 0:E1],
                row[:, R_RB:R_RB + E1].unsqueeze(1).to_broadcast([P, TILES, E1]), ALU.add).then_inc(rt1_b, 1)
            dve.wait_ge(rt1_p, 1)
            rank(rt[4][:, 0:n1], rt[4][:, 0:n1], E1, comb1[:], False)

            def weight1(n):
                return (lambda tile: comb1[:, tile, n - 1:n]) if n else None

            for n in range(MOE1.works):
                moe_dve(dve, MOE1, A1, S1, n, n % 2, n == 0, weight1(n), weight1(n - 1) if n else None)
            moe_low(dve, MOE1, A1, S1, E1, E1 % 2, 3 * MOE1.fc - 1)
            moe_acc(dve, MOE1, S1, E1, E1 % 2, 2, weight1(E1))


def moe_buffers(sb, scope, m, name):
    out = {}
    for key, shape, dt in (("s", [P, CHW], F32), ("t", [P, CHW], F32), ("hf", [P, CHW], F32),
                           ("hh", [P, m.fc, CHW], F32R), ("hl", [P, m.fc, CHW], F32R)):
        out[key] = [sb(f"{name}{key}{b}", shape, dt, scope) for b in range(2)]
    return out


def tail_down(pe, nc, m, W, A, S, bank):
    n, FC = m.works - 1, m.fc
    odd, c = n % 2, 2
    q = (3 * odd + c) % 2
    pe.wait_ge(S["hl_ready"], (3 * n + 3) * FC)
    for t in range(3):
        pe.wait_ge(S["acc_done"], 9 * n + 3 * c + t - 1)
        cols = slice(t * P, t * P + P)
        k = 0
        for fc in range(FC):
            hh, hl = A["hh"][q][:, fc, cols], A["hl"][q][:, fc, cols]
            for lhs, rhs in ((hh, W[odd]["dh"]), (hh, W[odd]["dl"]), (hl, W[odd]["dh"])):
                last = nc.tensor.matmul(bank[4 + (q + t) % 2][:, 0:D], lhs, rhs[:, fc, :], start=(k == 0),
                                        stop=(k == 3 * FC - 1))
                k += 1
        last.then_inc(S["down_ready"], 1)


def kernel(**inputs):
    import numpy as np
    import concourse.bacc as bacc
    from concourse.bass_utils import run_bass_kernel_spmd as run

    a = {k: np.asarray(v) for k, v in inputs.items()}

    def two(w):
        return np.concatenate([w[:P], np.concatenate([w[P:], w[P:]], axis=0)], axis=1)

    side = SIDE // PATCH
    x = a["x"].reshape(IMAGES, CHANNELS, side, PATCH, side, PATCH).transpose(0, 1, 2, 4, 3, 5)
    x = x.reshape(TOK, PATCH_K, P).transpose(2, 1, 0)
    x = np.concatenate([x[:, :, j:min(j + 2 * P, TOK)].reshape(P, -1) for j in range(0, TOK, 2 * P)], axis=1)
    tokw = a["L0_tok_W"].T.reshape(PATCH_K, P, D).transpose(1, 0, 2)

    consts = np.zeros((P, NCONST), np.float32)
    consts[:, C_ID:C_ID + P] = np.eye(P)
    i = np.arange(GW)
    same = (i[:, None] // SEQ) == (i[None, :] // SEQ)
    consts[:GW, C_MASK:C_MASK + GW] = np.where(same, 0.0, -1e30)
    consts[:GW, C_TRI:C_TRI + GW] = same & (i[:, None] <= i[None, :])
    inv = np.float32(1.0) / np.float32(10000.0) ** (np.arange(0, HD, 2, dtype=np.float32) / np.float32(HD))
    ang = (i % SEQ).astype(np.float32)[:, None] * inv[None, :]
    consts[:GW, C_COS:C_COS + HD] = np.repeat(np.cos(ang), 2, axis=1)
    consts[:GW, C_SIN:C_SIN + HD] = np.repeat(np.sin(ang), 2, axis=1) * np.where(np.arange(HD) < HD // 2, -1, 1)
    t = (i % SEQ + 1).astype(np.float32)
    consts[:GW, C_T], consts[:GW, C_RT], consts[:GW, C_NRT] = t, 1 / t, -1 / t
    e = np.arange(E0)
    consts[:, C_LOW:] = (e[None, :] < e[:, None]).astype(np.float32).reshape(1, -1)

    vec = np.concatenate([a["L0_tok_b"], a["L0_ffn_gate_bias"], a["L1_ffn_routing_bias"], np.zeros(1, np.float32),
                          a["L1_attn_prior_mu"].reshape(-1), a["L1_attn_prior_log_tau"].reshape(-1)])
    rows = np.broadcast_to(vec[None, :], (P, NROWS))

    wa = two(np.concatenate([a["L0_attn_W_q"], a["L0_attn_W_k"], a["L0_attn_W_v"], a["L0_ffn_gate_w"],
                             a["L1_ffn_router_w"], np.zeros((D, 1), np.float32)], axis=1))
    wg = a["L1_attn_Wg"].reshape(HEADS, 3, D)
    l1w = two(np.concatenate([a["L1_attn_Wq"].T, a["L1_attn_Wk"].T, a["L1_attn_Wu"].T, a["L1_attn_Wv"].T,
                              wg[:, 0].T, wg[:, 1].T], axis=1))
    wo = a["L1_attn_Wo"].T.reshape(2, HALF, D).transpose(1, 0, 2)

    def expert(gate, up, down, m):
        return np.concatenate([two(gate), two(up), down.reshape(m.fc, P, D).transpose(1, 0, 2).reshape(P, -1)], axis=1)

    moe0 = [expert(a["L0_ffn_w1s"], a["L0_ffn_w3s"], a["L0_ffn_w2s"], MOE0)]
    moe0 += [expert(a["L0_ffn_w1"][j], a["L0_ffn_w3"][j], a["L0_ffn_w2"][j], MOE0) for j in range(E0)]
    moe1 = [expert(a["L1_ffn_shared_gate"], a["L1_ffn_shared_up"], a["L1_ffn_shared_down"], MOE1)]
    moe1 += [expert(a["L1_ffn_routed_gate"][j], a["L1_ffn_routed_up"][j], a["L1_ffn_routed_down"][j], MOE1)
             for j in range(E1)]

    arrays = {"patches": x, "tokw": tokw, "consts": consts, "rows": rows, "wa": wa, "l1w": l1w, "wo": wo,
              "moe0w": np.stack(moe0), "moe1w": np.stack(moe1)}
    arrays = {k: np.ascontiguousarray(v, dtype=np.float32) for k, v in arrays.items()}
    nc = bacc.Bacc("TRN2", target_bir_lowering=False, num_devices=1)
    args = [nc.dram_tensor(k, v.shape, F32, kind="ExternalInput").ap() for k, v in arrays.items()]
    out = nc.dram_tensor("out", (TOK, D), F32, kind="ExternalOutput").ap()
    tower(nc, *args, out)
    got = run(nc, [arrays], core_ids=[0]).results[0]["out"]
    return got.reshape(IMAGES, SEQ, D)
```

```python
from contextlib import ExitStack

import concourse.bass as bass
from concourse import mybir

F32 = mybir.dt.float32
F32R = mybir.dt.float32r
I32 = mybir.dt.int32
ALU = mybir.AluOpType
ACT = mybir.ActivationFunctionType
AX = mybir.AxisListType

IMAGES, CHANNELS, SIDE, PATCH = 32, 3, 96, 16
SEQ = (SIDE // PATCH) ** 2
TOK = IMAGES * SEQ
D = 192
P = 128
TILES = TOK // P
CH = 3
CHW = TOK // CH
PATCH_K = CHANNELS * PATCH * PATCH // P
GI = 3
GW = GI * SEQ
GROUPS = -(-IMAGES // GI)
XW = GROUPS * GW
BATCHES = [(0, 4), (4, 8), (8, GROUPS)]
HALF = D // 2
HEADS = 12
HD = D // HEADS
QKVG = 4 * D + 2 * HEADS
L1H = QKVG // 2 // 2 * 2
SLOT = 64
E0, F0 = 8, 768
E1, F1 = 3, 384
E1P = 4
PICKS = 2
WT = 256
WORKS = (PICKS * TOK - E0) // WT + E0
SLOTS = WORKS * WT
FULL = -(-TOK // WT)
LIMIT = 10.0
SILU_LIMIT = 9.999546021312976
NWA = 3 * D + E0 + E1P
EPS = 1e-5

ZW = 1536

C_ID = 0
C_MASK = C_ID + P
C_TRI = C_MASK + GW
C_COS = C_TRI + GW
C_SIN = C_COS + HD
C_T = C_SIN + HD
C_RT = C_T + 1
C_NRT = C_RT + 1
C_LOW = C_NRT + 1
C_BEFORE = C_LOW + E0 * E0
C_ONE = C_BEFORE + P
C_FULL = C_ONE + P
C_WORK = C_FULL + FULL
NCONST = C_WORK + WORKS
R_TOKB = 0
R_GB = R_TOKB + D
R_RB = R_GB + E0
R_MU = R_RB + E1P
R_TAU = R_MU + D
NROWS = R_TAU + HEADS


class Moe:

    def __init__(self, experts, width, clip):
        self.works = experts + 1
        self.width = width
        self.clip = clip
        self.fc = width // P
        self.cols = 4 * width + self.fc * D
        self.pieces = 4 + 2


MOE0, MOE1 = Moe(E0, F0, True), Moe(E1, F1, False)


class Steps:

    def __init__(self, eng, sem):
        self.eng, self.sem, self.n = eng, sem, 0

    def step(self, ins):
        ins.then_inc(self.sem, 1)
        self.n += 1
        return self.n

    def settle(self, n=None):
        self.eng.wait_ge(self.sem, self.n if n is None else n)

    def link(self, ins):
        self.step(ins)
        self.settle()


def tower(nc, patches, tokw, consts, rows, wa, l1w, wo, moe0w, moe0d, moe1w, xs, ys, out):
    with ExitStack() as ctx:
        def sb(name, shape, dt=F32, scope=ctx):
            return scope.enter_context(nc.sbuf_tensor(name, shape, dt))

        def sem(name):
            return ctx.enter_context(nc.semaphore(name))

        bank = [ctx.enter_context(nc.psum_tensor(f"bank{i}", [P, 512], F32)) for i in range(8)]

        H = sb("H", [P, TILES, D])
        Y = sb("Y", [P, TILES, 256])
        X01h = sb("X01h", [P, XW], F32R)
        X01l = sb("X01l", [P, XW], F32R)
        X2h = sb("X2h", [P, XW], F32R)
        X2l = sb("X2l", [P, XW], F32R)
        const = sb("const", [P, NCONST])
        row = sb("row", [P, NROWS])
        WAh = sb("WAh", [P, NWA], F32R)
        WAl = sb("WAl", [P, NWA], F32R)
        WA2 = sb("WA2", [P, NWA], F32R)
        L1h = sb("L1h", [P, QKVG], F32R)
        L1l = sb("L1l", [P, QKVG], F32R)
        L12 = sb("L12", [P, QKVG], F32R)
        wo_sb = sb("wo_sb", [HALF, 2, D])
        stat = sb("stat", [P, TILES, 6])
        mv = sb("mv", [P, TILES, 2])
        ve = sb("ve", [P, TILES])
        sd = sb("sd", [P, TILES])
        rstd = sb("rstd", [P, TILES])
        comb = sb("comb", [P, TILES, E0])
        comb1 = sb("comb1", [P, TILES, E1])

        ident = const[:, C_ID:C_ID + P]
        amask = const[0:GW, C_MASK:C_MASK + GW]
        tri = const[0:GW, C_TRI:C_TRI + GW]

        tau = sb("tau", [GW, HEADS])
        tmu = sb("tmu", [GW, D])
        tden = sb("tden", [GW, HEADS])
        sT = sb("sT", [HEADS, XW])
        smax = sb("smax", [HEADS, GROUPS * GI])
        rt = [sb(f"rt{i}", [P, TILES * E0]) for i in range(6)]
        rk = [sb(f"rk{i}", [P, TILES * E0 * E0]) for i in range(2)]
        rsum = [sb(f"rsum{i}", [P, TILES]) for i in range(2)]
        sel = sb("sel", [P, TILES * E0])
        count = sb("count", [P, E0])
        works = sb("works", [P, E0])
        base = sb("base", [P, E0])
        slot = sb("slot", [P, TILES * E0])
        smx = sb("smx", [P, TILES])
        smn = sb("smn", [P, TILES])
        wpick = sb("wpick", [P, PICKS, TILES])
        idx = sb("idx", [P, PICKS, TILES], I32)
        eidf = sb("eidf", [P, WORKS])
        eid = sb("eid", [P, WORKS], I32)

        r1a, r1b = ExitStack(), ExitStack()
        W0 = []
        with r1a:
            for b in range(2):
                W0.append(dict(
                    stage=sb(f"stage{b}", [P, 4 * F0], F32, r1a),
                    h=sb(f"w0h{b}", [P, 2, F0], F32R, r1a), l=sb(f"w0l{b}", [P, 2, F0], F32R, r1a),
                    t=sb(f"w0t{b}", [P, 2, F0], F32R, r1a), down=sb(f"w0d{b}", [P, MOE0.fc, D], F32, r1a)))
            XR = [sb(f"XR{b}", [P, WT // P, 256], F32, r1a) for b in range(2)]
            XWh = [sb(f"XWh{b}", [P, 2 * WT], F32R, r1a) for b in range(2)]
            XWl = [sb(f"XWl{b}", [P, 2 * WT], F32R, r1a) for b in range(2)]
            YO = [sb(f"YO{b}", [P, WT // P, D], F32, r1a) for b in range(2)]
            with ExitStack() as s:
                patch = sb("patch", [P, PATCH_K * TOK], F32, s)
                tokw_sb = sb("tokw_sb", [P, PATCH_K, D], F32, s)
                zero = sb("zero", [P, ZW], F32, s)
            with ExitStack() as s:
                qT = sb("qT", [HALF, 2, XW], F32, s)
                kT = sb("kT", [HALF, 2, XW], F32, s)
                V = sb("V", [GW, GROUPS, D], F32, s)
                Pm = sb("Pm", [GW, GROUPS, GW], F32, s)
                PT = sb("PT", [GW, GROUPS, GW], F32, s)
                oT = sb("oT", [HALF, 2, XW], F32, s)
                mx = sb("mx", [GW, GROUPS], F32, s)
                rs = sb("rs", [GW, GROUPS], F32, s)
                rr = sb("rr", [GW, GROUPS], F32, s)
            with ExitStack() as s:
                A0 = dict(s=[sb(f"a0s{b}", [P, CHW], F32, s) for b in range(2)],
                          t=[sb(f"a0t{b}", [P, CHW], F32, s) for b in range(2)],
                          h=[sb(f"a0h{b}", [P, MOE0.fc, CHW], F32, s) for b in range(2)])
                G = sb("G", [P, TILES, PICKS, D], F32, s)
        with r1b:
            QK = sb("QK", [GW, GROUPS, QKVG], F32, r1b)
            rotA = sb("rotA", [GW, 4, 2 * D], F32, r1b)
            rotB = sb("rotB", [GW, 4, 2 * D], F32, r1b)
            qw = sb("qw", [GW, 4, HEADS, SLOT], F32, r1b)
            kw = sb("kw", [GW, 4, HEADS, SLOT], F32, r1b)
            AT = sb("AT", [GW, HEADS, GW], F32, r1b)
            ES = sb("ES", [GW, GROUPS, 2 * HEADS], F32, r1b)
            SG = sb("SG", [GW, GROUPS, 2 * HEADS], F32, r1b)
            CO = sb("CO", [GW, 3, GROUPS, HEADS], F32, r1b)
            W1 = []
            for b in range(2):
                W1.append(dict(
                    stage=sb(f"stage1{b}", [P, MOE1.cols], F32, r1b),
                    h=sb(f"w1h{b}", [P, 2, F1], F32R, r1b), l=sb(f"w1l{b}", [P, 2, F1], F32R, r1b),
                    t=sb(f"w1t{b}", [P, 2, F1], F32R, r1b),
                    dh=sb(f"d1h{b}", [P, MOE1.fc, D], F32R, r1b), dl=sb(f"d1l{b}", [P, MOE1.fc, D], F32R, r1b)))
            CK = sb("CK", [GW, 2, 4, HEADS], F32, r1b)
            CQ = sb("CQ", [GW, 3, 4, HEADS], F32, r1b)
            nrm = sb("nrm", [GW, 4, 2 * HEADS], F32, r1b)
            rn = sb("rn", [GW, 4, 2 * HEADS], F32, r1b)
            qkT = sb("qkT", [P, 12, GW], F32, r1b)
        with ExitStack() as s:
            A1 = moe_buffers(sb, s, MOE1, "a1")
        ld_patch = [sem(f"ld_patch{j}") for j in range(5)]
        ld_tokw, ld_const, ld_row, ld_wo = sem("ld_tokw"), sem("ld_const"), sem("ld_row"), sem("ld_wo")
        ld_stage = [sem(f"ld_stage{b}") for b in range(2)]
        ld_stage1 = [sem(f"ld_stage1{b}") for b in range(2)]
        pads = sem("pads")
        split_hi, split_lo = sem("split_hi"), sem("split_lo")
        tok_done, tok_h = sem("tok_done"), sem("tok_h")
        dve_step, act_step, pool_step = sem("dve_step"), sem("act_step"), sem("pool_step")
        ln_var, ln_sd, ln_y, ln_xt, ln_hi, ln_lo = (sem("ln_" + s) for s in ("var", "sd", "y", "xt", "hi", "lo"))
        proj_done = sem("proj_done")
        proj_out = [sem("proj_act"), sem("proj_dve")]
        a0_s, a0_shift, a0_exp, a0_p, a0_pt, a0_ptc, a0_o, a0_back, a0_h = (
            sem("a0_" + s) for s in ("s", "shift", "exp", "p", "pt", "ptc", "o", "back", "h"))
        a0_oc = [sem("a0_oc_act"), sem("a0_oc_dve")]
        rt_z, rt_neg, rt_e, rt_u, rt_ln, rt_sp, rt_sc = (
            sem("rt_" + s) for s in ("z", "neg", "e", "u", "ln", "sp", "sc"))
        rt1_z, rt1_b, rt1_p = sem("rt1_z"), sem("rt1_b"), sem("rt1_p")
        moe_sems = []
        r_sel, r_pos, r_idx, r_eid = (sem("r_" + s) for s in ("sel", "pos", "idx", "eid"))
        zeroed, zero_set, scattered = sem("zeroed"), sem("zero_set"), sem("scattered")
        ld_w2 = [sem(f"ld_w2{b}") for b in range(2)]
        ld_x = [sem(f"ld_x{b}") for b in range(2)]
        st_y = [sem(f"st_y{b}") for b in range(2)]
        ld_g = [sem(f"ld_g{c}") for c in range(CH)]
        x_T, x_hi, x_lo, y_done, mixed = (sem(s) for s in ("x_T", "x_hi", "x_lo", "y_done", "mixed"))
        for m in range(2):
            moe_sems.append({k: sem(f"moe{m}_{k}") for k in (
                "w_hi", "w_lo", "gu_ready", "silu_ready", "clip_ready", "h_ready", "hh_ready", "hl_ready",
                "down_ready", "acc_done")})
        l1_proj = sem("l1_proj")
        l1_out = [sem("l1_out_act"), sem("l1_out_dve")]
        (l1_us, l1_s, l1_st, l1_sh, l1_ex, l1_et, l1_es, l1_cum, l1_sig, l1_tau, l1_co) = (
            sem("l1_" + s) for s in ("us", "s", "st", "sh", "ex", "et", "es", "cum", "sig", "tau", "co"))
        (l1_rope, l1_sw, l1_sq, l1_n2, l1_nr, l1_cq, l1_qw, l1_kw, l1_T, l1_Tca, l1_Tcd, l1_A, l1_Am,
         l1_O, l1_Oc, l1_cen, l1_csq, l1_var, l1_std, l1_on, l1_oT, l1_oTc, l1_f, l1_h) = (
            sem("l1_" + s) for s in ("rope", "sw", "sq", "n2", "nr", "cq", "qw", "kw", "T", "Tca", "Tcd",
                                     "A", "Am", "O", "Oc", "cen", "csq", "var", "std", "on", "oT", "oTc", "f", "h"))
        pad_w = sem("pad_w")
        stored = sem("stored")

        def terms(weights, wcols, xcols):
            wh, wl, w2 = weights
            return [(X01h[:, xcols], wh[wcols]), (X01h[:, xcols], wl[wcols]), (X01l[:, xcols], wh[wcols]),
                    (X2h[:, xcols], w2[wcols]), (X2l[:, xcols], w2[wcols])]

        def wcols2(a, b):
            return (slice(0, P), slice(a, b))

        OT = Y[0:HALF].rearrange("p a b -> p (a b)").rearrange("p (h n) -> p h n", h=2)
        W1b = Y[0:GW].rearrange("p a b -> p (a b)")[:, 0:GROUPS * D].rearrange("p (g d) -> p g d", d=D)

        block = ctx.enter_context(nc.Block())
        PBLK = [(2 * j, min(2 * j + 2, TILES)) for j in range(5)]

        @block.sync
        def _(sp):
            sp.dma_start(tokw_sb[:], tokw).then_inc(ld_tokw, 16)
            for j, (t0, t1) in enumerate(PBLK):
                a, b = t0 * P * PATCH_K, t1 * P * PATCH_K
                sp.dma_start(patch[:, a:b], patches[:, a:b]).then_inc(ld_patch[j], 16)
                if j == 0:
                    sp.dma_start(row[:], rows).then_inc(ld_row, 16)
                    sp.dma_start(const[:], consts).then_inc(ld_const, 16)
            sp.dma_start(W0[0]["stage"][:, 0:2 * NWA], wa).then_inc(ld_stage[0], 16)
            sp.dma_start(W0[1]["stage"][:, 0:2 * QKVG], l1w).then_inc(ld_stage[1], 16)
            sp.dma_start(wo_sb[:], wo).then_inc(ld_wo, 16)
            sp.wait_ge(zero_set, 1)
            xz = xs.rearrange("(p j) d -> p (j d)", p=P)
            for j in range(SLOTS // P * D // ZW):
                sp.dma_start(xz[:, j * ZW:(j + 1) * ZW], zero[:]).then_inc(zeroed, 16)
            S = moe_sems[0]
            sp.wait_ge(split_lo, 2)
            sp.dma_start(W0[0]["stage"][:], moe0w[0]).then_inc(ld_stage[0], 16)
            sp.dma_start(W0[0]["down"].rearrange("p a b -> p (a b)"), moe0d[0]).then_inc(ld_w2[0], 16)
            sp.wait_ge(split_lo, 4)
            sp.wait_ge(r_eid, 1)
            experts = {}

            def load_weights(n):
                if n >= 2:
                    sp.wait_ge(S["w_lo"], 4 * (n - 1))
                experts[n] = sp.value_load(eid[0:1, n - 1:n], min_val=1, max_val=E0)
                sp.dma_start(W0[n % 2]["stage"][:], moe0w[bass.ds(experts[n], 1)].rearrange(
                    "e p c -> (e p) c")).then_inc(ld_stage[n % 2], 16)

            def load_down(n):
                if n >= 2:
                    sp.wait_ge(S["down_ready"], 9 + 2 * (n - 2))
                sp.dma_start(W0[n % 2]["down"].rearrange("p a b -> p (a b)"), moe0d[bass.ds(
                    experts[n], 1)].rearrange("e p c -> (e p) c")).then_inc(ld_w2[n % 2], 16)

            def load_rows(n):
                if n >= 3:
                    sp.wait_ge(x_T, n - 2)
                rows = xs[(n - 1) * WT:n * WT, :].rearrange("(a p) d -> p a d", p=P)
                sp.dma_start(XR[n % 2][:, :, 0:D], rows).then_inc(ld_x[n % 2], 16)
                sp.dma_start(XR[n % 2][:, :, D:256], rows[:, :, P:D]).then_inc(ld_x[n % 2], 16)

            load_weights(1)
            load_down(1)
            sp.wait_ge(scattered, 16 * PICKS * TILES)
            load_rows(1)
            load_weights(2)
            load_rows(2)
            for n in range(2, WORKS + 1):
                if n < WORKS:
                    load_weights(n + 1)
                if n > 2:
                    load_rows(n)
                load_down(n)
            sp.wait_ge(mixed, TILES)
            for n in range(MOE1.works):
                if n >= 2:
                    sp.wait_ge(moe_sems[1]["w_lo"], MOE1.pieces * (n - 1))
                sp.dma_start(W1[n % 2]["stage"][:], moe1w[n]).then_inc(ld_stage1[n % 2], 16)
            last = (MOE1.works - 1) * TILES
            for c in range(CH):
                sp.wait_ge(moe_sems[1]["acc_done"], last + 3 * (c + 1))
                sp.dma_start(out.rearrange("(t p) d -> p t d", p=P)[:, 3 * c:3 * c + 3, :],
                             H[:, 3 * c:3 * c + 3, :]).then_inc(stored, 16)
            sp.wait_ge(stored, 16 * CH)

        def moe_pe(pe, m, W, A, S, n, odd, first):
            M, (g0, g1), (u0, u1), (d0, d1) = m, (0, 1), (2, 3), (4, 5)
            FC = M.fc

            def gate_up(c):
                if c == 0:
                    pe.wait_ge(S["w_lo"], n * M.pieces + M.pieces)
                for fc in range(FC):
                    par = ((3 * odd + c) * FC + fc) % 2
                    if not (first and c == 0 and fc < 2):
                        pe.wait_ge(S["h_ready"], n * (3 * FC) + (c * FC + fc - 1))
                    for mat, bk in ((0, (g0, g1)[par]), (1, (u0, u1)[par])):
                        w = W[odd]
                        ts = terms((w["h"][:], w["l"][:], w["t"][:]),
                                   (slice(0, P), mat, slice(fc * P, fc * P + P)), slice(c * CHW, c * CHW + CHW))
                        for i, (x, wt) in enumerate(ts):
                            last = nc.tensor.matmul(bank[bk][:, 0:CHW], wt, x, start=(i == 0), stop=(i == 4))
                    last.then_inc(S["gu_ready"], 1)

            def down(nn, o, c):
                q = (o * 3 + c) % 2
                pe.wait_ge(S["hl_ready"], nn * (3 * FC) + (c + 1) * FC)
                for t in range(3):
                    dpar = (q + t) % 2
                    if not (first and c == 0 and t < 2 and nn is n):
                        pe.wait_ge(S["acc_done"], nn * 9 + (3 * c + t - 1))
                    w = W[o]
                    cols = slice(t * P, t * P + P)
                    k = 0
                    for fc in range(FC):
                        hh, hl = A["hh"][q][:, fc, cols], A["hl"][q][:, fc, cols]
                        for lhs, rhs in ((hh, w["dh"]), (hh, w["dl"]), (hl, w["dh"])):
                            last = nc.tensor.matmul(bank[(d0, d1)[dpar]][:, 0:D], lhs, rhs[:, fc, :],
                                                    start=(k == 0), stop=(k == 3 * FC - 1))
                            k += 1
                    last.then_inc(S["down_ready"], 1)

            gate_up(0)
            if not first:
                down(n - 1, 1 - odd, 2)
            gate_up(1)
            down(n, odd, 0)
            gate_up(2)
            down(n, odd, 1)
            return down

        def split_hi_piece(m, W, odd, i):
            w, F = W[odd], m.width
            if i < 4:
                mat, two = i // 2, i % 2
                src = w["stage"][:, (2 * mat + two) * F:(2 * mat + two + 1) * F]
                return src, (w["t"] if two else w["h"])[:, mat, :]
            half = m.fc // 2 if m.fc % 2 == 0 else m.fc - 1
            a, b = (0, half) if i == 4 else (half, m.fc)
            src = w["stage"][:, 4 * F + a * D:4 * F + b * D].rearrange("p (f d) -> p f d", d=D)
            return src, w["dh"][:, a:b, :]

        def split_lo_piece(m, W, odd, i):
            w, F = W[odd], m.width
            src, hi = split_hi_piece(m, W, odd, i)
            if i < 4:
                mat, two = i // 2, i % 2
                if two:
                    t = w["t"][64:P, mat, :]
                    return src[64:P], t, t
                return src, hi, w["l"][:, mat, :]
            half = m.fc // 2 if m.fc % 2 == 0 else m.fc - 1
            a, b = (0, half) if i == 4 else (half, m.fc)
            return src, hi, w["dl"][:, a:b, :]

        def moe_weights_act(act, m, W, S, L, n, odd, i, used, n_pairs):
            if i == 0:
                act.wait_ge(L[odd], n_pairs)
                if used is not None:
                    act.wait_ge(S["down_ready"], used)
            src, hi = split_hi_piece(m, W, odd, i)
            nc.scalar.activation(hi, src, ACT.Copy).then_inc(S["w_hi"], 1)

        def moe_weights_pool(pool, m, W, S, n, odd):
            for i in range(m.pieces):
                if i or not isinstance(n, int) or n:
                    pool.wait_ge(S["w_lo"], n * m.pieces + i)
                pool.wait_ge(S["w_hi"], n * m.pieces + (i + 1))
                src, hi, dst = split_lo_piece(m, W, odd, i)
                nc.gpsimd.tensor_tensor(dst, src, hi.bitcast(F32), ALU.subtract).then_inc(S["w_lo"], 1)

        def moe_act(act, m, W, A, S, L, n, odd, first, last, n_pairs):
            FC = m.fc
            for c in range(CH):
                for fc in range(FC):
                    par = ((3 * odd + c) * FC + fc) % 2
                    k1 = c * FC + fc + 1
                    act.wait_ge(S["gu_ready"], n * (3 * FC) + k1)
                    if not (first and k1 <= 2):
                        act.wait_ge(S["h_ready"], n * (3 * FC) + (k1 - 2))
                    nc.scalar.activation(A["s"][par][:], bank[par][:, 0:CHW], ACT.Silu).then_inc(S["silu_ready"], 1)
                    if not (first and k1 == 1):
                        moe_high(act, m, A, S, n, odd, c * FC + fc - 1)
                    i = (c - 1) * FC + fc
                    if not last and 0 <= i < m.pieces:
                        used = n * 9 if not first else None
                        moe_weights_act(act, m, W, S, L, n + 1, 1 - odd, i, used, n_pairs)

        def moe_high(act, m, A, S, n, odd, k):
            FC = m.fc
            kk = (3 * odd * FC + k) % (6 * FC)
            q, fc, par = (kk // FC) % 2, kk % FC, kk % 2
            act.wait_ge(S["h_ready"], n * (3 * FC) + (k + 1))
            nc.scalar.activation(A["hh"][q][:, fc, :], A["hf"][par][:], ACT.Copy).then_inc(S["hh_ready"], 1)

        def moe_low(dve, m, A, S, n, odd, k):
            FC = m.fc
            kk = (3 * odd * FC + k) % (6 * FC)
            q, fc, par = (kk // FC) % 2, kk % FC, kk % 2
            dve.wait_ge(S["hh_ready"], n * (3 * FC) + (k + 1))
            nc.vector.tensor_tensor(A["hl"][q][:, fc, :], A["hf"][par][:], A["hh"][q][:, fc, :].bitcast(F32),
                                    ALU.subtract).then_inc(S["hl_ready"], 1)

        def moe_acc(dve, m, S, n, odd, c, weight):
            q = (3 * odd + c) % 2
            for t in range(3):
                tile = 3 * c + t
                dve.wait_ge(S["down_ready"], n * 9 + (tile + 1))
                if weight is None:
                    nc.vector.tensor_tensor(H[:, tile, :], bank[4 + (q + t) % 2][:, 0:D], H[:, tile, :],
                                            ALU.add).then_inc(S["acc_done"], 1)
                else:
                    dve.wait_ge(S["acc_done"], n * 9 + (tile - 8))
                    nc.vector.scalar_tensor_tensor(
                        out=H[:, tile, :], in0=bank[4 + (q + t) % 2][:, 0:D], scalar=weight(tile),
                        in1=H[:, tile, :], op0=ALU.mult, op1=ALU.add).then_inc(S["acc_done"], 1)

        def moe_dve(dve, m, A, S, n, odd, first, weight, before):
            FC = m.fc
            for c in range(CH):
                for fc in range(FC):
                    par = ((3 * odd + c) * FC + fc) % 2
                    k1 = c * FC + fc + 1
                    dve.wait_ge(S["gu_ready"], n * (3 * FC) + k1)
                    if m.clip:
                        nc.vector.tensor_scalar(A["t"][par][:], bank[2 + par][:, 0:CHW], LIMIT, -LIMIT, ALU.min,
                                                ALU.max).then_inc(S["clip_ready"], 1)
                    if not (first and k1 == 1):
                        moe_low(dve, m, A, S, n, odd, k1 - 2)
                    dve.wait_ge(S["silu_ready"], n * (3 * FC) + k1)
                    if m.clip:
                        dve.wait_ge(S["clip_ready"], n * (3 * FC) + k1)
                        ins = nc.vector.scalar_tensor_tensor(out=A["hf"][par][:], in0=A["s"][par][:],
                                                             scalar=SILU_LIMIT, in1=A["t"][par][:], op0=ALU.min,
                                                             op1=ALU.mult)
                    else:
                        ins = nc.vector.tensor_tensor(A["hf"][par][:], bank[2 + par][:, 0:CHW], A["s"][par][:],
                                                      ALU.mult)
                    ins.then_inc(S["h_ready"], 1)
                if c == 0 and not first:
                    moe_acc(dve, m, S, n - 1, 1 - odd, 2, before)
                elif c > 0:
                    moe_acc(dve, m, S, n, odd, c - 1, weight)

        FC0 = MOE0.fc
        S0 = moe_sems[0]

        def e_operands(n, c, w, cols):
            ws = [w["h"][cols], w["l"][cols], w["h"][cols], w["t"][cols], w["t"][cols]]
            if c is not None:
                xc = slice(c * CHW, (c + 1) * CHW)
                xs_ = [X01h[:, xc], X01h[:, xc], X01l[:, xc], X2h[:, xc], X2l[:, xc]]
            else:
                h, l = XWh[n], XWl[n]
                xs_ = [h[:, 0:WT], h[:, 0:WT], l[:, 0:WT], h[:, WT:2 * WT], l[:, WT:2 * WT]]
            return list(zip(xs_, ws))

        def e_gate_up(pe, q, n, par, c):
            width = WT if c is None else CHW
            if c is None:
                pe.wait_ge(x_lo, n)
            pe.wait_ge(S0["w_lo"], n * 4 + 4)
            for fc in range(FC0):
                if not (isinstance(q, int) and q == 0 and fc < 2):
                    pe.wait_ge(S0["h_ready"], q * FC0 + (fc - 1))
                for mat in range(2):
                    for i, (x, w) in enumerate(e_operands(par, c, W0[par], (slice(0, P), mat,
                                                                            slice(fc * P, fc * P + P)))):
                        last = nc.tensor.matmul(bank[2 * mat + fc % 2][:, 0:width], w, x, start=(i == 0),
                                                stop=(i == 4))
                last.then_inc(S0["gu_ready"], 1)

        def e_down(pe, q, qpar, n, par, shared, loaded):
            pe.wait_ge(S0["h_ready"], q * FC0 + FC0)
            pe.wait_ge(ld_w2[par], loaded)
            for t in range(3 if shared else 2):
                if shared:
                    d = 3 * q + t
                    if d >= 2:
                        pe.wait_ge(S0["acc_done"], d - 1)
                elif isinstance(n, int) and n == 1:
                    pe.wait_ge(S0["acc_done"], 8 + t)
                else:
                    pe.wait_ge(y_done, n * 2 + (t - 3))
                for fc in range(FC0):
                    last = nc.tensor.matmul(bank[e_bank(qpar, t, shared)][:, 0:D],
                                            A0["h"][qpar][:, fc, t * P:(t + 1) * P], W0[par]["down"][:, fc, :],
                                            start=(fc == 0), stop=(fc == FC0 - 1))
                last.then_inc(S0["down_ready"], 1)

        def e_bank(qpar, t, shared):
            return 4 + ((qpar + t) % 2 if shared else (1 + t) % 2)

        def e_rows(pe, n, par, loaded):
            pe.wait_ge(ld_x[par], loaded)
            if not (isinstance(n, int) and n == 1):
                pe.wait_ge(x_lo, n - 1)
            for half in range(2):
                for t in range(WT // P):
                    last = nc.tensor.transpose(bank[6][:, half * WT + t * P:half * WT + (t + 1) * P],
                                               XR[par][:, t, half * P:(half + 1) * P], ident)
            last.then_inc(x_T, 1)

        def e_split_act(act, n, par, i, staged, q):
            if i == 0:
                act.wait_ge(ld_stage[par], staged)
                if q is not None:
                    act.wait_ge(S0["gu_ready"], q * FC0)
            mat, two = i // 2, i % 2
            nc.scalar.activation(W0[par]["t" if two else "h"][:, mat, :],
                                 W0[par]["stage"][:, (2 * mat + two) * F0:(2 * mat + two + 1) * F0],
                                 ACT.Copy).then_inc(S0["w_hi"], 1)

        def e_split_pool(pool, n, par):
            for i in range(4):
                pool.wait_ge(S0["w_hi"], n * 4 + (i + 1))
                if i or not isinstance(n, int) or n:
                    pool.wait_ge(S0["w_lo"], n * 4 + i)
                mat, two = i // 2, i % 2
                src = W0[par]["stage"][:, (2 * mat + two) * F0:(2 * mat + two + 1) * F0]
                if two:
                    dst = W0[par]["t"][64:P, mat, :]
                    ins = nc.gpsimd.tensor_tensor(dst, src[64:P], dst.bitcast(F32), ALU.subtract)
                else:
                    ins = nc.gpsimd.tensor_tensor(W0[par]["l"][:, mat, :], src, W0[par]["h"][:, mat, :].bitcast(F32),
                                                  ALU.subtract)
                ins.then_inc(S0["w_lo"], 1)

        def e_act(act, q, width, following, rows, store):
            for fc in range(FC0):
                act.wait_ge(S0["gu_ready"], q * FC0 + (fc + 1))
                if not (isinstance(q, int) and q == 0 and fc < 2):
                    act.wait_ge(S0["h_ready"], q * FC0 + (fc - 1))
                nc.scalar.activation(A0["s"][fc % 2][:, 0:width], bank[fc % 2][:, 0:width],
                                     ACT.Silu).then_inc(S0["silu_ready"], 1)
                if following is not None and 1 <= fc <= 4:
                    e_split_act(act, *following[:2], fc - 1, *following[2:])
                if store is not None and fc == 5:
                    e_store(act, *store)
            if rows is not None:
                n, par, used = rows
                act.wait_ge(x_T, n)
                if used is not None:
                    act.wait_ge(S0["gu_ready"], used)
                nc.scalar.activation(XWh[par][:], bank[6][:], ACT.Copy).then_inc(x_hi, 1)

        def e_store(act, n, par):
            act.wait_ge(y_done, n * 2)
            dst = ys[bass.ds(n - 1, 1)] if not isinstance(n, int) else ys[n - 1:n]
            act.dma_start(dst.rearrange("w (a p) d -> p (w a) d", p=P), YO[par][:]).then_inc(st_y[par], 16)

        def e_dve(dve, q, qpar, width, freed, rows, before):
            if freed is not None:
                dve.wait_ge(S0["down_ready"], freed)
            for fc in range(FC0):
                dve.wait_ge(S0["gu_ready"], q * FC0 + (fc + 1))
                nc.vector.tensor_scalar(A0["t"][fc % 2][:, 0:width], bank[2 + fc % 2][:, 0:width], LIMIT, -LIMIT,
                                        ALU.min, ALU.max).then_inc(S0["clip_ready"], 1)
                dve.wait_ge(S0["silu_ready"], q * FC0 + (fc + 1))
                dve.wait_ge(S0["clip_ready"], q * FC0 + (fc + 1))
                nc.vector.scalar_tensor_tensor(out=A0["h"][qpar][:, fc, 0:width], in0=A0["s"][fc % 2][:, 0:width],
                                               scalar=SILU_LIMIT, in1=A0["t"][fc % 2][:, 0:width], op0=ALU.min,
                                               op1=ALU.mult).then_inc(S0["h_ready"], 1)
            if rows is not None:
                n, par = rows
                dve.wait_ge(x_hi, n)
                nc.vector.tensor_tensor(XWl[par][:], bank[6][:], XWh[par][:].bitcast(F32),
                                        ALU.subtract).then_inc(x_lo, 1)
            if before is not None:
                before()

        def e_acc(dve, c):
            for t in range(3):
                dve.wait_ge(S0["down_ready"], 3 * c + t + 1)
                nc.vector.tensor_tensor(H[:, 3 * c + t, :], bank[e_bank(c % 2, t, True)][:, 0:D], H[:, 3 * c + t, :],
                                        ALU.add).then_inc(S0["acc_done"], 1)

        def e_copy(dve, n, par, stored_):
            if stored_ is not None:
                dve.wait_ge(st_y[par], stored_)
            for t in range(WT // P):
                dve.wait_ge(S0["down_ready"], n * 2 + (8 + t))
                nc.vector.tensor_copy(YO[par][:, t, :], bank[e_bank(0, t, False)][:, 0:D]).then_inc(y_done, 1)

        @block.tensor
        def _(pe):
            pe.wait_ge(ld_tokw, 16)
            for j, (t0, t1) in enumerate(PBLK):
                pe.wait_ge(ld_patch[j], 16)
                n = (t1 - t0) * P
                pb = patch[:, t0 * P * PATCH_K:t1 * P * PATCH_K].rearrange("p (k n) -> p k n", n=n)
                for t in range(t1 - t0):
                    for k in range(PATCH_K):
                        last = nc.tensor.matmul(bank[j][:, t * D:(t + 1) * D], pb[:, k, t * P:(t + 1) * P],
                                                tokw_sb[:, k, :], start=(k == 0), stop=(k == PATCH_K - 1))
                last.then_inc(tok_done, 1)

            def transposes(k):
                if k == 0:
                    pe.wait_ge(ld_const, 16)
                for c in range(CH):
                    pe.wait_ge(ln_y, 3 * k + c + 1)
                    for half in range(2):
                        for t in range(3):
                            last = nc.tensor.transpose(bank[2 * c + half][:, t * P:(t + 1) * P],
                                                       Y[:, 3 * c + t, half * P:(half + 1) * P], ident)
                    last.then_inc(ln_xt, 1)

            transposes(0)
            pe.wait_ge(ln_lo, 6)
            pe.wait_ge(split_lo, 2)
            pe.wait_ge(pads, 4)
            wa3 = (WAh, WAl, WA2)
            jobs = [("t", mat * D + half * HALF, c) for mat in range(2) for half in range(2) for c in range(3)]
            jobs += [("v", g, 0) for g in range(0, GROUPS, 2)]
            for j, (kind, a, c) in enumerate(jobs):
                if j >= 8:
                    pe.wait_ge(proj_out[j % 2], (j - 8) // 2 + 1)
                if kind == "t":
                    w3 = XW // 3
                    for i, (x, w) in enumerate(terms(wa3, wcols2(a, a + HALF), slice(c * w3, (c + 1) * w3))):
                        last = nc.tensor.matmul(bank[j % 8][0:HALF, 0:w3], w, x, start=(i == 0), stop=(i == 4))
                else:
                    for g in range(a, min(a + 2, GROUPS)):
                        for i, (x, w) in enumerate(terms(wa3, wcols2(2 * D, 3 * D), slice(g * GW, (g + 1) * GW))):
                            last = nc.tensor.matmul(bank[j % 8][0:GW, (g - a) * D:(g - a + 1) * D], x, w,
                                                    start=(i == 0), stop=(i == 4))
                last.then_inc(proj_done, 1)
            pe.wait_ge(proj_out[0], 7)
            pe.wait_ge(proj_out[1], 6)
            for b, (g0, g1) in enumerate(BATCHES):
                for g in range(g0, g1):
                    cols = slice(g * GW, (g + 1) * GW)
                    for half in range(2):
                        last = nc.tensor.matmul(bank[2 + b][0:GW, (g - g0) * GW:(g - g0 + 1) * GW],
                                                qT[:, half, cols], kT[:, half, cols], start=(half == 0),
                                                stop=(half == 1))
                last.then_inc(a0_s, 1)
            pe.wait_ge(proj_out[0], 9)
            pe.wait_ge(proj_out[1], 9)
            for b, (g0, g1) in enumerate(BATCHES):
                pe.wait_ge(a0_p, b + 1)
                for g in range(g0, g1):
                    last = nc.tensor.transpose(bank[5 + b][0:GW, (g - g0) * GW:(g - g0 + 1) * GW], Pm[:, g, :],
                                               ident[0:GW, 0:GW])
                last.then_inc(a0_pt, 1)
            for b, (g0, g1) in enumerate(BATCHES):
                pe.wait_ge(a0_ptc, b + 1)
                for half in range(2):
                    for g in range(g0, g1):
                        last = nc.tensor.matmul(bank[2 * b + half][0:HALF, (g - g0) * GW:(g - g0 + 1) * GW],
                                                V[:, g, half * HALF:(half + 1) * HALF], PT[:, g, :],
                                                start=True, stop=True)
                    last.then_inc(a0_o, 1)
            pe.wait_ge(a0_oc[0], 3)
            pe.wait_ge(a0_oc[1], 3)
            for j, (t0, t1) in enumerate(PBLK):
                for t in range(t0, t1):
                    for half in range(2):
                        last = nc.tensor.transpose(
                            bank[(6 + j) % 8][:, (t - t0) * D + half * HALF:(t - t0) * D + (half + 1) * HALF],
                            oT[:, half, t * P:(t + 1) * P], ident[0:HALF, 0:HALF])
                last.then_inc(a0_back, 1)

            def router(col, width, z):
                for t in range(TILES):
                    for i, (x, w) in enumerate(terms(wa3, wcols2(col, col + width), slice(t * P, (t + 1) * P))):
                        last = nc.tensor.matmul(bank[6][:, t * width:(t + 1) * width], x, w, start=(i == 0),
                                                stop=(i == 4))
                last.then_inc(z, 1)

            transposes(1)
            pe.wait_ge(ln_lo, 12)
            router(3 * D, E0, rt_z)
            pe.wait_ge(r_sel, 1)
            nc.tensor.matmul(bank[7][:, 0:TILES * E0], const[:, C_BEFORE:C_BEFORE + P], sel[:], start=True,
                             stop=False)
            ones = const[:, C_ONE:C_ONE + P]
            for t in range(TILES - 1):
                later = TILES - 1 - t
                nc.tensor.matmul(bank[7][:, (t + 1) * E0:TILES * E0].rearrange("p (t e) -> p t e", e=E0), ones,
                                 sel[:, t * E0:(t + 1) * E0].unsqueeze(1).to_broadcast([P, later, E0]), start=False,
                                 stop=(t == TILES - 2))
            for t in range(TILES):
                last = nc.tensor.matmul(bank[7][:, P:P + E0], ones, sel[:, t * E0:(t + 1) * E0], start=(t == 0),
                                        stop=(t == TILES - 1))
            last.then_inc(r_pos, 1)
            e_gate_up(pe, 0, 0, 0, 0)
            e_gate_up(pe, 1, 0, 0, 1)
            e_down(pe, 0, 0, 0, 0, True, 16)
            e_gate_up(pe, 2, 0, 0, 2)
            e_rows(pe, 1, 1, 32)
            e_down(pe, 1, 1, 0, 0, True, 16)

            def e_pe(n, par, shared, x_loaded, w2_loaded, last=False):
                e_gate_up(pe, n + 2, n, par, None)
                if not last:
                    e_rows(pe, n + 1, 1 - par, x_loaded)
                if shared:
                    e_down(pe, 2, 0, 0, 0, True, 16)
                else:
                    e_down(pe, n + 1, 1 - par, n - 1, 1 - par, False, w2_loaded)

            e_pe(1, 1, True, 32, None)
            e_pe(2, 0, False, 64, 16)
            e_pe(3, 1, False, 64, 32)
            e_pe(4, 0, False, 96, 32)
            with pe.Fori(0, (WORKS - 6) // 2, 1) as i:
                e_pe(i * 2 + 5, 1, False, i * 32 + 96, i * 16 + 48)
                e_pe(i * 2 + 6, 0, False, i * 32 + 128, i * 16 + 48)
            e_pe(WORKS - 1, 1, False, 16 * WORKS, 8 * WORKS)
            e_pe(WORKS, 0, False, None, 8 * WORKS, last=True)
            e_down(pe, WORKS + 2, 0, WORKS, 0, False, 8 * WORKS + 16)

            transposes(2)
            pe.wait_ge(ln_lo, 18)
            pe.wait_ge(split_lo, 4)
            l13 = (L1h, L1l, L12)
            for g in range(GROUPS):
                if g >= 4:
                    pe.wait_ge(l1_out[0], g - 3)
                    pe.wait_ge(l1_out[1], g - 3)
                for half in range(2):
                    for i, (x, w) in enumerate(terms(l13, wcols2(half * L1H, (half + 1) * L1H),
                                                     slice(g * GW, (g + 1) * GW))):
                        last = nc.tensor.matmul(bank[(2 * g + half) % 8][0:GW, 0:L1H], x, w, start=(i == 0),
                                                stop=(i == 4))
                last.then_inc(l1_proj, 1)
            pe.wait_ge(l1_out[0], GROUPS)
            pe.wait_ge(l1_out[1], GROUPS)
            for j in range(6):
                for g in range(2 * j, min(2 * j + 2, GROUPS)):
                    last = nc.tensor.matmul(bank[(6 + j) % 8][0:GW, (g % 2) * D:(g % 2 + 1) * D], tri,
                                            QK[:, g, 2 * D:3 * D], start=True, stop=True)
                last.then_inc(l1_us, 1)
            pe.wait_ge(l1_s, 1)
            for b, (g0, g1) in enumerate(BATCHES):
                for g in range(g0, g1):
                    last = nc.tensor.transpose(bank[4 + b][0:HEADS, (g - g0) * GW:(g - g0 + 1) * GW],
                                               ES[:, g, HEADS:2 * HEADS], ident[0:GW, 0:GW])
                last.then_inc(l1_st, 1)
            pe.wait_ge(l1_ex, 1)
            for g in range(GROUPS):
                last = nc.tensor.transpose(bank[7][0:GW, g * HEADS:(g + 1) * HEADS], sT[:, g * GW:(g + 1) * GW],
                                           ident[0:HEADS, 0:HEADS])
            last.then_inc(l1_et, 1)
            pe.wait_ge(l1_es, 1)
            for g in range(GROUPS):
                last = nc.tensor.matmul(bank[0][0:GW, g * 2 * HEADS:(g + 1) * 2 * HEADS], tri, ES[:, g, :],
                                        start=True, stop=True)
            last.then_inc(l1_cum, 1)
            for b, (g0, g1) in enumerate(BATCHES):
                pe.wait_ge(l1_qw, b + 1)
                pe.wait_ge(l1_kw, b + 1)
                for g in range(g0, g1):
                    if g:
                        pe.wait_ge(l1_Tca, 2 * g)
                        pe.wait_ge(l1_Tcd, g)
                    for i in range(12):
                        last = nc.tensor.transpose(
                            bank[i // 4][:, (i % 4) * GW:(i % 4 + 1) * GW],
                            (qw, kw)[i // 6][:, g - g0, 2 * (i % 6):2 * (i % 6) + 2, :].rearrange("p a b -> p (a b)"),
                            ident[0:GW, 0:GW])
                        if i % 4 == 3:
                            last.then_inc(l1_T, 1)
                    pe.wait_ge(l1_Tca, 2 * g + 2)
                    pe.wait_ge(l1_Tcd, g + 1)
                    for k in range(2):
                        if g:
                            pe.wait_ge(l1_Am, 4 * (g - 1) + 2 * k + 2)
                        for h in range(6 * k, 6 * k + 6):
                            o, i = SLOT * (h % 2), h % 6 // 2
                            last = nc.tensor.matmul(bank[3 + 2 * k + h % 2][0:GW, i * GW:(i + 1) * GW],
                                                    qkT[o:o + 3 * HD, 6 + h // 2, :], qkT[o:o + 3 * HD, h // 2, :],
                                                    start=True, stop=True)
                            if h % 6 >= 4:
                                last.then_inc(l1_A, 1)
                    if g:
                        pe.wait_ge(l1_Oc, g)
                    for h in range(HEADS):
                        if h % 6 == 0:
                            pe.wait_ge(l1_Am, 4 * g + h // 3 + 2)
                        last = nc.tensor.matmul(bank[7][0:GW, h * HD:(h + 1) * HD], AT[:, h, :],
                                                QK[:, g, 3 * D + h * HD:3 * D + (h + 1) * HD], start=True,
                                                stop=True)
                    last.then_inc(l1_O, 1)
            for g in range(GROUPS):
                if g == 0:
                    pe.wait_ge(l1_on, 1)
                if g >= 2:
                    pe.wait_ge(l1_oTc, g - 1)
                for half in range(2):
                    last = nc.tensor.transpose(bank[g % 2][0:HALF, half * GW:(half + 1) * GW],
                                               QK[:, g, 2 * D + half * HALF:2 * D + (half + 1) * HALF],
                                               ident[0:GW, 0:GW])
                last.then_inc(l1_oT, 1)
            pe.wait_ge(l1_oTc, GROUPS)
            pe.wait_ge(ld_wo, 16)
            for j, (t0, t1) in enumerate(PBLK):
                for t in range(t0, t1):
                    for half in range(2):
                        last = nc.tensor.matmul(bank[2 + j][:, (t - t0) * D:(t - t0 + 1) * D],
                                                OT[:, half, t * P:(t + 1) * P], wo_sb[:, half, :],
                                                start=(half == 0), stop=(half == 1))
                last.then_inc(l1_f, 1)

            transposes(3)
            pe.wait_ge(ln_lo, 24)
            router(3 * D + E0, E1P, rt1_z)
            M, S = MOE1, moe_sems[1]
            for n in range(M.works):
                moe_pe(pe, M, W1, A1, S, n, n % 2, n == 0)
            tail_down(pe, nc, M, W1, A1, S, bank)

        @block.scalar
        def _(act):
            def norm_act(k):
                act.wait_ge(ln_var, k + 1)
                nc.scalar.activation(sd[:], ve[:], ACT.Sqrt).then_inc(ln_sd, 1)
                for c in range(CH):
                    act.wait_ge(ln_xt, 3 * k + c + 1)
                    cols = slice(c * CHW, (c + 1) * CHW)
                    nc.scalar.activation(X01h[:, cols], bank[2 * c][:, 0:CHW], ACT.Copy).then_inc(ln_hi, 1)
                    nc.scalar.activation(X2h[:, cols], bank[2 * c + 1][:, 0:CHW], ACT.Copy).then_inc(ln_hi, 1)

            for s, (wh, w2, n) in enumerate(((WAh, WA2, NWA), (L1h, L12, QKVG))):
                act.wait_ge(ld_stage[s], 16)
                nc.scalar.activation(wh[:], W0[s]["stage"][:, 0:n], ACT.Copy).then_inc(split_hi, 1)
                nc.scalar.activation(w2[:], W0[s]["stage"][:, n:2 * n], ACT.Copy).then_inc(split_hi, 1)
            norm_act(0)
            act.wait_ge(zeroed, 16 * (SLOTS // P * D // ZW))
            for j in range(0, 18, 2):
                act.wait_ge(proj_done, j + 1)
                if j < 12:
                    half, c = (j // 3) % 2, j % 3
                    dst = (qT if j < 6 else kT)[:, half, c * (XW // 3):(c + 1) * (XW // 3)]
                    src = bank[j % 8][0:HALF, 0:XW // 3]
                else:
                    g = 2 * (j - 12)
                    n = min(2, GROUPS - g)
                    dst = V[:, g:g + n, :]
                    src = bank[j % 8][0:GW, 0:n * D].rearrange("p (g d) -> p g d", d=D)
                nc.scalar.activation(dst, src, ACT.Copy).then_inc(proj_out[0], 1)
            for b, (g0, g1) in enumerate(BATCHES):
                act.wait_ge(a0_shift, b + 1)
                nc.scalar.activation(Pm[:, g0:g1, :], Pm[:, g0:g1, :], ACT.Exp,
                                     scale=float(D) ** -0.5).then_inc(a0_exp, 1)
            for b, (g0, g1) in enumerate(BATCHES):
                act.wait_ge(a0_pt, b + 1)
                nc.scalar.activation(PT[:, g0:g1, :], bank[5 + b][0:GW, 0:(g1 - g0) * GW].rearrange(
                    "p (g q) -> p g q", q=GW), ACT.Copy).then_inc(a0_ptc, 1)
            for b, (g0, g1) in enumerate(BATCHES):
                act.wait_ge(a0_o, 2 * b + 1)
                nc.scalar.activation(oT[:, 0, g0 * GW:g1 * GW], bank[2 * b][0:HALF, 0:(g1 - g0) * GW],
                                     ACT.Copy).then_inc(a0_oc[0], 1)
            for i in range(4):
                e_split_act(act, 0, 0, i, 32, None)
            S1 = moe_sems[1]
            norm_act(1)
            act.wait_ge(rt_neg, 1)
            nc.scalar.activation(rt[1][:], rt[1][:], ACT.Exp).then_inc(rt_e, 1)
            act.wait_ge(rt_u, 1)
            nc.scalar.activation(rt[3][:], rt[2][:], ACT.Ln).then_inc(rt_ln, 1)
            act.wait_ge(rt_sp, 1)
            nc.scalar.activation(rt[4][:], rt[3][:], ACT.Sqrt).then_inc(rt_sc, 1)
            e_act(act, 0, CHW, None, None, None)
            e_act(act, 1, CHW, (1, 1, 32, None), None, None)
            e_act(act, 2, CHW, None, (1, 1, None), None)
            e_act(act, 3, WT, (2, 0, 48, 3), (2, 0, None), None)
            e_act(act, 4, WT, (3, 1, 48, 4), (3, 1, 24), None)
            e_act(act, 5, WT, (4, 0, 64, 5), (4, 0, 30), (1, 1))
            e_act(act, 6, WT, (5, 1, 64, 6), (5, 1, 36), (2, 0))
            with act.Fori(0, (WORKS - 6) // 2, 1) as i:
                e_act(act, i * 2 + 7, WT, (i * 2 + 6, 0, i * 16 + 80, i * 2 + 7), (i * 2 + 6, 0, i * 12 + 42),
                      (i * 2 + 3, 1))
                e_act(act, i * 2 + 8, WT, (i * 2 + 7, 1, i * 16 + 80, i * 2 + 8), (i * 2 + 7, 1, i * 12 + 48),
                      (i * 2 + 4, 0))
            e_act(act, WORKS + 1, WT, (WORKS, 0, 8 * WORKS + 32, WORKS + 1), (WORKS, 0, FC0 * (WORKS + 1)),
                  (WORKS - 3, 1))
            e_act(act, WORKS + 2, WT, None, None, (WORKS - 2, 0))
            e_store(act, WORKS - 1, 1)
            e_store(act, WORKS, 0)
            norm_act(2)

            act.wait_ge(ld_row, 16)
            act.wait_ge(l1_tau, 1)
            nc.scalar.activation(tau[:], tau[:], ACT.Exp).then_inc(l1_tau, 1)
            for g in range(GROUPS):
                act.wait_ge(l1_proj, g + 1)
                nc.scalar.activation(QK[:, g, 0:L1H], bank[(2 * g) % 8][0:GW, 0:L1H], ACT.Copy).then_inc(l1_out[0], 1)
            for n in range(2):
                for i in range(MOE1.pieces):
                    moe_weights_act(act, MOE1, W1, S1, ld_stage1, n, n, i, None, 16)
            act.wait_ge(l1_sh, 3)
            nc.scalar.activation(sT[:], sT[:], ACT.Exp).then_inc(l1_ex, 1)
            act.wait_ge(l1_out[1], GROUPS)
            nc.scalar.activation(SG[:], QK[:, :, 4 * D:QKVG], ACT.Sigmoid).then_inc(l1_sig, 1)
            for b, (g0, g1) in enumerate(BATCHES):
                n = g1 - g0
                act.wait_ge(l1_rope, b + 1)
                nc.scalar.activation(rotA[:, 0:n, :], QK[:, g0:g1, 0:2 * D], ACT.Square).then_inc(l1_sq, 1)
                act.wait_ge(l1_n2, b + 1)
                nc.scalar.activation(nrm[:, 0:n, :], nrm[:, 0:n, :], ACT.Sqrt).then_inc(l1_nr, 1)
                for g in range(g0, g1):
                    for i in range(2):
                        act.wait_ge(l1_T, 3 * g + i + 1)
                        if g:
                            act.wait_ge(l1_A, 4 * g)
                        nc.scalar.activation(qkT[:, 4 * i:4 * i + 4, :], bank[i][:, 0:4 * GW].rearrange(
                            "p (h q) -> p h q", q=GW), ACT.Copy).then_inc(l1_Tca, 1)
                    act.wait_ge(l1_O, g + 1)
                    nc.scalar.activation(QK[:, g, 2 * D:3 * D], bank[7][0:GW, 0:D], ACT.Copy).then_inc(l1_Oc, 1)
            act.wait_ge(l1_cen, 1)
            nc.scalar.activation(W1b, QK[:, :, 2 * D:3 * D], ACT.Square).then_inc(l1_csq, 1)
            act.wait_ge(l1_var, 1)
            nc.scalar.activation(CO[:, 1], CO[:, 0], ACT.Sqrt).then_inc(l1_std, 1)
            for g in range(GROUPS):
                act.wait_ge(l1_oT, g + 1)
                w = min(GW, TOK - g * GW)
                src = bank[g % 2][0:HALF, 0:2 * GW].rearrange("p (h q) -> p h q", h=2)[:, :, 0:w]
                nc.scalar.activation(OT[:, :, g * GW:g * GW + w], src, ACT.Copy).then_inc(l1_oTc, 1)
            norm_act(3)
            act.wait_ge(rt1_b, 1)
            nc.scalar.activation(rt[4][:, 0:TILES * E1], rt[0][:, 0:TILES * E1], ACT.Sigmoid).then_inc(rt1_p, 1)
            for n in range(MOE1.works):
                moe_act(act, MOE1, W1, A1, S1, ld_stage1, n, n % 2, n == 0, n in (0, E1), 32)
            moe_high(act, MOE1, A1, S1, E1, E1 % 2, 3 * MOE1.fc - 1)

        @block.gpsimd
        def _(pool):
            nc.gpsimd.memset(zero[:], 0.0).then_inc(zero_set, 1)
            for x in (X01h, X01l, X2h, X2l):
                nc.gpsimd.memset(x[:, TOK:XW].bitcast(F32), 0.0).then_inc(pads, 1)
            for s, (st, wh, wl, w2, n) in enumerate(((0, WAh, WAl, WA2, NWA), (1, L1h, L1l, L12, QKVG))):
                stage = W0[st]["stage"]
                pool.wait_ge(split_hi, 2 * s + 1)
                pool.wait_ge(*((split_lo, 2 * s) if s else (pads, 4)))
                nc.gpsimd.tensor_tensor(wl[:], stage[:, 0:n], wh[:].bitcast(F32), ALU.subtract).then_inc(split_lo, 1)
                pool.wait_ge(split_hi, 2 * s + 2)
                pool.wait_ge(split_lo, 2 * s + 1)
                nc.gpsimd.tensor_tensor(w2[64:P, :], stage[64:P, n:2 * n], w2[64:P, :].bitcast(F32),
                                        ALU.subtract).then_inc(split_lo, 1)
            S0, S1 = moe_sems
            pool.wait_ge(split_lo, 4)
            e_split_pool(pool, 0, 0)
            pool.wait_ge(zeroed, 16 * (SLOTS // P * D // ZW))
            pool.wait_ge(r_idx, 1)
            pool.wait_ge(S0["w_lo"], 4)
            for t in range(TILES):
                for j in range(PICKS):
                    nc.gpsimd.indirect_dma_start(
                        out=xs, out_offset=bass.IndirectOffsetOnAxis(ap=idx[:, j, t:t + 1], axis=0),
                        in_=Y[:, t, 0:D], in_offset=None).then_inc(scattered, 16)
            pool.wait_ge(scattered, 16 * PICKS * TILES)
            e_split_pool(pool, 1, 1)
            e_split_pool(pool, 2, 0)
            with pool.Fori(0, (WORKS - 4) // 2, 1) as i:
                e_split_pool(pool, i * 2 + 3, 1)
                e_split_pool(pool, i * 2 + 4, 0)
            e_split_pool(pool, WORKS - 1, 1)
            e_split_pool(pool, WORKS, 0)
            for par in range(2):
                pool.wait_ge(st_y[par], 8 * WORKS)
            for t in range(TILES):
                for j in range(PICKS):
                    nc.gpsimd.indirect_dma_start(
                        out=G[:, t, j, :], out_offset=None, in_=ys.rearrange("w s d -> (w s) d"),
                        in_offset=bass.IndirectOffsetOnAxis(ap=idx[:, j, t:t + 1], axis=0)).then_inc(ld_g[t // 3], 16)
            for c in range(CH):
                pool.wait_ge(ld_g[c], 16 * PICKS * 3)
            pool.wait_ge(l1_out[1], GROUPS)
            nc.gpsimd.memset(qw[:], 0.0).then_inc(pad_w, 1)
            nc.gpsimd.memset(kw[:], 0.0).then_inc(pad_w, 1)
            pool.wait_ge(pad_w, 2)
            for n in range(2):
                moe_weights_pool(pool, MOE1, W1, S1, n, n)
            for b, (g0, g1) in enumerate(BATCHES):
                n = g1 - g0
                pool.wait_ge(l1_cq, b + 1)
                if b:
                    pool.wait_ge(l1_T, 3 * g0)
                else:
                    pool.wait_ge(pad_w, 2)
                for j in range(3):
                    f = CK[:, j, 0:n, :] if j < 2 else rn[:, 0:n, HEADS:2 * HEADS]
                    last = nc.gpsimd.tensor_tensor(
                        kw[:, 0:n, :, j * HD:(j + 1) * HD],
                        QK[:, g0:g1, D:2 * D].rearrange("p g (h d) -> p g h d", d=HD),
                        f.unsqueeze(3).to_broadcast([GW, n, HEADS, HD]), ALU.mult)
                    last.then_inc(l1_kw if j == 2 else pool_step, 1)
            for n in range(2, MOE1.works):
                moe_weights_pool(pool, MOE1, W1, S1, n, n % 2)

        @block.vector
        def _(dve):
            own = Steps(dve, dve_step)

            def norm(k, ready):
                for t in range(TILES):
                    ready(t)
                    own.step(nc.vector.bn_stats(stat[:, t, :], H[:, t, :]))
                own.settle()
                for t in range(TILES):
                    own.step(nc.vector.bn_aggr(mv[:, t, :], stat[:, t, :]))
                own.settle()
                nc.vector.tensor_scalar(ve[:], mv[:, :, 1], EPS, None, ALU.add).then_inc(ln_var, 1)
                dve.wait_ge(ln_sd, k + 1)
                own.link(nc.vector.reciprocal(rstd[:], sd[:]))
                for c in range(CH):
                    for t in range(3 * c, 3 * c + 3):
                        own.step(nc.vector.tensor_scalar(Y[:, t, 0:D], H[:, t, :], mv[:, t, 0:1], rstd[:, t:t + 1],
                                                         ALU.subtract, ALU.mult))
                    own.settle()
                    nc.vector.tensor_copy(Y[:, 3 * c:3 * c + 3, D:256], Y[:, 3 * c:3 * c + 3, P:D]).then_inc(ln_y, 1)
                for c in range(CH):
                    cols = slice(c * CHW, (c + 1) * CHW)
                    dve.wait_ge(ln_hi, 6 * k + 2 * c + 1)
                    nc.vector.tensor_tensor(X01l[:, cols], bank[2 * c][:, 0:CHW], X01h[:, cols].bitcast(F32),
                                            ALU.subtract).then_inc(ln_lo, 1)
                    dve.wait_ge(ln_hi, 6 * k + 2 * c + 2)
                    nc.vector.tensor_tensor(X2l[:, cols], bank[2 * c + 1][:, 0:CHW],
                                            X2h[:, cols].bitcast(F32), ALU.subtract).then_inc(ln_lo, 1)

            def rank(sc, keys, E, comb_out, clip, chosen=None):
                shape = [P, TILES, E, E]
                r = keys.rearrange("p (t e) -> p t e", e=E)
                other, mine = r.unsqueeze(2).to_broadcast(shape), r.unsqueeze(3).to_broadcast(shape)
                k0 = rk[0][:, 0:TILES * E * E].rearrange("p (t e j) -> p t e j", e=E, j=E)
                k1 = rk[1][:, 0:TILES * E * E].rearrange("p (t e j) -> p t e j", e=E, j=E)
                low = const[:, C_LOW:C_LOW + E0 * E0].rearrange("p (e j) -> p e j", j=E0)[:, 0:E, 0:E]
                own.step(nc.vector.tensor_tensor(k0, other, mine, ALU.is_gt))
                own.link(nc.vector.tensor_tensor(k1, other, mine, ALU.is_equal))
                own.link(nc.vector.tensor_tensor(k1, k1, low.unsqueeze(1).to_broadcast(shape), ALU.mult))
                own.link(nc.vector.tensor_tensor(k0, k0, k1, ALU.add))
                rnk = rt[5][:, 0:TILES * E]
                own.link(nc.vector.tensor_reduce(rnk.rearrange("p (t e) -> p t e", e=E), k0, AX.X, ALU.add))
                if chosen is not None:
                    nc.vector.tensor_scalar(chosen, rnk, 1.5, None, ALU.is_lt).then_inc(r_sel, 1)
                own.link(nc.vector.scalar_tensor_tensor(out=rnk, in0=rnk, scalar=1.5, in1=sc, op0=ALU.is_lt,
                                                        op1=ALU.mult))
                own.link(nc.vector.tensor_reduce(rsum[0][:], rnk.rearrange("p (t e) -> p t e", e=E), AX.X, ALU.add))
                if clip:
                    own.link(nc.vector.tensor_scalar(rsum[0][:], rsum[0][:], 1e-6, None, ALU.max))
                own.link(nc.vector.reciprocal(rsum[1][:], rsum[0][:]))
                own.link(nc.vector.tensor_tensor(comb_out, rnk.rearrange("p (t e) -> p t e", e=E),
                                                 rsum[1][:].unsqueeze(2).to_broadcast([P, TILES, E]), ALU.mult))

            def tiles2(t0, t1):
                return H[:, t0:t1, :]

            def pair(b, t0, t1):
                return bank[b][:, 0:(t1 - t0) * D].rearrange("p (t d) -> p t d", d=D)

            dve.wait_ge(ld_row, 16)
            bias = row[:, R_TOKB:R_TOKB + D].unsqueeze(1)
            for j, (t0, t1) in enumerate(PBLK):
                dve.wait_ge(tok_done, j + 1)
                nc.vector.tensor_tensor(tiles2(t0, t1), pair(j, t0, t1), bias.to_broadcast([P, t1 - t0, D]),
                                        ALU.add).then_inc(tok_h, 1)
            norm(0, lambda t: dve.wait_ge(tok_h, t // 2 + 1))

            dve.wait_ge(ld_const, 16)
            dve.wait_ge(zeroed, 16 * (SLOTS // P * D // ZW))
            for j in range(1, 18, 2):
                dve.wait_ge(proj_done, j + 1)
                if j < 12:
                    half, c = (j // 3) % 2, j % 3
                    dst = (qT if j < 6 else kT)[:, half, c * (XW // 3):(c + 1) * (XW // 3)]
                    src = bank[j % 8][0:HALF, 0:XW // 3]
                else:
                    g = 2 * (j - 12)
                    n = min(2, GROUPS - g)
                    dst = V[:, g:g + n, :]
                    src = bank[j % 8][0:GW, 0:n * D].rearrange("p (g d) -> p g d", d=D)
                nc.vector.tensor_copy(dst, src).then_inc(proj_out[1], 1)
            for b, (g0, g1) in enumerate(BATCHES):
                n = g1 - g0
                dve.wait_ge(a0_s, b + 1)
                pm = Pm[:, g0:g1, :]
                own.link(nc.vector.tensor_tensor(
                    pm, bank[2 + b][0:GW, 0:n * GW].rearrange("p (g q) -> p g q", q=GW),
                    amask.unsqueeze(1).to_broadcast([GW, n, GW]), ALU.add))
                own.link(nc.vector.tensor_reduce(mx[:, g0:g1], pm, AX.X, ALU.max))
                nc.vector.tensor_tensor(pm, pm, mx[:, g0:g1].unsqueeze(2).to_broadcast([GW, n, GW]),
                                        ALU.subtract).then_inc(a0_shift, 1)
            for b, (g0, g1) in enumerate(BATCHES):
                n = g1 - g0
                dve.wait_ge(a0_exp, b + 1)
                pm = Pm[:, g0:g1, :]
                own.link(nc.vector.tensor_reduce(rs[:, g0:g1], pm, AX.X, ALU.add))
                own.link(nc.vector.reciprocal(rr[:, g0:g1], rs[:, g0:g1]))
                nc.vector.tensor_tensor(pm, pm, rr[:, g0:g1].unsqueeze(2).to_broadcast([GW, n, GW]),
                                        ALU.mult).then_inc(a0_p, 1)
            for b, (g0, g1) in enumerate(BATCHES):
                dve.wait_ge(a0_o, 2 * b + 2)
                nc.vector.tensor_copy(oT[:, 1, g0 * GW:g1 * GW],
                                      bank[2 * b + 1][0:HALF, 0:(g1 - g0) * GW]).then_inc(a0_oc[1], 1)
            for j, (t0, t1) in enumerate(PBLK):
                dve.wait_ge(a0_back, j + 1)
                nc.vector.tensor_tensor(tiles2(t0, t1), pair((6 + j) % 8, t0, t1), tiles2(t0, t1),
                                        ALU.add).then_inc(a0_h, 1)
            norm(1, lambda t: dve.wait_ge(a0_h, t // 2 + 1))

            z, e, u, l, sc = (rt[i][:] for i in range(5))
            dve.wait_ge(rt_z, 1)
            own.link(nc.vector.tensor_copy(z, bank[6][:, 0:TILES * E0]))
            nc.vector.scalar_tensor_tensor(out=e, in0=z, scalar=-1.0, in1=z, op0=ALU.mult,
                                           op1=ALU.min).then_inc(rt_neg, 1)
            dve.wait_ge(rt_e, 1)
            nc.vector.tensor_scalar(u, e, 1.0, None, ALU.add).then_inc(rt_u, 1)
            dve.wait_ge(rt_u, 1)
            own.step(nc.vector.scalar_tensor_tensor(out=e, in0=u, scalar=1.0, in1=e, op0=ALU.subtract,
                                                    op1=ALU.subtract))
            own.link(nc.vector.reciprocal(sc, u))
            own.link(nc.vector.tensor_tensor(e, e, sc, ALU.mult))
            dve.wait_ge(rt_ln, 1)
            own.link(nc.vector.tensor_tensor(l, l, e, ALU.subtract))
            nc.vector.scalar_tensor_tensor(out=l, in0=z, scalar=0.0, in1=l, op0=ALU.max,
                                           op1=ALU.add).then_inc(rt_sp, 1)
            dve.wait_ge(rt_sc, 1)
            own.link(nc.vector.tensor_tensor(
                u.rearrange("p (t e) -> p t e", e=E0), sc.rearrange("p (t e) -> p t e", e=E0),
                row[:, R_GB:R_GB + E0].unsqueeze(1).to_broadcast([P, TILES, E0]), ALU.add))
            rank(sc, u, E0, comb[:], True, sel[:])

            te = lambda x: x.rearrange("p (t e) -> p t e", e=E0)
            ee = [P, E0, E0]
            low = const[:, C_LOW:C_LOW + E0 * E0].rearrange("p (e j) -> p e j", j=E0)
            dve.wait_ge(r_pos, 1)
            own.link(nc.vector.tensor_copy(count[:], bank[7][:, P:P + E0]))
            k0 = rk[0][:, 0:E0 * FULL].rearrange("p (e k) -> p e k", k=FULL)
            own.link(nc.vector.tensor_tensor(
                k0, count[:].unsqueeze(2).to_broadcast([P, E0, FULL]),
                const[:, C_FULL:C_FULL + FULL].unsqueeze(1).to_broadcast([P, E0, FULL]), ALU.is_gt))
            own.link(nc.vector.tensor_reduce(works[:], k0, AX.X, ALU.add))
            k1 = rk[1][:, 0:E0 * E0].rearrange("p (e j) -> p e j", j=E0)
            own.link(nc.vector.tensor_tensor(k1, low, works[:].unsqueeze(1).to_broadcast(ee), ALU.mult))
            own.link(nc.vector.tensor_reduce(base[:], k1, AX.X, ALU.add))
            own.link(nc.vector.tensor_scalar(count[:], base[:], float(WT), 1.0, ALU.mult, ALU.add))
            own.link(nc.vector.tensor_tensor(te(slot[:]), te(bank[7][:, 0:TILES * E0]),
                                             count[:].unsqueeze(1).to_broadcast([P, TILES, E0]), ALU.add))
            own.link(nc.vector.tensor_tensor(slot[:], slot[:], sel[:], ALU.mult))
            own.step(nc.vector.tensor_reduce(smx[:], te(slot[:]), AX.X, ALU.max))
            own.link(nc.vector.tensor_reduce(smn[:], te(slot[:]), AX.X, ALU.add))
            own.link(nc.vector.tensor_tensor(smn[:], smn[:], smx[:], ALU.subtract))
            own.step(nc.vector.tensor_scalar(idx[:, 0, :], smx[:], -1.0, None, ALU.add))
            own.settle()
            nc.vector.tensor_scalar(idx[:, 1, :], smn[:], -1.0, None, ALU.add).then_inc(r_idx, 1)
            own.link(nc.vector.tensor_tensor(works[:], works[:], base[:], ALU.add))
            k0 = rk[0][:, 0:WORKS * E0].rearrange("p (k e) -> p k e", e=E0)
            own.link(nc.vector.tensor_tensor(
                k0, const[:, C_WORK:C_WORK + WORKS].unsqueeze(2).to_broadcast([P, WORKS, E0]),
                works[:].unsqueeze(1).to_broadcast([P, WORKS, E0]), ALU.is_ge))
            own.link(nc.vector.tensor_reduce(eidf[:], k0, AX.X, ALU.add))
            nc.vector.tensor_scalar(eid[:], eidf[:], 1.0, float(E0), ALU.add, ALU.min).then_inc(r_eid, 1)
            own.link(nc.vector.tensor_tensor(te(rt[0][:]), te(slot[:]), smx[:].unsqueeze(2).to_broadcast(
                [P, TILES, E0]), ALU.is_equal))
            own.link(nc.vector.tensor_tensor(te(rt[0][:]), te(rt[0][:]), comb[:], ALU.mult))
            own.step(nc.vector.tensor_reduce(wpick[:, 0, :], te(rt[0][:]), AX.X, ALU.add))
            own.link(nc.vector.tensor_tensor(te(rt[1][:]), comb[:], te(rt[0][:]), ALU.subtract))
            own.link(nc.vector.tensor_reduce(wpick[:, 1, :], te(rt[1][:]), AX.X, ALU.add))

            S1 = moe_sems[1]
            e_dve(dve, 0, 0, CHW, None, None, None)
            e_dve(dve, 1, 1, CHW, None, None, lambda: e_acc(dve, 0))
            e_dve(dve, 2, 0, CHW, 3, (1, 1), lambda: e_acc(dve, 1))
            e_dve(dve, 3, 1, WT, 6, (2, 0), lambda: e_acc(dve, 2))
            e_dve(dve, 4, 0, WT, 9, (3, 1), lambda: e_copy(dve, 1, 1, None))
            e_dve(dve, 5, 1, WT, 11, (4, 0), lambda: e_copy(dve, 2, 0, None))
            e_dve(dve, 6, 0, WT, 13, (5, 1), lambda: e_copy(dve, 3, 1, 16))
            with dve.Fori(0, (WORKS - 6) // 2, 1) as i:
                e_dve(dve, i * 2 + 7, 1, WT, i * 4 + 15, (i * 2 + 6, 0), lambda: e_copy(dve, i * 2 + 4, 0, i * 16 + 16))
                e_dve(dve, i * 2 + 8, 0, WT, i * 4 + 17, (i * 2 + 7, 1), lambda: e_copy(dve, i * 2 + 5, 1, i * 16 + 32))
            e_dve(dve, WORKS + 1, 1, WT, 2 * WORKS + 3, (WORKS, 0), lambda: e_copy(dve, WORKS - 2, 0, 8 * WORKS - 32))
            e_dve(dve, WORKS + 2, 0, WT, 2 * WORKS + 5, None, lambda: e_copy(dve, WORKS - 1, 1, 8 * WORKS - 16))
            e_copy(dve, WORKS, 0, 8 * WORKS - 16)
            for t in range(TILES):
                dve.wait_ge(ld_g[t // 3], 16 * PICKS * 3)
                own.link(nc.vector.scalar_tensor_tensor(out=H[:, t, :], in0=G[:, t, 0, :], scalar=wpick[:, 0, t:t + 1],
                                                        in1=H[:, t, :], op0=ALU.mult, op1=ALU.add))
                nc.vector.scalar_tensor_tensor(out=H[:, t, :], in0=G[:, t, 1, :], scalar=wpick[:, 1, t:t + 1],
                                               in1=H[:, t, :], op0=ALU.mult, op1=ALU.add).then_inc(mixed, 1)
            norm(2, lambda t: dve.wait_ge(mixed, t + 1))

            gw = lambda ap: ap.rearrange("p g (h d) -> p g h d", d=HD)
            t_, rt_, nrt_ = (const[0:GW, c:c + 1] for c in (C_T, C_RT, C_NRT))
            nc.vector.tensor_scalar(tau[:], row[0:GW, R_TAU:R_TAU + HEADS], -50.0, 30.0, ALU.max,
                                    ALU.min).then_inc(l1_tau, 1)
            for g in range(GROUPS):
                dve.wait_ge(l1_proj, g + 1)
                nc.vector.tensor_copy(QK[:, g, L1H:QKVG], bank[(2 * g + 1) % 8][0:GW, 0:L1H]).then_inc(l1_out[1], 1)
            dve.wait_ge(l1_tau, 2)
            own.step(nc.vector.tensor_tensor(tmu[:].rearrange("p (h d) -> p h d", d=HD),
                                             row[0:GW, R_MU:R_MU + D].rearrange("p (h d) -> p h d", d=HD),
                                             tau[:].unsqueeze(2).to_broadcast([GW, HEADS, HD]), ALU.mult))
            own.link(nc.vector.tensor_scalar(tden[:], tau[:], t_, None, ALU.add))
            own.link(nc.vector.reciprocal(tau[:], tden[:]))
            own.link(nc.vector.tensor_scalar(tden[:], tau[:], -1.0 / float(HD) ** 0.5, None, ALU.mult))
            for j in range(6):
                g0, g1 = 2 * j, min(2 * j + 2, GROUPS)
                dve.wait_ge(l1_us, j + 1)
                own.step(nc.vector.tensor_tensor(
                    W1b[:, g0:g1, :], bank[(6 + j) % 8][0:GW, 0:(g1 - g0) * D].rearrange("p (g d) -> p g d", d=D),
                    tmu[:].unsqueeze(1).to_broadcast([GW, g1 - g0, D]), ALU.add))
            own.settle()
            own.link(nc.vector.tensor_tensor(W1b, W1b, QK[:, :, 2 * D:3 * D], ALU.mult))
            own.link(nc.vector.tensor_reduce(CO[:, 0], gw(W1b), AX.X, ALU.add))
            nc.vector.tensor_tensor(ES[:, :, HEADS:2 * HEADS], CO[:, 0],
                                    tden[:].unsqueeze(1).to_broadcast([GW, GROUPS, HEADS]), ALU.mult).then_inc(l1_s, 1)
            for b, (g0, g1) in enumerate(BATCHES):
                n = (g1 - g0) * GI
                dve.wait_ge(l1_st, b + 1)
                src = bank[4 + b][0:HEADS, 0:n * SEQ].rearrange("p (i s) -> p i s", s=SEQ)
                m = smax[:, g0 * GI:g1 * GI]
                own.link(nc.vector.tensor_reduce(m, src, AX.X, ALU.max))
                nc.vector.tensor_tensor(sT[:, g0 * GW:g1 * GW].rearrange("p (i s) -> p i s", s=SEQ), src,
                                        m.unsqueeze(2).to_broadcast([HEADS, n, SEQ]), ALU.subtract).then_inc(l1_sh, 1)
            dve.wait_ge(l1_et, 1)
            nc.vector.tensor_copy(ES[:, :, 0:HEADS], bank[7][0:GW, 0:GROUPS * HEADS].rearrange(
                "p (g h) -> p g h", h=HEADS)).then_inc(l1_es, 1)
            dve.wait_ge(l1_cum, 1)
            dve.wait_ge(l1_sig, 1)
            cum = bank[0][0:GW, 0:GROUPS * 2 * HEADS].rearrange("p (g h) -> p g h", h=2 * HEADS)
            al, be, ga = CO[:, 0], CO[:, 1], CO[:, 2]
            s1, sh = SG[:, :, 0:HEADS], SG[:, :, HEADS:2 * HEADS]
            dve.wait_ge(l1_s, 1)
            own.link(nc.vector.tensor_scalar(ga, cum[:, :, 0:HEADS], 1e-12, None, ALU.add))
            own.link(nc.vector.reciprocal(al, ga))
            own.step(nc.vector.tensor_tensor(al, al, sh, ALU.mult))
            own.link(nc.vector.tensor_tensor(be, s1, sh, ALU.subtract))
            own.link(nc.vector.tensor_scalar(be, be, rt_, None, ALU.mult))
            own.link(nc.vector.tensor_tensor(ga, cum[:, :, HEADS:2 * HEADS], be, ALU.mult))
            own.link(nc.vector.tensor_tensor(ga, ga, sh, ALU.add))
            own.link(nc.vector.tensor_scalar(ga, ga, nrt_, None, ALU.mult))
            dve.wait_ge(l1_es, 1)
            for b, (g0, g1) in enumerate(BATCHES):
                n = g1 - g0
                src = QK[:, g0:g1, 0:2 * D].rearrange("p g (h d) -> p g h d", d=HD)
                A4 = rotA[:, 0:n, :].rearrange("p g (h d) -> p g h d", d=HD)
                B4 = rotB[:, 0:n, :].rearrange("p g (h d) -> p g h d", d=HD)
                hh = HD // 2

                def table(c, m):
                    return const[0:GW, c:c + m].unsqueeze(1).unsqueeze(1).to_broadcast([GW, n, 2 * HEADS, m])

                own.step(nc.vector.tensor_tensor(A4, src, table(C_COS, HD), ALU.mult))
                own.step(nc.vector.tensor_tensor(B4[:, :, :, 0:hh], src[:, :, :, hh:HD], table(C_SIN, hh), ALU.mult))
                own.link(nc.vector.tensor_tensor(B4[:, :, :, hh:HD], src[:, :, :, 0:hh], table(C_SIN + hh, hh),
                                                 ALU.mult))
                nc.vector.tensor_tensor(QK[:, g0:g1, 0:2 * D], rotA[:, 0:n, :], rotB[:, 0:n, :],
                                        ALU.add).then_inc(l1_rope, 1)
                dve.wait_ge(l1_sq, b + 1)
                nc.vector.tensor_reduce(nrm[:, 0:n, :], A4, AX.X, ALU.add).then_inc(l1_n2, 1)
                dve.wait_ge(l1_nr, b + 1)
                own.link(nc.vector.tensor_scalar(nrm[:, 0:n, :], nrm[:, 0:n, :], 1e-12, None, ALU.max))
                if b:
                    dve.wait_ge(l1_kw, b)
                own.link(nc.vector.reciprocal(rn[:, 0:n, :], nrm[:, 0:n, :]))
                own.step(nc.vector.tensor_tensor(CK[:, 0, 0:n, :], ES[:, g0:g1, 0:HEADS],
                                                 rn[:, 0:n, HEADS:2 * HEADS], ALU.mult))
                nc.vector.tensor_tensor(CK[:, 1, 0:n, :], ES[:, g0:g1, HEADS:2 * HEADS],
                                        rn[:, 0:n, HEADS:2 * HEADS], ALU.mult).then_inc(l1_cq, 1)
                for j in range(3):
                    own.step(nc.vector.tensor_tensor(CQ[:, j, 0:n, :], CO[:, j, g0:g1, :], rn[:, 0:n, 0:HEADS],
                                                     ALU.mult))
                own.settle()
                if b:
                    dve.wait_ge(l1_T, 3 * g0)
                else:
                    dve.wait_ge(pad_w, 2)
                for j in range(3):
                    nc.vector.tensor_tensor(
                        qw[:, 0:n, :, j * HD:(j + 1) * HD], gw(QK[:, g0:g1, 0:D]),
                        CQ[:, j, 0:n, :].unsqueeze(3).to_broadcast([GW, n, HEADS, HD]),
                        ALU.mult).then_inc(l1_qw if j == 2 else dve_step, 1)
                    own.n += j < 2
                for g in range(g0, g1):
                    dve.wait_ge(l1_T, 3 * g + 3)
                    if g:
                        dve.wait_ge(l1_A, 4 * g)
                    nc.vector.tensor_copy(qkT[:, 8:12, :], bank[2][:, 0:4 * GW].rearrange(
                        "p (h q) -> p h q", q=GW)).then_inc(l1_Tcd, 1)
                    for k in range(4):
                        dve.wait_ge(l1_A, 4 * g + k + 1)
                        if g:
                            dve.wait_ge(l1_O, g)
                        h0 = 6 * (k // 2) + k % 2
                        nc.vector.tensor_tensor(
                            AT[:, h0:h0 + 5:2, :], bank[3 + k][0:GW, 0:3 * GW].rearrange("p (h q) -> p h q", q=GW),
                            tri.unsqueeze(1).to_broadcast([GW, 3, GW]), ALU.mult).then_inc(l1_Am, 1)
            O = gw(QK[:, :, 2 * D:3 * D])
            dve.wait_ge(l1_Oc, GROUPS)
            bc = [GW, GROUPS, HEADS, HD]
            own.link(nc.vector.tensor_reduce(CO[:, 0], O, AX.X, ALU.add))
            own.link(nc.vector.tensor_scalar(CO[:, 1], CO[:, 0], 1.0 / HD, None, ALU.mult))
            nc.vector.tensor_tensor(O, O, CO[:, 1].unsqueeze(3).to_broadcast(bc), ALU.subtract).then_inc(l1_cen, 1)
            dve.wait_ge(l1_csq, 1)
            own.link(nc.vector.tensor_reduce(CO[:, 2], gw(W1b), AX.X, ALU.add))
            nc.vector.tensor_scalar(CO[:, 0], CO[:, 2], 1.0 / HD, EPS, ALU.mult, ALU.add).then_inc(l1_var, 1)
            dve.wait_ge(l1_std, 1)
            own.link(nc.vector.reciprocal(CO[:, 2], CO[:, 1]))
            dve.wait_ge(l1_cen, 1)
            nc.vector.tensor_tensor(O, O, CO[:, 2].unsqueeze(3).to_broadcast(bc), ALU.mult).then_inc(l1_on, 1)
            for j, (t0, t1) in enumerate(PBLK):
                dve.wait_ge(l1_f, j + 1)
                nc.vector.tensor_tensor(tiles2(t0, t1), pair(2 + j, t0, t1), tiles2(t0, t1),
                                        ALU.add).then_inc(l1_h, 1)
            norm(3, lambda t: dve.wait_ge(l1_h, t // 2 + 1))

            dve.wait_ge(rt1_z, 1)
            n1 = TILES * E1
            z3 = rt[0][:, 0:n1]
            nc.vector.tensor_tensor(
                z3.rearrange("p (t e) -> p t e", e=E1),
                bank[6][:, 0:TILES * E1P].rearrange("p (t e) -> p t e", e=E1P)[:, :, 0:E1],
                row[:, R_RB:R_RB + E1].unsqueeze(1).to_broadcast([P, TILES, E1]), ALU.add).then_inc(rt1_b, 1)
            dve.wait_ge(rt1_p, 1)
            rank(rt[4][:, 0:n1], rt[4][:, 0:n1], E1, comb1[:], False)

            def weight1(n):
                return (lambda tile: comb1[:, tile, n - 1:n]) if n else None

            for n in range(MOE1.works):
                moe_dve(dve, MOE1, A1, S1, n, n % 2, n == 0, weight1(n), weight1(n - 1) if n else None)
            moe_low(dve, MOE1, A1, S1, E1, E1 % 2, 3 * MOE1.fc - 1)
            moe_acc(dve, MOE1, S1, E1, E1 % 2, 2, weight1(E1))


def moe_buffers(sb, scope, m, name):
    out = {}
    for key, shape, dt in (("s", [P, CHW], F32), ("t", [P, CHW], F32), ("hf", [P, CHW], F32),
                           ("hh", [P, m.fc, CHW], F32R), ("hl", [P, m.fc, CHW], F32R)):
        out[key] = [sb(f"{name}{key}{b}", shape, dt, scope) for b in range(2)]
    return out


def tail_down(pe, nc, m, W, A, S, bank):
    n, FC = m.works - 1, m.fc
    odd, c = n % 2, 2
    q = (3 * odd + c) % 2
    pe.wait_ge(S["hl_ready"], (3 * n + 3) * FC)
    for t in range(3):
        pe.wait_ge(S["acc_done"], 9 * n + 3 * c + t - 1)
        cols = slice(t * P, t * P + P)
        k = 0
        for fc in range(FC):
            hh, hl = A["hh"][q][:, fc, cols], A["hl"][q][:, fc, cols]
            for lhs, rhs in ((hh, W[odd]["dh"]), (hh, W[odd]["dl"]), (hl, W[odd]["dh"])):
                last = nc.tensor.matmul(bank[4 + (q + t) % 2][:, 0:D], lhs, rhs[:, fc, :], start=(k == 0),
                                        stop=(k == 3 * FC - 1))
                k += 1
        last.then_inc(S["down_ready"], 1)


def kernel(**inputs):
    import numpy as np
    import concourse.bacc as bacc
    from concourse.bass_utils import run_bass_kernel_spmd as run

    a = {k: np.asarray(v) for k, v in inputs.items()}

    def two(w):
        return np.concatenate([w[:P], np.concatenate([w[P:], w[P:]], axis=0)], axis=1)

    side = SIDE // PATCH
    x = a["x"].reshape(IMAGES, CHANNELS, side, PATCH, side, PATCH).transpose(0, 1, 2, 4, 3, 5)
    x = x.reshape(TOK, PATCH_K, P).transpose(2, 1, 0)
    x = np.concatenate([x[:, :, j:min(j + 2 * P, TOK)].reshape(P, -1) for j in range(0, TOK, 2 * P)], axis=1)
    tokw = a["L0_tok_W"].T.reshape(PATCH_K, P, D).transpose(1, 0, 2)

    consts = np.zeros((P, NCONST), np.float32)
    consts[:, C_ID:C_ID + P] = np.eye(P)
    i = np.arange(GW)
    same = (i[:, None] // SEQ) == (i[None, :] // SEQ)
    consts[:GW, C_MASK:C_MASK + GW] = np.where(same, 0.0, -1e30)
    consts[:GW, C_TRI:C_TRI + GW] = same & (i[:, None] <= i[None, :])
    inv = np.float32(1.0) / np.float32(10000.0) ** (np.arange(0, HD, 2, dtype=np.float32) / np.float32(HD))
    ang = (i % SEQ).astype(np.float32)[:, None] * inv[None, :]
    consts[:GW, C_COS:C_COS + HD] = np.repeat(np.cos(ang), 2, axis=1)
    consts[:GW, C_SIN:C_SIN + HD] = np.repeat(np.sin(ang), 2, axis=1) * np.where(np.arange(HD) < HD // 2, -1, 1)
    t = (i % SEQ + 1).astype(np.float32)
    consts[:GW, C_T], consts[:GW, C_RT], consts[:GW, C_NRT] = t, 1 / t, -1 / t
    e = np.arange(E0)
    consts[:, C_LOW:C_LOW + E0 * E0] = (e[None, :] < e[:, None]).astype(np.float32).reshape(1, -1)
    p = np.arange(P)
    consts[:, C_BEFORE:C_BEFORE + P] = p[:, None] < p[None, :]
    consts[:, C_ONE:C_ONE + P] = 1.0
    consts[:, C_FULL:C_FULL + FULL] = WT * np.arange(FULL)
    consts[:, C_WORK:C_WORK + WORKS] = np.arange(WORKS)

    vec = np.concatenate([a["L0_tok_b"], a["L0_ffn_gate_bias"], a["L1_ffn_routing_bias"], np.zeros(1, np.float32),
                          a["L1_attn_prior_mu"].reshape(-1), a["L1_attn_prior_log_tau"].reshape(-1)])
    rows = np.broadcast_to(vec[None, :], (P, NROWS))

    wa = two(np.concatenate([a["L0_attn_W_q"], a["L0_attn_W_k"], a["L0_attn_W_v"], a["L0_ffn_gate_w"],
                             a["L1_ffn_router_w"], np.zeros((D, 1), np.float32)], axis=1))
    wg = a["L1_attn_Wg"].reshape(HEADS, 3, D)
    l1w = two(np.concatenate([a["L1_attn_Wq"].T, a["L1_attn_Wk"].T, a["L1_attn_Wu"].T, a["L1_attn_Wv"].T,
                              wg[:, 0].T, wg[:, 1].T], axis=1))
    wo = a["L1_attn_Wo"].T.reshape(2, HALF, D).transpose(1, 0, 2)

    def expert(gate, up, down, m):
        return np.concatenate([two(gate), two(up), down.reshape(m.fc, P, D).transpose(1, 0, 2).reshape(P, -1)], axis=1)

    moe0 = [expert(a["L0_ffn_w1s"], a["L0_ffn_w3s"], a["L0_ffn_w2s"], MOE0)]
    moe0 += [expert(a["L0_ffn_w1"][j], a["L0_ffn_w3"][j], a["L0_ffn_w2"][j], MOE0) for j in range(E0)]
    moe1 = [expert(a["L1_ffn_shared_gate"], a["L1_ffn_shared_up"], a["L1_ffn_shared_down"], MOE1)]
    moe1 += [expert(a["L1_ffn_routed_gate"][j], a["L1_ffn_routed_up"][j], a["L1_ffn_routed_down"][j], MOE1)
             for j in range(E1)]

    arrays = {"patches": x, "tokw": tokw, "consts": consts, "rows": rows, "wa": wa, "l1w": l1w, "wo": wo,
              "moe0w": np.stack(moe0)[:, :, :4 * F0], "moe0d": np.stack(moe0)[:, :, 4 * F0:], "moe1w": np.stack(moe1)}
    arrays = {k: np.ascontiguousarray(v, dtype=np.float32) for k, v in arrays.items()}
    nc = bacc.Bacc("TRN2", target_bir_lowering=False, num_devices=1)
    args = [nc.dram_tensor(k, v.shape, F32, kind="ExternalInput").ap() for k, v in arrays.items()]
    out = nc.dram_tensor("out", (TOK, D), F32, kind="ExternalOutput").ap()
    xs = nc.dram_tensor("slots_in", (SLOTS, D), F32, kind="Internal").ap()
    ys = nc.dram_tensor("slots_out", (WORKS, WT, D), F32, kind="Internal").ap()
    tower(nc, *args, xs, ys, out)
    got = run(nc, [arrays], core_ids=[0]).results[0]["out"]
    return got.reshape(IMAGES, SEQ, D)
```

```python
from contextlib import ExitStack

import concourse.bass as bass
from concourse import mybir

F32 = mybir.dt.float32
F32R = mybir.dt.float32r
I32 = mybir.dt.int32
ALU = mybir.AluOpType
ACT = mybir.ActivationFunctionType
AX = mybir.AxisListType

IMAGES, CHANNELS, SIDE, PATCH = 32, 3, 96, 16
SEQ = (SIDE // PATCH) ** 2
TOK = IMAGES * SEQ
D = 192
P = 128
TILES = TOK // P
CH = 3
CHW = TOK // CH
PATCH_K = CHANNELS * PATCH * PATCH // P
GI = 3
GW = GI * SEQ
GROUPS = -(-IMAGES // GI)
XW = GROUPS * GW
BATCHES = [(0, 4), (4, 8), (8, GROUPS)]
HALF = D // 2
HEADS = 12
HD = D // HEADS
QKVG = 4 * D + 2 * HEADS
L1H = QKVG // 2 // 2 * 2
SLOT = 64
E0, F0 = 8, 768
E1, F1 = 3, 384
E1P = 4
PICKS = 2
WT = 256
WORKS = (PICKS * TOK - E0) // WT + E0
SLOTS = WORKS * WT
FULL = -(-TOK // WT)
LIMIT = 10.0
SILU_LIMIT = 9.999546021312976
NWA = 3 * D + E0 + E1P
EPS = 1e-5

LN_BANKS = (((5, 6), (7, 0), (1, 2)), ((4, 5), (6, 7), (4, 5)), ((0, 1), (6, 7), (0, 1)), ((3, 4), (0, 1), (7, 4)))

ZW = 1536

C_ID = 0
C_MASK = C_ID + P
C_TRI = C_MASK + GW
C_COS = C_TRI + GW
C_SIN = C_COS + HD
C_T = C_SIN + HD
C_RT = C_T + 1
C_NRT = C_RT + 1
C_LOW = C_NRT + 1
C_BEFORE = C_LOW + E0 * E0
C_ONE = C_BEFORE + P
C_FULL = C_ONE + P
C_WORK = C_FULL + FULL
NCONST = C_WORK + WORKS
R_TOKB = 0
R_GB = R_TOKB + D
R_RB = R_GB + E0
R_MU = R_RB + E1P
R_TAU = R_MU + D
NROWS = R_TAU + HEADS


PAIRS = [(g, min(g + 2, GROUPS)) for g in range(0, GROUPS, 2)]
CHAIN = [("us", 0), ("us", 1), ("st", 0), ("us", 2), ("et", 0), ("us", 3), ("cum", 0), ("st", 1), ("us", 4),
         ("et", 1), ("us", 5), ("cum", 1), ("st", 2), ("et", 2), ("cum", 2)]
CHAIN_AT = (0, 0, 0, 1, 2, 3, 4, 5, 7, 8, 10)
CHAIN_IN = ((10,), (11,), (12,), (), (13,), (14,))
CHAIN_BANK = [6 + i % 2 if i < CHAIN_AT[-1] else 7 for i in range(len(CHAIN))]
BATCH_OF = [b for b, (g0, g1) in enumerate(BATCHES) for _ in range(g0, g1)]
OUT_ORDER = [(k, n) for c in range(CH) for k, n in [("t", g) for g in range(*BATCHES[c])] +
             [("f", t) for t in range(3 * c, 3 * c + 3)]]
OUT_BANKS = [7] * 7 + [(5, 6, 7)[i % 3] for i in range(7)] + [(6, 5)[i % 2] for i in range(6)]
OUTPUT = [(k, n, OUT_BANKS[i], next((OUT_ORDER[j] for j in range(i - 1, -1, -1) if OUT_BANKS[j] == OUT_BANKS[i]),
                                    None)) for i, (k, n) in enumerate(OUT_ORDER)]
OUT_AT = {7: (0, 1, 2), 8: (3, 4, 5), 9: (6,)}


class Moe:

    def __init__(self, experts, width):
        self.works = experts + 1
        self.width = width
        self.fc = width // P
        self.cols = 4 * width + self.fc * D
        self.pieces = 4 + 2


MOE0, MOE1 = Moe(E0, F0), Moe(E1, F1)


class Steps:

    def __init__(self, eng, sem):
        self.eng, self.sem, self.n = eng, sem, 0

    def step(self, ins):
        ins.then_inc(self.sem, 1)
        self.n += 1

    def settle(self):
        self.eng.wait_ge(self.sem, self.n)

    def link(self, ins):
        self.step(ins)
        self.settle()


def tower(nc, patches, tokw, consts, rows, wa, l1w, wo, moe0w, moe0d, moe1w, xs, ys, out):
    with ExitStack() as ctx:
        def sb(name, shape, dt=F32, scope=ctx):
            return scope.enter_context(nc.sbuf_tensor(name, shape, dt))

        def sem(name):
            return ctx.enter_context(nc.semaphore(name))

        bank = [ctx.enter_context(nc.psum_tensor(f"bank{i}", [P, 512], F32)) for i in range(8)]

        H = sb("H", [P, TILES, D])
        Y = sb("Y", [P, TILES, 256])
        with ExitStack() as s:
            X = sb("X", [P, 4 * XW], F32R, s)
        XB = sb("XB", [P, 4 * XW])
        X01h, X01l, X2h, X2l = (X[:, i * XW:(i + 1) * XW] for i in range(4))
        const = sb("const", [P, NCONST])
        row = sb("row", [P, NROWS])
        WAh = sb("WAh", [P, NWA], F32R)
        WAl = sb("WAl", [P, NWA], F32R)
        WA2 = sb("WA2", [P, NWA], F32R)
        with ExitStack() as s:
            L1w = sb("L1w", [P, 3 * QKVG], F32R, s)
        OT = sb("OT", [HALF, 2, XW])
        L1h, L1l, L12 = (L1w[:, i * QKVG:(i + 1) * QKVG] for i in range(3))
        wo_sb = sb("wo_sb", [HALF, 2, D])
        stat = sb("stat", [P, TILES, 6])
        mv = sb("mv", [P, TILES, 2])
        ve = sb("ve", [P, TILES])
        sd = sb("sd", [P, TILES])
        rstd = sb("rstd", [P, TILES])
        comb = sb("comb", [P, TILES, E0])
        comb1 = sb("comb1", [P, TILES, E1])

        ident = const[:, C_ID:C_ID + P]
        amask = const[0:GW, C_MASK:C_MASK + GW]
        tri = const[0:GW, C_TRI:C_TRI + GW]

        tau = sb("tau", [GW, HEADS])
        tmu = sb("tmu", [GW, D])
        tden = sb("tden", [GW, HEADS])
        sT = sb("sT", [HEADS, XW])
        smax = sb("smax", [HEADS, GROUPS * GI])
        rt = [sb(f"rt{i}", [P, TILES * E0]) for i in range(6)]
        rk = [sb(f"rk{i}", [P, TILES * E0 * E0]) for i in range(2)]
        rsum = [sb(f"rsum{i}", [P, TILES]) for i in range(2)]
        sel = sb("sel", [P, TILES * E0])
        selsum = sb("selsum", [P, (TILES + 1) * E0])
        count = sb("count", [P, E0])
        works = sb("works", [P, E0])
        base = sb("base", [P, E0])
        slot = sb("slot", [P, TILES * E0])
        smx = sb("smx", [P, TILES])
        smn = sb("smn", [P, TILES])
        wpick = sb("wpick", [P, PICKS, TILES])
        idx = sb("idx", [P, PICKS, TILES], I32)
        eidf = sb("eidf", [P, WORKS])
        eid = sb("eid", [P, WORKS], I32)

        r1a, r1b = ExitStack(), ExitStack()
        W0 = []
        with r1a:
            for b in range(2):
                W0.append(dict(
                    stage=sb(f"stage{b}", [P, 4 * F0], F32, r1a),
                    h=sb(f"w0h{b}", [P, 2, F0], F32R, r1a), l=sb(f"w0l{b}", [P, 2, F0], F32R, r1a),
                    t=sb(f"w0t{b}", [P, 2, F0], F32R, r1a), down=sb(f"w0d{b}", [P, MOE0.fc, D], F32, r1a)))
            XR = [sb(f"XR{b}", [P, WT // P, 256], F32, r1a) for b in range(2)]
            XWh = [sb(f"XWh{b}", [P, 2 * WT], F32R, r1a) for b in range(2)]
            XWl = [sb(f"XWl{b}", [P, 2 * WT], F32R, r1a) for b in range(2)]
            YO = [sb(f"YO{b}", [P, WT // P, D], F32, r1a) for b in range(2)]
            with ExitStack() as s:
                patch = sb("patch", [P, PATCH_K * TOK], F32, s)
                tokw_sb = sb("tokw_sb", [P, PATCH_K, D], F32, s)
                zero = sb("zero", [P, ZW], F32, s)
            with ExitStack() as s:
                qT = sb("qT", [HALF, 2, XW], F32, s)
                kT = sb("kT", [HALF, 2, XW], F32, s)
                V = sb("V", [GW, GROUPS, D], F32, s)
                Pm = sb("Pm", [GW, GROUPS, GW], F32, s)
                PT = sb("PT", [GW, GROUPS, GW], F32, s)
                oT = sb("oT", [HALF, 2, XW], F32, s)
                mx = sb("mx", [GW, GROUPS], F32, s)
                rs = sb("rs", [GW, GROUPS], F32, s)
                rr = sb("rr", [GW, GROUPS], F32, s)
            with ExitStack() as s:
                A0 = dict(s=[sb(f"a0s{b}", [P, CHW], F32, s) for b in range(2)],
                          t=[sb(f"a0t{b}", [P, CHW], F32, s) for b in range(2)],
                          h=[sb(f"a0h{b}", [P, MOE0.fc, CHW], F32, s) for b in range(2)])
                G = sb("G", [P, TILES, PICKS, D], F32, s)
        with r1b:
            QK = sb("QK", [GW, GROUPS, QKVG], F32, r1b)
            rotA = [sb(f"rotA{b}", [GW, 2, 2 * D], F32, r1b) for b in range(2)]
            rotB = [sb(f"rotB{b}", [GW, 2, 2 * D], F32, r1b) for b in range(2)]
            qkw = sb("qkw", [GW, 2, 2, 2, HEADS, SLOT], F32, r1b)
            qw, kw = ([qkw[:, b, i] for b in range(2)] for i in range(2))
            AT = [sb(f"AT{b}", [GW, HEADS, GW], F32, r1b) for b in range(2)]
            EG = sb("EG", [GW, GROUPS, 2 * HEADS], F32, r1b)
            UB = sb("UB", [GW, GROUPS, HEADS], F32, r1b)
            HM, HV, HR = (sb(n, [GW, GROUPS, HEADS], F32, r1b) for n in ("HM", "HV", "HR"))
            ES = sb("ES", [GW, GROUPS, 2 * HEADS], F32, r1b)
            SG = sb("SG", [GW, GROUPS, 2 * HEADS], F32, r1b)
            CO = sb("CO", [GW, 3, GROUPS, HEADS], F32, r1b)
            W1 = []
            for b in range(2):
                W1.append(dict(
                    stage=sb(f"stage1{b}", [P, MOE1.cols], F32, r1b),
                    h=sb(f"w1h{b}", [P, 2, F1], F32R, r1b), l=sb(f"w1l{b}", [P, 2, F1], F32R, r1b),
                    t=sb(f"w1t{b}", [P, 2, F1], F32R, r1b),
                    dh=sb(f"d1h{b}", [P, MOE1.fc, D], F32R, r1b), dl=sb(f"d1l{b}", [P, MOE1.fc, D], F32R, r1b)))
            CK = [sb(f"CK{b}", [GW, 2, 2, HEADS], F32, r1b) for b in range(2)]
            CQ = [sb(f"CQ{b}", [GW, 3, 2, HEADS], F32, r1b) for b in range(2)]
            nrm = [sb(f"nrm{b}", [GW, 2, 2 * HEADS], F32, r1b) for b in range(2)]
            rn = [sb(f"rn{b}", [GW, 2, 2 * HEADS], F32, r1b) for b in range(2)]
        with ExitStack() as s:
            A1 = moe_buffers(sb, s, MOE1, "a1")
        ld_patch = [sem(f"ld_patch{j}") for j in range(5)]
        ld_tokw, ld_const, ld_row, ld_wo = sem("ld_tokw"), sem("ld_const"), sem("ld_row"), sem("ld_wo")
        ld_stage = [sem(f"ld_stage{b}") for b in range(2)]
        ld_stage1 = [sem(f"ld_stage1{b}") for b in range(2)]
        pads = sem("pads")
        split_hi, split_lo = sem("split_hi"), sem("split_lo")
        tok_done = sem("tok_done")
        dve_step, pool_step = sem("dve_step"), sem("pool_step")
        ln_var, ln_sd, ln_y, ln_xt, ln_hi, ln_lo = (sem("ln_" + s) for s in ("var", "sd", "y", "xt", "hi", "lo"))
        proj_done = sem("proj_done")
        proj_out = [sem("proj_act"), sem("proj_dve")]
        a0_s, a0_shift, a0_exp, a0_p, a0_pt, a0_ptc, a0_o, a0_back = (
            sem("a0_" + s) for s in ("s", "shift", "exp", "p", "pt", "ptc", "o", "back"))
        a0_oc = [sem("a0_oc_act"), sem("a0_oc_dve")]
        rt_z, rt_neg, rt_e, rt_u, rt_ln, rt_sp, rt_sc = (
            sem("rt_" + s) for s in ("z", "neg", "e", "u", "ln", "sp", "sc"))
        rt1_z, rt1_b, rt1_p = sem("rt1_z"), sem("rt1_b"), sem("rt1_p")
        r_own, r_sel, r_pos, r_idx, r_eid = (sem("r_" + s) for s in ("own", "sel", "pos", "idx", "eid"))
        zeroed, zero_set, scattered = sem("zeroed"), sem("zero_set"), sem("scattered")
        ld_w2 = [sem(f"ld_w2{b}") for b in range(2)]
        ld_x = [sem(f"ld_x{b}") for b in range(2)]
        st_y = [sem(f"st_y{b}") for b in range(2)]
        ld_g = [sem(f"ld_g{c}") for c in range(CH)]
        x_T, x_hi, x_lo, y_done = (sem(s) for s in ("x_T", "x_hi", "x_lo", "y_done"))
        moe_sems = [{k: sem(f"moe{m}_{k}") for k in names} for m, names in enumerate((
            ("w_hi", "w_lo", "gu_ready", "silu_ready", "clip_ready", "h_ready", "down_ready", "acc_done"),
            ("w_hi", "w_lo", "gu_ready", "silu_ready", "h_ready", "hh_ready", "hl_ready", "down_ready",
             "acc_done")))]
        (l1_proj, l1_out, l1_chain, l1_read, l1_s, l1_ex, l1_eg, l1_tau, l1_zero) = (
            sem("l1_" + s) for s in ("proj", "out", "chain", "read", "s", "ex", "eg", "tau", "zero"))
        (l1_ra, l1_rb, l1_rope, l1_sq, l1_n2, l1_nr, l1_ck, l1_qw, l1_kw, l1_T, l1_Tc, l1_A, l1_Am, l1_O, l1_Oc) = (
            sem("l1_" + s) for s in ("ra", "rb", "rope", "sq", "n2", "nr", "ck", "qw", "kw", "T", "Tc", "A", "Am",
                                     "O", "Oc"))
        (l1_mu, l1_cen, l1_csq, l1_var, l1_std, l1_hr, l1_on, l1_oT, l1_oTc, l1_f, l1_h) = (
            sem("l1_" + s) for s in ("mu", "cen", "csq", "var", "std", "hr", "on", "oT", "oTc", "f", "h"))
        stored = sem("stored")

        def terms(weights, wcols, xcols):
            wh, wl, w2 = weights
            return [(X01h[:, xcols], wh[wcols]), (X01h[:, xcols], wl[wcols]), (X01l[:, xcols], wh[wcols]),
                    (X2h[:, xcols], w2[wcols]), (X2l[:, xcols], w2[wcols])]

        def wcols2(a, b):
            return (slice(0, P), slice(a, b))

        W2 = 6 * 2 * GW
        qT1 = [XB[:, b * W2:(b + 1) * W2].rearrange("p (i c q) -> p i c q", c=2, q=GW) for b in range(2)]
        kT1 = [XB[:, 2 * W2 + b * 6 * GW:2 * W2 + (b + 1) * 6 * GW].rearrange("p (i q) -> p i q", q=GW)
               for b in range(2)]
        W1b = Y[0:GW].rearrange("p a b -> p (a b)")[:, 0:GROUPS * D].rearrange("p (g d) -> p g d", d=D)

        block = ctx.enter_context(nc.Block())
        PBLK = [(2 * j, min(2 * j + 2, TILES)) for j in range(5)]

        @block.sync
        def _(sp):
            sp.dma_start(tokw_sb[:], tokw).then_inc(ld_tokw, 16)
            for j, (t0, t1) in enumerate(PBLK):
                a, b = t0 * P * PATCH_K, t1 * P * PATCH_K
                sp.dma_start(patch[:, a:b], patches[:, a:b]).then_inc(ld_patch[j], 16)
                if j == 0:
                    sp.dma_start(row[:], rows).then_inc(ld_row, 16)
                    sp.dma_start(const[:], consts).then_inc(ld_const, 16)
            sp.dma_start(W0[0]["stage"][:, 0:2 * NWA], wa).then_inc(ld_stage[0], 16)
            sp.dma_start(W0[1]["stage"][:, 0:2 * QKVG], l1w).then_inc(ld_stage[1], 16)
            sp.dma_start(wo_sb[:], wo).then_inc(ld_wo, 16)
            sp.wait_ge(zero_set, 1)
            xz = xs.rearrange("(p j) d -> p (j d)", p=P)
            for j in range(SLOTS // P * D // ZW):
                sp.dma_start(xz[:, j * ZW:(j + 1) * ZW], zero[:]).then_inc(zeroed, 16)
            S = moe_sems[0]
            sp.wait_ge(split_lo, 2)
            sp.dma_start(W0[0]["stage"][:], moe0w[0]).then_inc(ld_stage[0], 16)
            sp.dma_start(W0[0]["down"].rearrange("p a b -> p (a b)"), moe0d[0]).then_inc(ld_w2[0], 16)
            sp.wait_ge(split_lo, 4)
            sp.wait_ge(r_eid, 1)
            experts = {}

            def load_weights(n):
                if n >= 2:
                    sp.wait_ge(S["w_lo"], 4 * (n - 1))
                experts[n] = sp.value_load(eid[0:1, n - 1:n], min_val=1, max_val=E0)
                sp.dma_start(W0[n % 2]["stage"][:], moe0w[bass.ds(experts[n], 1)].rearrange(
                    "e p c -> (e p) c")).then_inc(ld_stage[n % 2], 16)

            def load_down(n):
                if n >= 2:
                    sp.wait_ge(S["down_ready"], 9 + 2 * (n - 2))
                sp.dma_start(W0[n % 2]["down"].rearrange("p a b -> p (a b)"), moe0d[bass.ds(
                    experts[n], 1)].rearrange("e p c -> (e p) c")).then_inc(ld_w2[n % 2], 16)

            def load_rows(n):
                if n >= 3:
                    sp.wait_ge(x_T, n - 2)
                rows = xs[(n - 1) * WT:n * WT, :].rearrange("(a p) d -> p a d", p=P)
                sp.dma_start(XR[n % 2][:, :, 0:D], rows).then_inc(ld_x[n % 2], 16)
                sp.dma_start(XR[n % 2][:, :, D:256], rows[:, :, P:D]).then_inc(ld_x[n % 2], 16)

            load_weights(1)
            load_down(1)
            load_weights(2)
            sp.wait_ge(scattered, 16 * PICKS * TILES)
            load_rows(1)
            load_rows(2)
            for n in range(2, WORKS + 1):
                if n > 2:
                    load_rows(n)
                if n < WORKS:
                    load_weights(n + 1)
                load_down(n)
            sp.wait_ge(ln_var, 3 * CH)
            for n in range(MOE1.works):
                if n >= 2:
                    sp.wait_ge(moe_sems[1]["w_lo"], MOE1.pieces * (n - 1))
                sp.dma_start(W1[n % 2]["stage"][:], moe1w[n]).then_inc(ld_stage1[n % 2], 16)
            last = (MOE1.works - 1) * TILES
            for c in range(CH):
                sp.wait_ge(moe_sems[1]["acc_done"], last + 3 * (c + 1))
                sp.dma_start(out.rearrange("(t p) d -> p t d", p=P)[:, 3 * c:3 * c + 3, :],
                             H[:, 3 * c:3 * c + 3, :]).then_inc(stored, 16)
            sp.wait_ge(stored, 16 * CH)

        def moe_pe(pe, m, W, A, S, n, odd, first, after=None):
            FC = m.fc

            def gate_up(c):
                if c == 0:
                    pe.wait_ge(S["w_lo"], n * m.pieces + m.pieces)
                for fc in range(FC):
                    par = ((3 * odd + c) * FC + fc) % 2
                    if not (first and c == 0 and fc < 2):
                        pe.wait_ge(S["h_ready"], n * (3 * FC) + (c * FC + fc - 1))
                    for mat, bk in ((0, par), (1, 2 + par)):
                        w = W[odd]
                        ts = terms((w["h"][:], w["l"][:], w["t"][:]),
                                   (slice(0, P), mat, slice(fc * P, fc * P + P)), slice(c * CHW, c * CHW + CHW))
                        for i, (x, wt) in enumerate(ts):
                            last = nc.tensor.matmul(bank[bk][:, 0:CHW], wt, x, start=(i == 0), stop=(i == 4))
                    last.then_inc(S["gu_ready"], 1)

            def down(nn, o, c):
                q = (o * 3 + c) % 2
                pe.wait_ge(S["hl_ready"], nn * (3 * FC) + (c + 1) * FC)
                for t in range(3):
                    d = 9 * nn + 3 * c + t
                    if d >= 4:
                        pe.wait_ge(S["acc_done"], d - 3)
                    w = W[o]
                    cols = slice(t * P, t * P + P)
                    k = 0
                    for fc in range(FC):
                        hh, hl = A["hh"][q][:, fc, cols], A["hl"][q][:, fc, cols]
                        for lhs, rhs in ((hh, w["dh"]), (hh, w["dl"]), (hl, w["dh"])):
                            last = nc.tensor.matmul(bank[4 + d % 4][:, 0:D], lhs, rhs[:, fc, :],
                                                    start=(k == 0), stop=(k == 3 * FC - 1))
                            k += 1
                    last.then_inc(S["down_ready"], 1)

            gate_up(0)
            if after is not None:
                after()
            if not first:
                down(n - 1, 1 - odd, 2)
            gate_up(1)
            down(n, odd, 0)
            gate_up(2)
            down(n, odd, 1)
            return down

        def split_hi_piece(m, W, odd, i):
            w, F = W[odd], m.width
            if i < 4:
                mat, two = i // 2, i % 2
                src = w["stage"][:, (2 * mat + two) * F:(2 * mat + two + 1) * F]
                return src, (w["t"] if two else w["h"])[:, mat, :]
            a, b = ((0, m.fc - 1), (m.fc - 1, m.fc))[i - 4]
            src = w["stage"][:, 4 * F + a * D:4 * F + b * D].rearrange("p (f d) -> p f d", d=D)
            return src, w["dh"][:, a:b, :]

        def split_lo_piece(m, W, odd, i):
            w, F = W[odd], m.width
            src, hi = split_hi_piece(m, W, odd, i)
            if i < 4:
                mat, two = i // 2, i % 2
                if two:
                    t = w["t"][64:P, mat, :]
                    return src[64:P], t, t
                return src, hi, w["l"][:, mat, :]
            a, b = ((0, m.fc - 1), (m.fc - 1, m.fc))[i - 4]
            return src, hi, w["dl"][:, a:b, :]

        def moe_weights_act(act, m, W, S, L, n, odd, i, used, n_pairs):
            if i == 0:
                act.wait_ge(L[odd], n_pairs)
                if used is not None:
                    act.wait_ge(S["down_ready"], used)
            src, hi = split_hi_piece(m, W, odd, i)
            nc.scalar.activation(hi, src, ACT.Copy).then_inc(S["w_hi"], 1)

        def moe_weights_pool(pool, m, W, S, n, odd, pieces=None):
            for i in range(m.pieces) if pieces is None else pieces:
                if i or n:
                    pool.wait_ge(S["w_lo"], n * m.pieces + i)
                pool.wait_ge(S["w_hi"], n * m.pieces + (i + 1))
                src, hi, dst = split_lo_piece(m, W, odd, i)
                nc.gpsimd.tensor_tensor(dst, src, hi.bitcast(F32), ALU.subtract).then_inc(S["w_lo"], 1)

        def moe_act(act, m, W, A, S, L, n, odd, first, last, n_pairs, after=None):
            FC = m.fc
            for c in range(CH):
                for fc in range(FC):
                    par = ((3 * odd + c) * FC + fc) % 2
                    k1 = c * FC + fc + 1
                    act.wait_ge(S["gu_ready"], n * (3 * FC) + k1)
                    if not (first and k1 <= 2):
                        act.wait_ge(S["h_ready"], n * (3 * FC) + (k1 - 2))
                    nc.scalar.activation(A["s"][par][:], bank[par][:, 0:CHW], ACT.Silu).then_inc(S["silu_ready"], 1)
                    if not (first and k1 == 1):
                        moe_high(act, m, A, S, n, odd, c * FC + fc - 1)
                    if after is not None and k1 == FC:
                        after()
                    i = (c - 1) * FC + fc
                    if not last and 0 <= i < m.pieces:
                        used = n * 9 if not first else None
                        moe_weights_act(act, m, W, S, L, n + 1, 1 - odd, i, used, n_pairs)

        def moe_high(act, m, A, S, n, odd, k):
            FC = m.fc
            kk = (3 * odd * FC + k) % (6 * FC)
            q, fc, par = (kk // FC) % 2, kk % FC, kk % 2
            act.wait_ge(S["h_ready"], n * (3 * FC) + (k + 1))
            nc.scalar.activation(A["hh"][q][:, fc, :], A["hf"][par][:], ACT.Copy).then_inc(S["hh_ready"], 1)

        def moe_low(dve, m, A, S, n, odd, k):
            FC = m.fc
            kk = (3 * odd * FC + k) % (6 * FC)
            q, fc, par = (kk // FC) % 2, kk % FC, kk % 2
            dve.wait_ge(S["hh_ready"], n * (3 * FC) + (k + 1))
            nc.vector.tensor_tensor(A["hl"][q][:, fc, :], A["hf"][par][:], A["hh"][q][:, fc, :].bitcast(F32),
                                    ALU.subtract).then_inc(S["hl_ready"], 1)

        def moe_acc(dve, m, S, n, c, weight):
            for t in range(3):
                tile = 3 * c + t
                dve.wait_ge(S["down_ready"], n * 9 + (tile + 1))
                if weight is None:
                    nc.vector.tensor_tensor(H[:, tile, :], bank[4 + (9 * n + tile) % 4][:, 0:D], H[:, tile, :],
                                            ALU.add).then_inc(S["acc_done"], 1)
                else:
                    dve.wait_ge(S["acc_done"], n * 9 + (tile - 8))
                    nc.vector.scalar_tensor_tensor(
                        out=H[:, tile, :], in0=bank[4 + (9 * n + tile) % 4][:, 0:D], scalar=weight(tile),
                        in1=H[:, tile, :], op0=ALU.mult, op1=ALU.add).then_inc(S["acc_done"], 1)

        def moe_dve(dve, m, A, S, n, odd, first, weight, before, after=None):
            FC = m.fc
            for c in range(CH):
                for fc in range(FC):
                    par = ((3 * odd + c) * FC + fc) % 2
                    k1 = c * FC + fc + 1
                    dve.wait_ge(S["gu_ready"], n * (3 * FC) + k1)
                    dve.wait_ge(S["silu_ready"], n * (3 * FC) + k1)
                    if not (first and k1 <= 2):
                        dve.wait_ge(S["hl_ready"], n * (3 * FC) + (k1 - 2))
                    nc.vector.tensor_tensor(A["hf"][par][:], bank[2 + par][:, 0:CHW], A["s"][par][:],
                                            ALU.mult).then_inc(S["h_ready"], 1)
                    if not (first and k1 == 1):
                        moe_low(dve, m, A, S, n, odd, k1 - 2)
                if after is not None and c == 0:
                    after()
                if c == 0 and not first:
                    moe_acc(dve, m, S, n - 1, 2, before)
                elif c > 0:
                    moe_acc(dve, m, S, n, c - 1, weight)

        FC0 = MOE0.fc
        S0, S1 = moe_sems

        def e_operands(n, c, w, cols):
            ws = [w["h"][cols], w["l"][cols], w["h"][cols], w["t"][cols], w["t"][cols]]
            if c is not None:
                xc = slice(c * CHW, (c + 1) * CHW)
                xpart = [X01h[:, xc], X01h[:, xc], X01l[:, xc], X2h[:, xc], X2l[:, xc]]
            else:
                h, l = XWh[n], XWl[n]
                xpart = [h[:, 0:WT], h[:, 0:WT], l[:, 0:WT], h[:, WT:2 * WT], l[:, WT:2 * WT]]
            return list(zip(xpart, ws))

        def e_gate_up(pe, q, n, par, c, units=range(MOE0.fc)):
            width = WT if c is None else CHW
            if units[0] == 0:
                if c is None:
                    pe.wait_ge(x_lo, n)
                pe.wait_ge(S0["w_lo"], n * 4 + 4)
            for fc in units:
                if not (isinstance(q, int) and q == 0 and fc < 2):
                    pe.wait_ge(S0["silu_ready"], q * FC0 + (fc - 1))
                    pe.wait_ge(S0["clip_ready"], q * FC0 + (fc - 1))
                for mat in range(2):
                    for i, (x, w) in enumerate(e_operands(par, c, W0[par], (slice(0, P), mat,
                                                                            slice(fc * P, fc * P + P)))):
                        last = nc.tensor.matmul(bank[2 * mat + fc % 2][:, 0:width], w, x, start=(i == 0),
                                                stop=(i == 4))
                last.then_inc(S0["gu_ready"], 1)

        def e_down(pe, q, qpar, n, par, shared, loaded):
            pe.wait_ge(S0["h_ready"], q * FC0 + FC0)
            pe.wait_ge(ld_w2[par], loaded)
            for t in range(3 if shared else 2):
                if shared:
                    d = 3 * q + t
                    if d >= 2:
                        pe.wait_ge(S0["acc_done"], d - 1)
                elif isinstance(n, int) and n == 1:
                    pe.wait_ge(S0["acc_done"], 8 + t)
                else:
                    pe.wait_ge(y_done, n * 2 + (t - 3))
                for fc in range(FC0):
                    last = nc.tensor.matmul(bank[e_bank(qpar, t, shared)][:, 0:D],
                                            A0["h"][qpar][:, fc, t * P:(t + 1) * P], W0[par]["down"][:, fc, :],
                                            start=(fc == 0), stop=(fc == FC0 - 1))
                last.then_inc(S0["down_ready"], 1)

        def e_bank(qpar, t, shared):
            return 4 + ((qpar + t) % 2 if shared else (1 + t) % 2)

        def e_rows(pe, n, par, loaded):
            pe.wait_ge(ld_x[par], loaded)
            if not (isinstance(n, int) and n == 1):
                pe.wait_ge(x_lo, n - 1)
            for half in range(2):
                for t in range(WT // P):
                    last = nc.tensor.transpose(bank[6][:, half * WT + t * P:half * WT + (t + 1) * P],
                                               XR[par][:, t, half * P:(half + 1) * P], ident)
            last.then_inc(x_T, 1)

        def e_split_act(act, n, par, i, staged, q):
            if i == 0:
                act.wait_ge(ld_stage[par], staged)
                if q is not None:
                    act.wait_ge(S0["gu_ready"], q * FC0)
            mat, two = i // 2, i % 2
            nc.scalar.activation(W0[par]["t" if two else "h"][:, mat, :],
                                 W0[par]["stage"][:, (2 * mat + two) * F0:(2 * mat + two + 1) * F0],
                                 ACT.Copy).then_inc(S0["w_hi"], 1)

        def e_split_low(engine, eng, n, par):
            for i in range(4):
                eng.wait_ge(S0["w_hi"], n * 4 + (i + 1))
                if i or not isinstance(n, int) or n:
                    eng.wait_ge(S0["w_lo"], n * 4 + i)
                mat, two = i // 2, i % 2
                src = W0[par]["stage"][:, (2 * mat + two) * F0:(2 * mat + two + 1) * F0]
                if two:
                    dst = W0[par]["t"][64:P, mat, :]
                    ins = engine.tensor_tensor(dst, src[64:P], dst.bitcast(F32), ALU.subtract)
                else:
                    ins = engine.tensor_tensor(W0[par]["l"][:, mat, :], src, W0[par]["h"][:, mat, :].bitcast(F32),
                                               ALU.subtract)
                ins.then_inc(S0["w_lo"], 1)

        def e_act(act, q, width, following, rows, store, between={}):
            for fc in range(FC0):
                act.wait_ge(S0["gu_ready"], q * FC0 + (fc + 1))
                if not (isinstance(q, int) and q == 0 and fc < 2):
                    act.wait_ge(S0["h_ready"], q * FC0 + (fc - 1))
                nc.scalar.activation(A0["s"][fc % 2][:, 0:width], bank[fc % 2][:, 0:width],
                                     ACT.Silu).then_inc(S0["silu_ready"], 1)
                if following is not None and 1 <= fc <= 4:
                    e_split_act(act, *following[:2], fc - 1, *following[2:])
                if store is not None and fc == 5:
                    e_store(act, *store)
                if fc in between:
                    between[fc]()
            if rows is not None:
                n, par, used = rows
                act.wait_ge(x_T, n)
                if used is not None:
                    act.wait_ge(S0["gu_ready"], used)
                nc.scalar.activation(XWh[par][:], bank[6][:], ACT.Copy).then_inc(x_hi, 1)

        def e_store(act, n, par):
            act.wait_ge(y_done, n * 2)
            dst = ys[bass.ds(n - 1, 1)] if not isinstance(n, int) else ys[n - 1:n]
            act.dma_start(dst.rearrange("w (a p) d -> p (w a) d", p=P), YO[par][:]).then_inc(st_y[par], 16)

        def e_dve(dve, q, qpar, width, freed, rows, before, between={}):
            if freed is not None:
                dve.wait_ge(S0["down_ready"], freed)
            for fc in range(FC0):
                dve.wait_ge(S0["gu_ready"], q * FC0 + (fc + 1))
                nc.vector.tensor_scalar(A0["t"][fc % 2][:, 0:width], bank[2 + fc % 2][:, 0:width], LIMIT, -LIMIT,
                                        ALU.min, ALU.max).then_inc(S0["clip_ready"], 1)
                dve.wait_ge(S0["silu_ready"], q * FC0 + (fc + 1))
                dve.wait_ge(S0["clip_ready"], q * FC0 + (fc + 1))
                nc.vector.scalar_tensor_tensor(out=A0["h"][qpar][:, fc, 0:width], in0=A0["s"][fc % 2][:, 0:width],
                                               scalar=SILU_LIMIT, in1=A0["t"][fc % 2][:, 0:width], op0=ALU.min,
                                               op1=ALU.mult).then_inc(S0["h_ready"], 1)
                if fc in between:
                    between[fc]()
            if rows is not None:
                n, par = rows
                dve.wait_ge(x_hi, n)
                nc.vector.tensor_tensor(XWl[par][:], bank[6][:], XWh[par][:].bitcast(F32),
                                        ALU.subtract).then_inc(x_lo, 1)
            if before is not None:
                before()

        def e_acc(dve, c):
            for t in range(3):
                dve.wait_ge(S0["down_ready"], 3 * c + t + 1)
                nc.vector.tensor_tensor(H[:, 3 * c + t, :], bank[e_bank(c % 2, t, True)][:, 0:D], H[:, 3 * c + t, :],
                                        ALU.add).then_inc(S0["acc_done"], 1)

        def e_copy(dve, n, par, stored_):
            if stored_ is not None:
                dve.wait_ge(st_y[par], stored_)
            for t in range(WT // P):
                dve.wait_ge(S0["down_ready"], n * 2 + (8 + t))
                nc.vector.tensor_copy(YO[par][:, t, :], bank[e_bank(0, t, False)][:, 0:D]).then_inc(y_done, 1)

        @block.tensor
        def _(pe):
            def transposes(k, c):
                if (k, c) == (0, 0):
                    pe.wait_ge(ld_const, 16)
                pe.wait_ge(ln_y, 3 * k + c + 1)
                for half in range(2):
                    for t in range(3):
                        last = nc.tensor.transpose(bank[LN_BANKS[k][c][half]][:, t * P:(t + 1) * P],
                                                   Y[:, 3 * c + t, half * P:(half + 1) * P], ident)
                last.then_inc(ln_xt, 1)

            pe.wait_ge(ld_tokw, 16)
            for j, (t0, t1) in enumerate(PBLK):
                pe.wait_ge(ld_patch[j], 16)
                n = (t1 - t0) * P
                pb = patch[:, t0 * P * PATCH_K:t1 * P * PATCH_K].rearrange("p (k n) -> p k n", n=n)
                for t in range(t1 - t0):
                    for k in range(PATCH_K):
                        last = nc.tensor.matmul(bank[j][:, t * D:(t + 1) * D], pb[:, k, t * P:(t + 1) * P],
                                                tokw_sb[:, k, :], start=(k == 0), stop=(k == PATCH_K - 1))
                last.then_inc(tok_done, 1)
                if j >= 3:
                    transposes(0, j - 3)


            transposes(0, 2)
            pe.wait_ge(ln_lo, 6)
            pe.wait_ge(split_lo, 2)
            pe.wait_ge(pads, 4)
            wa3 = (WAh, WAl, WA2)
            jobs = [("t", mat * D + half * HALF, c) for mat in range(2) for half in range(2) for c in range(3)]
            jobs += [("v", g, 0) for g in range(0, GROUPS, 2)]
            for j, (kind, a, c) in enumerate(jobs):
                if j >= 8:
                    pe.wait_ge(proj_out[j % 2], (j - 8) // 2 + 1)
                if kind == "t":
                    w3 = XW // 3
                    for i, (x, w) in enumerate(terms(wa3, wcols2(a, a + HALF), slice(c * w3, (c + 1) * w3))):
                        last = nc.tensor.matmul(bank[j % 8][0:HALF, 0:w3], w, x, start=(i == 0), stop=(i == 4))
                else:
                    for g in range(a, min(a + 2, GROUPS)):
                        for i, (x, w) in enumerate(terms(wa3, wcols2(2 * D, 3 * D), slice(g * GW, (g + 1) * GW))):
                            last = nc.tensor.matmul(bank[j % 8][0:GW, (g - a) * D:(g - a + 1) * D], x, w,
                                                    start=(i == 0), stop=(i == 4))
                last.then_inc(proj_done, 1)
            pe.wait_ge(proj_out[0], 7)
            pe.wait_ge(proj_out[1], 6)
            for b, (g0, g1) in enumerate(BATCHES):
                for g in range(g0, g1):
                    cols = slice(g * GW, (g + 1) * GW)
                    for half in range(2):
                        last = nc.tensor.matmul(bank[2 + b][0:GW, (g - g0) * GW:(g - g0 + 1) * GW],
                                                qT[:, half, cols], kT[:, half, cols], start=(half == 0),
                                                stop=(half == 1))
                last.then_inc(a0_s, 1)
            pe.wait_ge(proj_out[0], 9)
            pe.wait_ge(proj_out[1], 9)
            for b, (g0, g1) in enumerate(BATCHES):
                pe.wait_ge(a0_p, b + 1)
                for g in range(g0, g1):
                    last = nc.tensor.transpose(bank[5 + b][0:GW, (g - g0) * GW:(g - g0 + 1) * GW], Pm[:, g, :],
                                               ident[0:GW, 0:GW])
                last.then_inc(a0_pt, 1)
            for b, (g0, g1) in enumerate(BATCHES):
                pe.wait_ge(a0_ptc, b + 1)
                for half in range(2):
                    for g in range(g0, g1):
                        last = nc.tensor.matmul(bank[2 * b + half][0:HALF, (g - g0) * GW:(g - g0 + 1) * GW],
                                                V[:, g, half * HALF:(half + 1) * HALF], PT[:, g, :],
                                                start=True, stop=True)
                    last.then_inc(a0_o, 1)
            pe.wait_ge(a0_oc[0], 3)
            pe.wait_ge(a0_oc[1], 3)
            for j, (t0, t1) in enumerate(PBLK):
                for t in range(t0, t1):
                    for half in range(2):
                        last = nc.tensor.transpose(
                            bank[(6 + j) % 8][:, (t - t0) * D + half * HALF:(t - t0) * D + (half + 1) * HALF],
                            oT[:, half, t * P:(t + 1) * P], ident[0:HALF, 0:HALF])
                last.then_inc(a0_back, 1)

            def router(col, width, z):
                for t in range(TILES):
                    for i, (x, w) in enumerate(terms(wa3, wcols2(col, col + width), slice(t * P, (t + 1) * P))):
                        last = nc.tensor.matmul(bank[6][:, t * width:(t + 1) * width], x, w, start=(i == 0),
                                                stop=(i == 4))
                last.then_inc(z, 1)

            transposes(1, 0)
            transposes(1, 1)
            pe.wait_ge(ln_lo, 8)
            transposes(1, 2)
            e_gate_up(pe, 0, 0, 0, 0, range(3))
            pe.wait_ge(ln_lo, 12)
            router(3 * D, E0, rt_z)
            e_gate_up(pe, 0, 0, 0, 0, range(3, FC0))
            e_gate_up(pe, 1, 0, 0, 1, range(2))
            pe.wait_ge(r_sel, 1)
            nc.tensor.matmul(bank[7][:, 0:(TILES + 1) * E0], const[:, C_ONE:C_ONE + P], selsum[:], start=True,
                             stop=False)
            nc.tensor.matmul(bank[7][:, 0:TILES * E0], const[:, C_BEFORE:C_BEFORE + P], sel[:], start=False,
                             stop=True).then_inc(r_pos, 1)
            e_gate_up(pe, 1, 0, 0, 1, range(2, FC0))
            e_down(pe, 0, 0, 0, 0, True, 16)
            e_gate_up(pe, 2, 0, 0, 2)
            e_down(pe, 1, 1, 0, 0, True, 16)
            e_down(pe, 2, 0, 0, 0, True, 16)
            e_rows(pe, 1, 1, 32)

            def e_pe(n, par, x_loaded, w2_loaded, last=False):
                e_gate_up(pe, n + 2, n, par, None)
                if not last:
                    e_rows(pe, n + 1, 1 - par, x_loaded)
                if w2_loaded is not None:
                    e_down(pe, n + 1, 1 - par, n - 1, 1 - par, False, w2_loaded)

            e_pe(1, 1, 32, None)
            e_pe(2, 0, 64, 16)
            e_pe(3, 1, 64, 32)
            e_pe(4, 0, 96, 32)
            with pe.Fori(0, (WORKS - 6) // 2, 1) as i:
                e_pe(i * 2 + 5, 1, i * 32 + 96, i * 16 + 48)
                e_pe(i * 2 + 6, 0, i * 32 + 128, i * 16 + 48)
            e_pe(WORKS - 1, 1, 16 * WORKS, 8 * WORKS)
            e_pe(WORKS, 0, None, 8 * WORKS, last=True)
            e_down(pe, WORKS + 2, 0, WORKS, 0, False, 8 * WORKS + 16)

            transposes(2, 0)
            pe.wait_ge(split_lo, 4)
            l13 = (L1h, L1l, L12)

            def chain(i):
                kind, j = CHAIN[i]
                b = CHAIN_BANK[i]
                if i >= 2:
                    pe.wait_ge(l1_read, i - 1 if i < CHAIN_AT[-1] else i)
                if kind == "us":
                    g0, g1 = PAIRS[j]
                    pe.wait_ge(l1_out, 2 * g1)
                    for g in range(g0, g1):
                        last = nc.tensor.matmul(bank[b][0:GW, (g - g0) * D:(g - g0 + 1) * D], tri,
                                                QK[:, g, 2 * D:3 * D], start=True, stop=True)
                    last.then_inc(l1_chain, 1)
                    return
                g0, g1 = BATCHES[j]
                if kind == "st":
                    pe.wait_ge(l1_s, -(-g1 // 2))
                elif kind == "et":
                    pe.wait_ge(l1_ex, j + 1)
                else:
                    pe.wait_ge(l1_read, CHAIN.index(("et", j)) + 1)
                for g in range(g0, g1):
                    k = g - g0
                    if kind == "st":
                        last = nc.tensor.transpose(bank[b][0:HEADS, k * GW:(k + 1) * GW],
                                                   ES[:, g, HEADS:2 * HEADS], ident[0:GW, 0:GW])
                    elif kind == "et":
                        last = nc.tensor.transpose(bank[b][0:GW, k * HEADS:(k + 1) * HEADS],
                                                   sT[:, g * GW:(g + 1) * GW], ident[0:HEADS, 0:HEADS])
                    else:
                        last = nc.tensor.matmul(bank[b][0:GW, k * 2 * HEADS:(k + 1) * 2 * HEADS], tri, ES[:, g, :],
                                                start=True, stop=True)
                last.then_inc(l1_chain, 1)

            link = 0
            for g in range(GROUPS):
                if g == 3:
                    transposes(2, 1)
                elif g == 5:
                    pe.wait_ge(l1_out, 8)
                    transposes(2, 2)
                pe.wait_ge(ln_lo, 12 + 2 * -(-min((g + 1) * GW, TOK) // CHW) if g != 6 else 18)
                if g >= 3:
                    pe.wait_ge(l1_out, 2 * (g - 3) + 2)
                for half in range(2):
                    for i, (x, w) in enumerate(terms(l13, wcols2(half * L1H, (half + 1) * L1H),
                                                     slice(g * GW, (g + 1) * GW))):
                        last = nc.tensor.matmul(bank[(2 * g + half) % 6][0:GW, 0:L1H], x, w, start=(i == 0),
                                                stop=(i == 4))
                last.then_inc(l1_proj, 1)
                while link < CHAIN_AT[g]:
                    chain(link)
                    link += 1

            def head_T(g):
                j, par = g // 2, g // 2 % 2
                pe.wait_ge(l1_qw, j + 1)
                pe.wait_ge(l1_kw, j + 1)
                if g:
                    pe.wait_ge(l1_Tc, 6 * g)
                for i in range(12):
                    last = nc.tensor.transpose(
                        bank[i // 4][:, (i % 4) * GW:(i % 4 + 1) * GW],
                        (qw, kw)[i // 6][par][:, g % 2, 2 * (i % 6):2 * (i % 6) + 2, :].rearrange(
                            "p a b -> p (a b)"), ident[0:GW, 0:GW])
                    if i % 4 == 3:
                        last.then_inc(l1_T, 1)

            def head_A(g):
                pe.wait_ge(l1_Tc, 6 * g + 6)
                for p in range(6):
                    if g and p % 2 == 0:
                        pe.wait_ge(l1_Am, 3 * (g - 1) + p // 2 + 1)
                    last = nc.tensor.matmul(bank[3 + p // 2][0:GW, (p % 2) * 2 * GW:(p % 2 + 1) * 2 * GW],
                                            kT1[g % 2][:, p, :], qT1[g % 2][:, p, :, :].rearrange("p c q -> p (c q)"),
                                            start=True, stop=True)
                    if p % 2:
                        last.then_inc(l1_A, 1)

            def head_O(g):
                if g:
                    pe.wait_ge(l1_Oc, g)
                else:
                    pe.wait_ge(l1_read, CHAIN_AT[-1])
                for h in range(HEADS):
                    if h % 4 == 0:
                        pe.wait_ge(l1_Am, 3 * g + h // 4 + 1)
                    last = nc.tensor.matmul(bank[6][0:GW, h * HD:(h + 1) * HD], AT[g % 2][:, h, :],
                                            QK[:, g, 3 * D + h * HD:3 * D + (h + 1) * HD], start=True, stop=True)
                last.then_inc(l1_O, 1)

            def head_out(i):
                kind, n, b, used = OUTPUT[i]
                if i == 0:
                    pe.wait_ge(l1_read, len(CHAIN))
                if used is not None:
                    pe.wait_ge({"t": l1_oTc, "f": l1_h}[used[0]], used[1] + 1)
                if kind == "t":
                    pe.wait_ge(l1_on, BATCH_OF[n] + 1)
                    for half in range(2):
                        last = nc.tensor.transpose(bank[b][0:HALF, half * GW:(half + 1) * GW],
                                                   QK[:, n, 2 * D + half * HALF:2 * D + (half + 1) * HALF],
                                                   ident[0:GW, 0:GW])
                    last.then_inc(l1_oT, 1)
                else:
                    if n == 0:
                        pe.wait_ge(ld_wo, 16)
                    pe.wait_ge(l1_oTc, -(-(n + 1) * P // GW))
                    for half in range(2):
                        last = nc.tensor.matmul(bank[b][:, 0:D], OT[:, half, n * P:(n + 1) * P], wo_sb[:, half, :],
                                                start=(half == 0), stop=(half == 1))
                    last.then_inc(l1_f, 1)

            pe.wait_ge(l1_out, 2 * GROUPS)
            head_T(0)
            for g in range(GROUPS):
                outs = OUT_AT.get(g, ())
                if g + 1 < GROUPS:
                    head_T(g + 1)
                for i in outs[0:1]:
                    head_out(i)
                head_A(g)
                for i in outs[1:2]:
                    head_out(i)
                if g:
                    head_O(g - 1)
                for i in outs[2:3]:
                    head_out(i)
                for i in CHAIN_IN[g] if g < len(CHAIN_IN) else ():
                    chain(i)
            head_O(GROUPS - 1)
            transposes(3, 0)
            head_out(7)
            pe.wait_ge(l1_Oc, GROUPS)
            for i in range(8, 14):
                head_out(i)
            transposes(3, 1)
            for i in range(14, 20):
                head_out(i)

            def router1():
                transposes(3, 2)
                pe.wait_ge(ln_lo, 24)
                router(3 * D + E0, E1P, rt1_z)

            pe.wait_ge(ln_lo, 22)
            for n in range(MOE1.works):
                down = moe_pe(pe, MOE1, W1, A1, S1, n, n % 2, n == 0, router1 if n == 0 else None)
            down(E1, E1 % 2, 2)

        @block.scalar
        def _(act):
            def deviations(k, c):
                act.wait_ge(ln_var, 3 * k + c + 1)
                tc = slice(3 * c, 3 * c + 3)
                nc.scalar.activation(sd[:, tc], ve[:, tc], ACT.Sqrt).then_inc(ln_sd, 1)

            def high(k, c):
                act.wait_ge(ln_xt, 3 * k + c + 1)
                cols = slice(c * CHW, (c + 1) * CHW)
                for x, b in zip((X01h, X2h), LN_BANKS[k][c]):
                    nc.scalar.activation(x[:, cols], bank[b][:, 0:CHW], ACT.Copy).then_inc(ln_hi, 1)

            def norm_act(k):
                deviations(k, 0)
                deviations(k, 1)
                high(k, 0)
                deviations(k, 2)
                high(k, 1)
                high(k, 2)

            for s, (wh, w2, n) in enumerate(((WAh, WA2, NWA), (L1h, L12, QKVG))):
                act.wait_ge(ld_stage[s], 16)
                nc.scalar.activation(wh[:], W0[s]["stage"][:, 0:n], ACT.Copy).then_inc(split_hi, 1)
                nc.scalar.activation(w2[:], W0[s]["stage"][:, n:2 * n], ACT.Copy).then_inc(split_hi, 1)
            norm_act(0)
            act.wait_ge(zeroed, 16 * (SLOTS // P * D // ZW))
            for j in range(0, 18, 2):
                act.wait_ge(proj_done, j + 1)
                if j < 12:
                    half, c = (j // 3) % 2, j % 3
                    dst = (qT if j < 6 else kT)[:, half, c * (XW // 3):(c + 1) * (XW // 3)]
                    src = bank[j % 8][0:HALF, 0:XW // 3]
                else:
                    g = 2 * (j - 12)
                    n = min(2, GROUPS - g)
                    dst = V[:, g:g + n, :]
                    src = bank[j % 8][0:GW, 0:n * D].rearrange("p (g d) -> p g d", d=D)
                nc.scalar.activation(dst, src, ACT.Copy).then_inc(proj_out[0], 1)
            for b, (g0, g1) in enumerate(BATCHES):
                act.wait_ge(a0_shift, b + 1)
                nc.scalar.activation(Pm[:, g0:g1, :], Pm[:, g0:g1, :], ACT.Exp,
                                     scale=float(D) ** -0.5).then_inc(a0_exp, 1)
            for b, (g0, g1) in enumerate(BATCHES):
                act.wait_ge(a0_pt, b + 1)
                nc.scalar.activation(PT[:, g0:g1, :], bank[5 + b][0:GW, 0:(g1 - g0) * GW].rearrange(
                    "p (g q) -> p g q", q=GW), ACT.Copy).then_inc(a0_ptc, 1)
            for b, (g0, g1) in enumerate(BATCHES):
                act.wait_ge(a0_o, 2 * b + 1)
                nc.scalar.activation(oT[:, 0, g0 * GW:g1 * GW], bank[2 * b][0:HALF, 0:(g1 - g0) * GW],
                                     ACT.Copy).then_inc(a0_oc[0], 1)
            for i in range(4):
                e_split_act(act, 0, 0, i, 32, None)
            norm_act(1)
            def softplus():
                act.wait_ge(rt_neg, 1)
                nc.scalar.activation(rt[1][:], rt[1][:], ACT.Exp).then_inc(rt_e, 1)
                act.wait_ge(rt_u, 1)
                nc.scalar.activation(rt[3][:], rt[2][:], ACT.Ln).then_inc(rt_ln, 1)
                act.wait_ge(rt_sp, 1)
                nc.scalar.activation(rt[4][:], rt[3][:], ACT.Sqrt).then_inc(rt_sc, 1)

            e_act(act, 0, CHW, None, None, None, {2: softplus})
            e_act(act, 1, CHW, None, None, None)
            e_act(act, 2, CHW, None, None, None)
            for n in (1, 2):
                for i in range(4):
                    e_split_act(act, n, n % 2, i, 16 * n + 16, None if n == 1 else 2)
            act.wait_ge(x_T, 1)
            nc.scalar.activation(XWh[1][:], bank[6][:], ACT.Copy).then_inc(x_hi, 1)
            e_act(act, 3, WT, None, (2, 0, None), None)
            e_act(act, 4, WT, (3, 1, 48, 4), (3, 1, 24), None)
            e_act(act, 5, WT, (4, 0, 64, 5), (4, 0, 30), (1, 1))
            e_act(act, 6, WT, (5, 1, 64, 6), (5, 1, 36), (2, 0))
            with act.Fori(0, (WORKS - 6) // 2, 1) as i:
                e_act(act, i * 2 + 7, WT, (i * 2 + 6, 0, i * 16 + 80, i * 2 + 7), (i * 2 + 6, 0, i * 12 + 42),
                      (i * 2 + 3, 1))
                e_act(act, i * 2 + 8, WT, (i * 2 + 7, 1, i * 16 + 80, i * 2 + 8), (i * 2 + 7, 1, i * 12 + 48),
                      (i * 2 + 4, 0))
            e_act(act, WORKS + 1, WT, (WORKS, 0, 8 * WORKS + 32, WORKS + 1), (WORKS, 0, FC0 * (WORKS + 1)),
                  (WORKS - 3, 1))
            e_act(act, WORKS + 2, WT, None, None, (WORKS - 2, 0))
            e_store(act, WORKS - 1, 1)
            e_store(act, WORKS, 0)
            act.wait_ge(l1_tau, 1)
            nc.scalar.activation(tau[:], tau[:], ACT.Exp).then_inc(l1_tau, 1)

            def project(g):
                act.wait_ge(l1_proj, g + 1)
                for half in range(2):
                    nc.scalar.activation(QK[:, g, half * L1H:(half + 1) * L1H],
                                         bank[(2 * g + half) % 6][0:GW, 0:L1H], ACT.Copy).then_inc(l1_out, 1)

            def exps(b):
                g0, g1 = BATCHES[b]
                act.wait_ge(l1_out, 2 * g1)
                nc.scalar.activation(EG[:, g0:g1, :], QK[:, g0:g1, 4 * D:QKVG], ACT.Exp, scale=-1.0).then_inc(l1_eg, 1)
                act.wait_ge(l1_read, CHAIN.index(("st", b)) + 1)
                cols = slice(g0 * GW, g1 * GW)
                nc.scalar.activation(sT[:, cols], sT[:, cols], ACT.Exp).then_inc(l1_ex, 1)

            def squares(j):
                g0, g1 = PAIRS[j]
                act.wait_ge(l1_rope, j + 1)
                nc.scalar.activation(rotA[j % 2][:, 0:g1 - g0, :], QK[:, g0:g1, 0:2 * D],
                                     ACT.Square).then_inc(l1_sq, 1)

            def roots(j):
                n = PAIRS[j][1] - PAIRS[j][0]
                act.wait_ge(l1_n2, j + 1)
                nc.scalar.activation(nrm[j % 2][:, 0:n, :], nrm[j % 2][:, 0:n, :], ACT.Sqrt).then_inc(l1_nr, 1)

            def head_copies(g):
                if g >= 2:
                    act.wait_ge(l1_A, 3 * (g - 1))
                elif g == 0:
                    act.wait_ge(l1_zero, 3)
                q, k = qT1[g % 2], kT1[g % 2]
                act.wait_ge(l1_T, 3 * g + 1)
                src = bank[0][:, 0:4 * GW].rearrange("p (i q) -> p i q", q=GW)
                for c in range(2):
                    ps = slice(64 * c, 64 * c + 64)
                    nc.scalar.activation(q[ps, 0:4, c, :], src[ps], ACT.Copy).then_inc(l1_Tc, 1)
                act.wait_ge(l1_T, 3 * g + 2)
                src = bank[1][:, 0:4 * GW].rearrange("p (i q) -> p i q", q=GW)
                for c in range(2):
                    ps = slice(64 * c, 64 * c + 64)
                    nc.scalar.activation(q[ps, 4:6, c, :], src[ps, 0:2], ACT.Copy).then_inc(l1_Tc, 1)
                nc.scalar.activation(k[:, 0:2, :], src[:, 2:4], ACT.Copy).then_inc(l1_Tc, 1)
                act.wait_ge(l1_T, 3 * g + 3)
                src = bank[2][:, 0:4 * GW].rearrange("p (i q) -> p i q", q=GW)
                nc.scalar.activation(k[:, 2:6, :], src, ACT.Copy).then_inc(l1_Tc, 1)

            def output_copy(g):
                act.wait_ge(l1_O, g + 1)
                nc.scalar.activation(QK[:, g, 2 * D:3 * D], bank[6][0:GW, 0:D], ACT.Copy).then_inc(l1_Oc, 1)

            def centred_squares(b):
                g0, g1 = BATCHES[b]
                act.wait_ge(l1_cen, b + 1)
                nc.scalar.activation(W1b[:, g0:g1, :], QK[:, g0:g1, 2 * D:3 * D], ACT.Square).then_inc(l1_csq, 1)

            def head_deviations(b):
                g0, g1 = BATCHES[b]
                act.wait_ge(l1_var, b + 1)
                nc.scalar.activation(HV[:, g0:g1], HV[:, g0:g1], ACT.Sqrt).then_inc(l1_std, 1)

            def out_copies(steps):
                for i in steps:
                    kind, g, b, _ = OUTPUT[i]
                    if kind == "t":
                        act.wait_ge(l1_oT, g + 1)
                        w = min(GW, TOK - g * GW)
                        src = bank[b][0:HALF, 0:2 * GW].rearrange("p (h q) -> p h q", h=2)[:, :, 0:w]
                        nc.scalar.activation(OT[:, :, g * GW:g * GW + w], src, ACT.Copy).then_inc(l1_oTc, 1)

            deviations(2, 0)
            high(2, 0)
            deviations(2, 1)
            for g in range(3):
                project(g)
            high(2, 1)
            deviations(2, 2)
            project(3)
            high(2, 2)
            for g in range(4, 7):
                project(g)
            exps(0)
            squares(0)
            for g in range(7, 10):
                project(g)
            exps(1)
            project(10)
            squares(1)
            roots(0)
            roots(1)
            head_copies(0)
            for g in range(GROUPS):
                outs = OUT_AT.get(g, ())
                if g in (6, 10):
                    head_deviations(g // 4 - 1)
                if g + 1 < GROUPS:
                    head_copies(g + 1)
                out_copies(outs[0:2])
                if g:
                    output_copy(g - 1)
                out_copies(outs[2:3])
                if g in (5, 9):
                    centred_squares(g // 4 - 1)
                if g == 3:
                    exps(2)
                j = g // 2 + 2
                if j < len(PAIRS):
                    (roots if g % 2 else squares)(j)
                for i in (g,) if g < GROUPS - 1 else (g, g + 1):
                    moe_weights_act(act, MOE1, W1, S1, ld_stage1, i // 6, i // 6, i % 6, None, 16)
            deviations(3, 0)
            output_copy(GROUPS - 1)
            centred_squares(2)
            head_deviations(2)
            high(3, 0)
            out_copies(range(7, 14))
            deviations(3, 1)
            high(3, 1)
            out_copies(range(14, 20))
            deviations(3, 2)

            def sigmoids():
                high(3, 2)
                act.wait_ge(rt1_b, 1)
                nc.scalar.activation(rt[4][:, 0:TILES * E1], rt[0][:, 0:TILES * E1], ACT.Sigmoid).then_inc(rt1_p, 1)

            for n in range(MOE1.works):
                moe_act(act, MOE1, W1, A1, S1, ld_stage1, n, n % 2, n == 0, n in (0, E1), 32,
                        sigmoids if n == 0 else None)
            moe_high(act, MOE1, A1, S1, E1, E1 % 2, 3 * MOE1.fc - 1)

        @block.gpsimd
        def _(pool):
            nc.gpsimd.memset(zero[:], 0.0).then_inc(zero_set, 1)
            for x in (X01h, X01l, X2h, X2l):
                nc.gpsimd.memset(x[:, TOK:XW].bitcast(F32), 0.0).then_inc(pads, 1)
            for s, (st, wh, wl, w2, n) in enumerate(((0, WAh, WAl, WA2, NWA), (1, L1h, L1l, L12, QKVG))):
                stage = W0[st]["stage"]
                pool.wait_ge(split_hi, 2 * s + 1)
                pool.wait_ge(*((split_lo, 2 * s) if s else (pads, 4)))
                nc.gpsimd.tensor_tensor(wl[:], stage[:, 0:n], wh[:].bitcast(F32), ALU.subtract).then_inc(split_lo, 1)
                pool.wait_ge(split_hi, 2 * s + 2)
                pool.wait_ge(split_lo, 2 * s + 1)
                nc.gpsimd.tensor_tensor(w2[64:P, :], stage[64:P, n:2 * n], w2[64:P, :].bitcast(F32),
                                        ALU.subtract).then_inc(split_lo, 1)
            pool.wait_ge(split_lo, 4)
            e_split_low(nc.gpsimd, pool, 0, 0)
            pool.wait_ge(zeroed, 16 * (SLOTS // P * D // ZW))
            pool.wait_ge(r_idx, 1)
            pool.wait_ge(S0["w_lo"], 4)
            for t in range(TILES):
                for j in range(PICKS):
                    nc.gpsimd.indirect_dma_start(
                        out=xs, out_offset=bass.IndirectOffsetOnAxis(ap=idx[:, j, t:t + 1], axis=0),
                        in_=Y[:, t, 0:D], in_offset=None).then_inc(scattered, 16)
            pool.wait_ge(scattered, 16 * PICKS * TILES)
            e_split_low(nc.gpsimd, pool, 2, 0)
            with pool.Fori(0, (WORKS - 4) // 2, 1) as i:
                e_split_low(nc.gpsimd, pool, i * 2 + 3, 1)
                e_split_low(nc.gpsimd, pool, i * 2 + 4, 0)
            e_split_low(nc.gpsimd, pool, WORKS - 1, 1)
            e_split_low(nc.gpsimd, pool, WORKS, 0)
            for par in range(2):
                pool.wait_ge(st_y[par], 8 * WORKS)
            for t in range(TILES):
                for j in range(PICKS):
                    nc.gpsimd.indirect_dma_start(
                        out=G[:, t, j, :], out_offset=None, in_=ys.rearrange("w s d -> (w s) d"),
                        in_offset=bass.IndirectOffsetOnAxis(ap=idx[:, j, t:t + 1], axis=0)).then_inc(ld_g[t // 3], 16)
            for c in range(CH):
                pool.wait_ge(ld_g[c], 16 * PICKS * 3)
            pool.wait_ge(ln_var, 3 * CH)
            nc.gpsimd.memset(qkw[:], 0.0).then_inc(l1_zero, 1)
            pool.wait_ge(l1_zero, 1)

            def rotate(j):
                g0, g1 = PAIRS[j]
                n, hh = g1 - g0, HD // 2
                pool.wait_ge(l1_out, 2 * g1)
                src = QK[:, g0:g1, 0:2 * D].rearrange("p g (h d) -> p g h d", d=HD)
                B4 = rotB[j % 2][:, 0:n, :].rearrange("p g (h d) -> p g h d", d=HD)
                for i in range(2):
                    a, b = i * hh, (1 - i) * hh
                    table = const[0:GW, C_SIN + a:C_SIN + a + hh].unsqueeze(1).unsqueeze(1)
                    nc.gpsimd.tensor_tensor(B4[:, :, :, a:a + hh], src[:, :, :, b:b + hh],
                                            table.to_broadcast([GW, n, 2 * HEADS, hh]), ALU.mult).then_inc(l1_rb, 1)
                pool.wait_ge(l1_rb, 2 * j + 2)
                pool.wait_ge(l1_ra, j + 1)
                nc.gpsimd.tensor_tensor(QK[:, g0:g1, 0:2 * D], rotA[j % 2][:, 0:n, :], rotB[j % 2][:, 0:n, :],
                                        ALU.add).then_inc(l1_rope, 1)

            def widen_keys(j):
                g0, g1 = PAIRS[j]
                n = g1 - g0
                pool.wait_ge(l1_ck, j + 1)
                if j >= 2:
                    pool.wait_ge(l1_T, 6 * (j - 1))
                for i in range(3):
                    f = CK[j % 2][:, i, 0:n, :] if i < 2 else rn[j % 2][:, 0:n, HEADS:2 * HEADS]
                    last = nc.gpsimd.tensor_tensor(
                        kw[j % 2][:, 0:n, :, i * HD:(i + 1) * HD],
                        QK[:, g0:g1, D:2 * D].rearrange("p g (h d) -> p g h d", d=HD),
                        f.unsqueeze(3).to_broadcast([GW, n, HEADS, HD]), ALU.mult)
                    last.then_inc(l1_kw if i == 2 else pool_step, 1)

            def head_norm(b, ready, factor, op, done):
                g0, g1 = BATCHES[b]
                pool.wait_ge(ready, b + 1)
                O = QK[:, g0:g1, 2 * D:3 * D].rearrange("p g (h d) -> p g h d", d=HD)
                nc.gpsimd.tensor_tensor(O, O, factor[:, g0:g1].unsqueeze(3).to_broadcast([GW, g1 - g0, HEADS, HD]),
                                        op).then_inc(done, 1)
                pool.wait_ge(done, b + 1)

            rotate(0)
            rotate(1)
            pool.wait_ge(l1_proj, GROUPS)
            pool.wait_ge(l1_rope, 2)
            for c in range(2):
                zeros = XB[64 * c:64 * c + 64, 0:2 * W2].rearrange("p (i c q) -> p i c q", c=2, q=GW)[:, :, 1 - c, :]
                nc.gpsimd.memset(zeros, 0.0).then_inc(l1_zero, 1)
                pool.wait_ge(l1_zero, 2 + c)
            widen_keys(0)
            for g in range(GROUPS):
                j = g // 2 + 2
                if g in (6, 10):
                    head_norm(g // 4 - 1, l1_hr, HR, ALU.mult, l1_on)
                if g % 2 == 0:
                    if j - 1 < len(PAIRS):
                        widen_keys(j - 1)
                    if j < len(PAIRS):
                        rotate(j)
                if g in (5, 9):
                    head_norm(g // 4 - 1, l1_mu, HM, ALU.subtract, l1_cen)
                pool.wait_ge(l1_kw, min(g // 2 + 2, len(PAIRS)))
                pool.wait_ge(l1_rope, min(g // 2 + 3, len(PAIRS)))
                for i in (g,) if g < GROUPS - 1 else (g, g + 1):
                    moe_weights_pool(pool, MOE1, W1, S1, i // 6, i // 6, (i % 6,))
                pool.wait_ge(S1["w_lo"], i + 1)
            head_norm(2, l1_mu, HM, ALU.subtract, l1_cen)
            head_norm(2, l1_hr, HR, ALU.mult, l1_on)
            for n in range(2, MOE1.works):
                moe_weights_pool(pool, MOE1, W1, S1, n, n % 2)

        @block.vector
        def _(dve):
            own = Steps(dve, dve_step)

            def statistics(k, c):
                for t in range(3 * c, 3 * c + 3):
                    own.step(nc.vector.bn_stats(stat[:, t, :], H[:, t, :]))
                own.settle()
                for t in range(3 * c, 3 * c + 3):
                    own.step(nc.vector.bn_aggr(mv[:, t, :], stat[:, t, :]))
                own.settle()
                nc.vector.tensor_scalar(ve[:, 3 * c:3 * c + 3], mv[:, 3 * c:3 * c + 3, 1], EPS, None,
                                        ALU.add).then_inc(ln_var, 1)

            def normal(k, c):
                tc = slice(3 * c, 3 * c + 3)
                dve.wait_ge(ln_sd, 3 * k + c + 1)
                own.link(nc.vector.reciprocal(rstd[:, tc], sd[:, tc]))
                for t in range(3 * c, 3 * c + 3):
                    own.step(nc.vector.tensor_scalar(Y[:, t, 0:D], H[:, t, :], mv[:, t, 0:1], rstd[:, t:t + 1],
                                                     ALU.subtract, ALU.mult))
                own.settle()
                nc.vector.tensor_copy(Y[:, tc, D:256], Y[:, tc, P:D]).then_inc(ln_y, 1)

            def low(k, c):
                cols = slice(c * CHW, (c + 1) * CHW)
                for i, (xl, xh) in enumerate(((X01l, X01h), (X2l, X2h))):
                    dve.wait_ge(ln_hi, 6 * k + 2 * c + i + 1)
                    nc.vector.tensor_tensor(xl[:, cols], bank[LN_BANKS[k][c][i]][:, 0:CHW],
                                            xh[:, cols].bitcast(F32), ALU.subtract).then_inc(ln_lo, 1)

            def norm(k, ready, paced=False):
                ready(0)
                statistics(k, 0)
                if paced:
                    normal(k, 0)
                ready(1)
                statistics(k, 1)
                if paced:
                    low(k, 0)
                    normal(k, 1)
                else:
                    normal(k, 0)
                ready(2)
                statistics(k, 2)
                if paced:
                    low(k, 1)
                else:
                    normal(k, 1)
                    low(k, 0)
                normal(k, 2)
                if not paced:
                    low(k, 1)
                low(k, 2)

            def compare(keys, E):
                shape = [P, TILES, E, E]
                r = keys.rearrange("p (t e) -> p t e", e=E)
                other, mine = r.unsqueeze(2).to_broadcast(shape), r.unsqueeze(3).to_broadcast(shape)
                k0 = rk[0][:, 0:TILES * E * E].rearrange("p (t e j) -> p t e j", e=E, j=E)
                k1 = rk[1][:, 0:TILES * E * E].rearrange("p (t e j) -> p t e j", e=E, j=E)
                low = const[:, C_LOW:C_LOW + E0 * E0].rearrange("p (e j) -> p e j", j=E0)[:, 0:E, 0:E]
                own.step(nc.vector.tensor_tensor(k0, other, mine, ALU.is_gt))
                own.link(nc.vector.tensor_tensor(k1, other, mine, ALU.is_equal))
                own.link(nc.vector.tensor_tensor(k1, k1, low.unsqueeze(1).to_broadcast(shape), ALU.mult))
                own.link(nc.vector.tensor_tensor(k0, k0, k1, ALU.add))
                own.link(nc.vector.tensor_reduce(rt[5][:, 0:TILES * E].rearrange("p (t e) -> p t e", e=E), k0, AX.X,
                                                 ALU.add))

            def share(sc, E, comb_out, clip):
                rnk = rt[5][:, 0:TILES * E]
                own.link(nc.vector.scalar_tensor_tensor(out=rnk, in0=rnk, scalar=1.5, in1=sc, op0=ALU.is_lt,
                                                        op1=ALU.mult))
                own.link(nc.vector.tensor_reduce(rsum[0][:], rnk.rearrange("p (t e) -> p t e", e=E), AX.X, ALU.add))
                if clip:
                    own.link(nc.vector.tensor_scalar(rsum[0][:], rsum[0][:], 1e-6, None, ALU.max))
                own.link(nc.vector.reciprocal(rsum[1][:], rsum[0][:]))
                own.link(nc.vector.tensor_tensor(comb_out, rnk.rearrange("p (t e) -> p t e", e=E),
                                                 rsum[1][:].unsqueeze(2).to_broadcast([P, TILES, E]), ALU.mult))

            def tiles2(t0, t1):
                return H[:, t0:t1, :]

            def pair(b, t0, t1):
                return bank[b][:, 0:(t1 - t0) * D].rearrange("p (t d) -> p t d", d=D)

            dve.wait_ge(ld_row, 16)
            bias = row[:, R_TOKB:R_TOKB + D].unsqueeze(1)

            def chunk_of(block):
                def ready(c):
                    for j in ((0, 1), (2,), (3, 4))[c]:
                        block(j, *PBLK[j])
                    own.settle()
                return ready

            def embedded(j, t0, t1):
                dve.wait_ge(tok_done, j + 1)
                own.step(nc.vector.tensor_tensor(tiles2(t0, t1), pair(j, t0, t1),
                                                 bias.to_broadcast([P, t1 - t0, D]), ALU.add))

            norm(0, chunk_of(embedded))

            dve.wait_ge(ld_const, 16)
            dve.wait_ge(zeroed, 16 * (SLOTS // P * D // ZW))
            for j in range(1, 18, 2):
                dve.wait_ge(proj_done, j + 1)
                if j < 12:
                    half, c = (j // 3) % 2, j % 3
                    dst = (qT if j < 6 else kT)[:, half, c * (XW // 3):(c + 1) * (XW // 3)]
                    src = bank[j % 8][0:HALF, 0:XW // 3]
                else:
                    g = 2 * (j - 12)
                    n = min(2, GROUPS - g)
                    dst = V[:, g:g + n, :]
                    src = bank[j % 8][0:GW, 0:n * D].rearrange("p (g d) -> p g d", d=D)
                nc.vector.tensor_copy(dst, src).then_inc(proj_out[1], 1)
            for b, (g0, g1) in enumerate(BATCHES):
                n = g1 - g0
                dve.wait_ge(a0_s, b + 1)
                pm = Pm[:, g0:g1, :]
                own.link(nc.vector.tensor_tensor(
                    pm, bank[2 + b][0:GW, 0:n * GW].rearrange("p (g q) -> p g q", q=GW),
                    amask.unsqueeze(1).to_broadcast([GW, n, GW]), ALU.add))
                own.link(nc.vector.tensor_reduce(mx[:, g0:g1], pm, AX.X, ALU.max))
                nc.vector.tensor_tensor(pm, pm, mx[:, g0:g1].unsqueeze(2).to_broadcast([GW, n, GW]),
                                        ALU.subtract).then_inc(a0_shift, 1)
            for b, (g0, g1) in enumerate(BATCHES):
                n = g1 - g0
                dve.wait_ge(a0_exp, b + 1)
                pm = Pm[:, g0:g1, :]
                own.link(nc.vector.tensor_reduce(rs[:, g0:g1], pm, AX.X, ALU.add))
                own.link(nc.vector.reciprocal(rr[:, g0:g1], rs[:, g0:g1]))
                nc.vector.tensor_tensor(pm, pm, rr[:, g0:g1].unsqueeze(2).to_broadcast([GW, n, GW]),
                                        ALU.mult).then_inc(a0_p, 1)
            for b, (g0, g1) in enumerate(BATCHES):
                dve.wait_ge(a0_o, 2 * b + 2)
                nc.vector.tensor_copy(oT[:, 1, g0 * GW:g1 * GW],
                                      bank[2 * b + 1][0:HALF, 0:(g1 - g0) * GW]).then_inc(a0_oc[1], 1)

            def attended(j, t0, t1):
                dve.wait_ge(a0_back, j + 1)
                own.step(nc.vector.tensor_tensor(tiles2(t0, t1), pair((6 + j) % 8, t0, t1), tiles2(t0, t1), ALU.add))

            norm(1, chunk_of(attended))

            z, e, u, l, sc = (rt[i][:] for i in range(5))

            def scores():
                dve.wait_ge(rt_z, 1)
                own.link(nc.vector.tensor_copy(z, bank[6][:, 0:TILES * E0]))
                nc.vector.scalar_tensor_tensor(out=e, in0=z, scalar=-1.0, in1=z, op0=ALU.mult,
                                               op1=ALU.min).then_inc(rt_neg, 1)
                dve.wait_ge(rt_e, 1)
                nc.vector.tensor_scalar(u, e, 1.0, None, ALU.add).then_inc(rt_u, 1)
                dve.wait_ge(rt_u, 1)
                own.step(nc.vector.scalar_tensor_tensor(out=e, in0=u, scalar=1.0, in1=e, op0=ALU.subtract,
                                                        op1=ALU.subtract))
                own.link(nc.vector.reciprocal(sc, u))
                own.link(nc.vector.tensor_tensor(e, e, sc, ALU.mult))
                dve.wait_ge(rt_ln, 1)
                own.link(nc.vector.tensor_tensor(l, l, e, ALU.subtract))
                nc.vector.scalar_tensor_tensor(out=l, in0=z, scalar=0.0, in1=l, op0=ALU.max,
                                               op1=ALU.add).then_inc(rt_sp, 1)
                dve.wait_ge(rt_sc, 1)
                own.link(nc.vector.tensor_tensor(
                    u.rearrange("p (t e) -> p t e", e=E0), sc.rearrange("p (t e) -> p t e", e=E0),
                    row[:, R_GB:R_GB + E0].unsqueeze(1).to_broadcast([P, TILES, E0]), ALU.add))

            def choose():
                nc.vector.tensor_scalar(sel[:], rt[5][:], 1.5, None, ALU.is_lt).then_inc(r_own, 1)
                dve.wait_ge(r_own, 1)
                own.link(nc.vector.tensor_scalar(selsum[:, 0:E0], sel[:, 0:E0], 0.0, None, ALU.mult))
                for t in range(TILES):
                    ins = nc.vector.tensor_tensor(selsum[:, (t + 1) * E0:(t + 2) * E0], selsum[:, t * E0:(t + 1) * E0],
                                                  sel[:, t * E0:(t + 1) * E0], ALU.add)
                    if t < TILES - 1:
                        own.link(ins)
                    else:
                        ins.then_inc(r_sel, 1)


            def te(x):
                return x.rearrange("p (t e) -> p t e", e=E0)

            ee = [P, E0, E0]
            lower = const[:, C_LOW:C_LOW + E0 * E0].rearrange("p (e j) -> p e j", j=E0)

            def bases():
                dve.wait_ge(r_pos, 1)
                own.link(nc.vector.tensor_copy(count[:], bank[7][:, TILES * E0:(TILES + 1) * E0]))
                k0 = rk[0][:, 0:E0 * FULL].rearrange("p (e k) -> p e k", k=FULL)
                own.link(nc.vector.tensor_tensor(
                    k0, count[:].unsqueeze(2).to_broadcast([P, E0, FULL]),
                    const[:, C_FULL:C_FULL + FULL].unsqueeze(1).to_broadcast([P, E0, FULL]), ALU.is_gt))
                own.link(nc.vector.tensor_reduce(works[:], k0, AX.X, ALU.add))
                k1 = rk[1][:, 0:E0 * E0].rearrange("p (e j) -> p e j", j=E0)
                own.link(nc.vector.tensor_tensor(k1, lower, works[:].unsqueeze(1).to_broadcast(ee), ALU.mult))
                own.link(nc.vector.tensor_reduce(base[:], k1, AX.X, ALU.add))
                own.link(nc.vector.tensor_scalar(count[:], base[:], float(WT), 1.0, ALU.mult, ALU.add))

            def slots():
                own.link(nc.vector.tensor_tensor(te(slot[:]), te(bank[7][:, 0:TILES * E0]),
                                                 count[:].unsqueeze(1).to_broadcast([P, TILES, E0]), ALU.add))
                own.link(nc.vector.tensor_tensor(slot[:], slot[:], sel[:], ALU.mult))
                own.step(nc.vector.tensor_reduce(smx[:], te(slot[:]), AX.X, ALU.max))
                own.link(nc.vector.tensor_reduce(smn[:], te(slot[:]), AX.X, ALU.add))
                own.link(nc.vector.tensor_tensor(smn[:], smn[:], smx[:], ALU.subtract))
                own.step(nc.vector.tensor_scalar(idx[:, 0, :], smx[:], -1.0, None, ALU.add))
                own.settle()
                nc.vector.tensor_scalar(idx[:, 1, :], smn[:], -1.0, None, ALU.add).then_inc(r_idx, 1)

            def experts():
                own.link(nc.vector.tensor_tensor(works[:], works[:], base[:], ALU.add))
                k0 = rk[0][:, 0:WORKS * E0].rearrange("p (k e) -> p k e", e=E0)
                own.link(nc.vector.tensor_tensor(
                    k0, const[:, C_WORK:C_WORK + WORKS].unsqueeze(2).to_broadcast([P, WORKS, E0]),
                    works[:].unsqueeze(1).to_broadcast([P, WORKS, E0]), ALU.is_ge))
                own.link(nc.vector.tensor_reduce(eidf[:], k0, AX.X, ALU.add))
                nc.vector.tensor_scalar(eid[:], eidf[:], 1.0, float(E0), ALU.add, ALU.min).then_inc(r_eid, 1)

            def weights():
                own.link(nc.vector.tensor_tensor(te(rt[0][:]), te(slot[:]), smx[:].unsqueeze(2).to_broadcast(
                    [P, TILES, E0]), ALU.is_equal))
                own.link(nc.vector.tensor_tensor(te(rt[0][:]), te(rt[0][:]), comb[:], ALU.mult))
                own.step(nc.vector.tensor_reduce(wpick[:, 0, :], te(rt[0][:]), AX.X, ALU.add))
                own.link(nc.vector.tensor_tensor(te(rt[1][:]), comb[:], te(rt[0][:]), ALU.subtract))
                own.link(nc.vector.tensor_reduce(wpick[:, 1, :], te(rt[1][:]), AX.X, ALU.add))

            e_dve(dve, 0, 0, CHW, None, None, None, {2: scores, 3: lambda: compare(u, E0), 4: choose})
            e_dve(dve, 1, 1, CHW, None, None, lambda: e_acc(dve, 0),
                  {2: bases, 3: slots, 4: experts})
            e_dve(dve, 2, 0, CHW, 3, None, lambda: e_acc(dve, 1), {0: lambda: share(sc, E0, comb[:], True), 1: weights})
            e_split_low(nc.vector, dve, 1, 1)
            e_acc(dve, 2)
            dve.wait_ge(x_hi, 1)
            nc.vector.tensor_tensor(XWl[1][:], bank[6][:], XWh[1][:].bitcast(F32), ALU.subtract).then_inc(x_lo, 1)
            e_dve(dve, 3, 1, WT, 6, (2, 0), None)
            e_dve(dve, 4, 0, WT, 9, (3, 1), lambda: e_copy(dve, 1, 1, None))
            e_dve(dve, 5, 1, WT, 11, (4, 0), lambda: e_copy(dve, 2, 0, None))
            e_dve(dve, 6, 0, WT, 13, (5, 1), lambda: e_copy(dve, 3, 1, 16))
            with dve.Fori(0, (WORKS - 6) // 2, 1) as i:
                e_dve(dve, i * 2 + 7, 1, WT, i * 4 + 15, (i * 2 + 6, 0), lambda: e_copy(dve, i * 2 + 4, 0, i * 16 + 16))
                e_dve(dve, i * 2 + 8, 0, WT, i * 4 + 17, (i * 2 + 7, 1), lambda: e_copy(dve, i * 2 + 5, 1, i * 16 + 32))
            e_dve(dve, WORKS + 1, 1, WT, 2 * WORKS + 3, (WORKS, 0), lambda: e_copy(dve, WORKS - 2, 0, 8 * WORKS - 32))
            e_dve(dve, WORKS + 2, 0, WT, 2 * WORKS + 5, None, lambda: e_copy(dve, WORKS - 1, 1, 8 * WORKS - 16))
            e_copy(dve, WORKS, 0, 8 * WORKS - 16)

            t_col, inv_t, neg_inv_t = (const[0:GW, c:c + 1] for c in (C_T, C_RT, C_NRT))
            nc.vector.tensor_scalar(tau[:], row[0:GW, R_TAU:R_TAU + HEADS], -50.0, 30.0, ALU.max,
                                    ALU.min).then_inc(l1_tau, 1)
            dve.wait_ge(l1_tau, 2)
            own.step(nc.vector.tensor_tensor(tmu[:].rearrange("p (h d) -> p h d", d=HD),
                                             row[0:GW, R_MU:R_MU + D].rearrange("p (h d) -> p h d", d=HD),
                                             tau[:].unsqueeze(2).to_broadcast([GW, HEADS, HD]), ALU.mult))
            own.link(nc.vector.tensor_scalar(tden[:], tau[:], t_col, None, ALU.add))
            own.link(nc.vector.reciprocal(tau[:], tden[:]))
            own.link(nc.vector.tensor_scalar(tden[:], tau[:], -1.0 / float(HD) ** 0.5, None, ALU.mult))

            def mixture(c):
                dve.wait_ge(ld_g[c], 16 * PICKS * 3)
                for j in range(PICKS):
                    for t in range(3 * c, 3 * c + 3):
                        own.step(nc.vector.scalar_tensor_tensor(
                            out=H[:, t, :], in0=G[:, t, j, :], scalar=wpick[:, j, t:t + 1], in1=H[:, t, :],
                            op0=ALU.mult, op1=ALU.add))
                    own.settle()

            norm(2, mixture, paced=True)

            def gw(ap):
                return ap.rearrange("p g (h d) -> p g h d", d=HD)

            def chain(i):
                kind, j = CHAIN[i]
                b = bank[CHAIN_BANK[i]]
                g0, g1 = (PAIRS if kind == "us" else BATCHES)[j]
                n = g1 - g0
                dve.wait_ge(l1_chain, i + 1)
                if kind == "us":
                    w = W1b[:, g0:g1, :]
                    nc.vector.tensor_tensor(w, b[0:GW, 0:n * D].rearrange("p (g d) -> p g d", d=D),
                                            tmu[:].unsqueeze(1).to_broadcast([GW, n, D]),
                                            ALU.add).then_inc(l1_read, 1)
                    dve.wait_ge(l1_read, i + 1)
                    own.link(nc.vector.tensor_tensor(w, w, QK[:, g0:g1, 2 * D:3 * D], ALU.mult))
                    own.link(nc.vector.tensor_reduce(UB[:, g0:g1], gw(w), AX.X, ALU.add))
                    nc.vector.tensor_tensor(ES[:, g0:g1, HEADS:2 * HEADS], UB[:, g0:g1],
                                            tden[:].unsqueeze(1).to_broadcast([GW, n, HEADS]),
                                            ALU.mult).then_inc(l1_s, 1)
                elif kind == "st":
                    src = b[0:HEADS, 0:n * GW].rearrange("p (i s) -> p i s", s=SEQ)
                    m = smax[:, g0 * GI:g1 * GI]
                    own.link(nc.vector.tensor_reduce(m, src, AX.X, ALU.max))
                    nc.vector.tensor_tensor(
                        sT[:, g0 * GW:g1 * GW].rearrange("p (i s) -> p i s", s=SEQ), src,
                        m.unsqueeze(2).to_broadcast([HEADS, n * GI, SEQ]), ALU.subtract).then_inc(l1_read, 1)
                elif kind == "et":
                    nc.vector.tensor_copy(ES[:, g0:g1, 0:HEADS], b[0:GW, 0:n * HEADS].rearrange(
                        "p (g h) -> p g h", h=HEADS)).then_inc(l1_read, 1)
                else:
                    cum = b[0:GW, 0:n * 2 * HEADS].rearrange("p (g h) -> p g h", h=2 * HEADS)
                    al, be, ga = (CO[:, k, g0:g1] for k in range(3))
                    sg = SG[:, g0:g1, :]
                    s1, sh = sg[:, :, 0:HEADS], sg[:, :, HEADS:2 * HEADS]
                    dve.wait_ge(l1_eg, j + 1)
                    own.link(nc.vector.tensor_scalar(EG[:, g0:g1, :], EG[:, g0:g1, :], 1.0, None, ALU.add))
                    own.step(nc.vector.reciprocal(sg, EG[:, g0:g1, :]))
                    own.link(nc.vector.tensor_scalar(ga, cum[:, :, 0:HEADS], 1e-12, None, ALU.add))
                    own.step(nc.vector.reciprocal(al, ga))
                    own.link(nc.vector.tensor_tensor(be, s1, sh, ALU.subtract))
                    own.step(nc.vector.tensor_tensor(al, al, sh, ALU.mult))
                    own.link(nc.vector.tensor_scalar(be, be, inv_t, None, ALU.mult))
                    nc.vector.tensor_tensor(ga, cum[:, :, HEADS:2 * HEADS], be, ALU.mult).then_inc(l1_read, 1)
                    dve.wait_ge(l1_read, i + 1)
                    own.link(nc.vector.tensor_tensor(ga, ga, sh, ALU.add))
                    own.link(nc.vector.tensor_scalar(ga, ga, neg_inv_t, None, ALU.mult))

            def cosines(j):
                g0, g1 = PAIRS[j]
                n = g1 - g0
                dve.wait_ge(l1_out, 2 * g1)
                table = const[0:GW, C_COS:C_COS + HD].unsqueeze(1).unsqueeze(1)
                nc.vector.tensor_tensor(gw(rotA[j % 2][:, 0:n, :]), gw(QK[:, g0:g1, 0:2 * D]),
                                        table.to_broadcast([GW, n, 2 * HEADS, HD]), ALU.mult).then_inc(l1_ra, 1)

            def norms(j):
                n = PAIRS[j][1] - PAIRS[j][0]
                dve.wait_ge(l1_sq, j + 1)
                nc.vector.tensor_reduce(nrm[j % 2][:, 0:n, :], gw(rotA[j % 2][:, 0:n, :]), AX.X,
                                        ALU.add).then_inc(l1_n2, 1)

            def widen_queries(j):
                g0, g1 = PAIRS[j]
                n, o = g1 - g0, j % 2
                dve.wait_ge(l1_s, j + 1)
                dve.wait_ge(l1_read, CHAIN.index(("cum", BATCH_OF[g0])) + 1)
                dve.wait_ge(l1_nr, j + 1)
                own.link(nc.vector.tensor_scalar(nrm[o][:, 0:n, :], nrm[o][:, 0:n, :], 1e-12, None, ALU.max))
                if j >= 2:
                    dve.wait_ge(l1_kw, j - 1)
                own.link(nc.vector.reciprocal(rn[o][:, 0:n, :], nrm[o][:, 0:n, :]))
                own.step(nc.vector.tensor_tensor(CK[o][:, 0, 0:n, :], ES[:, g0:g1, 0:HEADS],
                                                 rn[o][:, 0:n, HEADS:2 * HEADS], ALU.mult))
                nc.vector.tensor_tensor(CK[o][:, 1, 0:n, :], ES[:, g0:g1, HEADS:2 * HEADS],
                                        rn[o][:, 0:n, HEADS:2 * HEADS], ALU.mult).then_inc(l1_ck, 1)
                for i in range(3):
                    own.step(nc.vector.tensor_tensor(CQ[o][:, i, 0:n, :], CO[:, i, g0:g1, :], rn[o][:, 0:n, 0:HEADS],
                                                     ALU.mult))
                own.settle()
                if j >= 2:
                    dve.wait_ge(l1_T, 6 * (j - 1))
                else:
                    dve.wait_ge(l1_zero, 1)
                for i in range(3):
                    ins = nc.vector.tensor_tensor(
                        qw[o][:, 0:n, :, i * HD:(i + 1) * HD], gw(QK[:, g0:g1, 0:D]),
                        CQ[o][:, i, 0:n, :].unsqueeze(3).to_broadcast([GW, n, HEADS, HD]), ALU.mult)
                    if i < 2:
                        own.step(ins)
                    else:
                        ins.then_inc(l1_qw, 1)

            def masks(g):
                if g >= 2:
                    dve.wait_ge(l1_O, g - 1)
                for k in range(3):
                    dve.wait_ge(l1_A, 3 * g + k + 1)
                    nc.vector.tensor_tensor(
                        AT[g % 2][:, 4 * k:4 * k + 4, :], bank[3 + k][0:GW, 0:4 * GW].rearrange(
                            "p (h q) -> p h q", q=GW),
                        tri.unsqueeze(1).to_broadcast([GW, 4, GW]), ALU.mult).then_inc(l1_Am, 1)

            def head_means(b):
                g0, g1 = BATCHES[b]
                dve.wait_ge(l1_Oc, g1)
                own.link(nc.vector.tensor_reduce(HM[:, g0:g1], gw(QK[:, g0:g1, 2 * D:3 * D]), AX.X, ALU.add))
                nc.vector.tensor_scalar(HM[:, g0:g1], HM[:, g0:g1], 1.0 / HD, None, ALU.mult).then_inc(l1_mu, 1)

            def head_variances(b):
                g0, g1 = BATCHES[b]
                dve.wait_ge(l1_csq, b + 1)
                own.link(nc.vector.tensor_reduce(HR[:, g0:g1], gw(W1b[:, g0:g1, :]), AX.X, ALU.add))
                nc.vector.tensor_scalar(HV[:, g0:g1], HR[:, g0:g1], 1.0 / HD, EPS, ALU.mult,
                                        ALU.add).then_inc(l1_var, 1)

            def head_factors(b):
                g0, g1 = BATCHES[b]
                dve.wait_ge(l1_std, b + 1)
                nc.vector.reciprocal(HR[:, g0:g1], HV[:, g0:g1]).then_inc(l1_hr, 1)

            def add_outputs(steps):
                for i in steps:
                    kind, t, b, _ = OUTPUT[i]
                    if kind == "f":
                        dve.wait_ge(l1_f, t + 1)
                        nc.vector.tensor_tensor(H[:, t, :], bank[b][:, 0:D], H[:, t, :], ALU.add).then_inc(l1_h, 1)

            for i in range(2):
                chain(i)
            cosines(0)
            for i in range(2, 7):
                chain(i)
            cosines(1)
            norms(0)
            for i in range(7, 10):
                chain(i)
            norms(1)
            widen_queries(0)
            for g in range(GROUPS):
                j = g // 2 + 2
                if g in (6, 10):
                    head_factors(g // 4 - 1)
                if g in (5, 9):
                    head_means(g // 4 - 1)
                if g % 2 == 0 and j - 1 < len(PAIRS):
                    widen_queries(j - 1)
                if j < len(PAIRS):
                    (norms if g % 2 else cosines)(j)
                masks(g)
                for i in CHAIN_IN[g] if g < len(CHAIN_IN) else ():
                    chain(i)
                add_outputs(OUT_AT.get(g, ()))
                if g in (5, 9):
                    head_variances(g // 4 - 1)
            dve.wait_ge(l1_h, 3)
            statistics(3, 0)
            head_means(2)
            normal(3, 0)
            head_variances(2)
            head_factors(2)
            low(3, 0)
            add_outputs(range(7, 14))
            dve.wait_ge(l1_h, 6)
            statistics(3, 1)
            normal(3, 1)
            low(3, 1)
            add_outputs(range(14, 20))
            dve.wait_ge(l1_h, 9)
            statistics(3, 2)
            normal(3, 2)

            def router1():
                low(3, 2)
                dve.wait_ge(rt1_z, 1)
                n1 = TILES * E1
                z3 = rt[0][:, 0:n1]
                nc.vector.tensor_tensor(
                    z3.rearrange("p (t e) -> p t e", e=E1),
                    bank[6][:, 0:TILES * E1P].rearrange("p (t e) -> p t e", e=E1P)[:, :, 0:E1],
                    row[:, R_RB:R_RB + E1].unsqueeze(1).to_broadcast([P, TILES, E1]), ALU.add).then_inc(rt1_b, 1)
                dve.wait_ge(rt1_p, 1)
                compare(rt[4][:, 0:n1], E1)
                share(rt[4][:, 0:n1], E1, comb1[:], False)

            def weight1(n):
                return (lambda tile: comb1[:, tile, n - 1:n]) if n else None

            for n in range(MOE1.works):
                moe_dve(dve, MOE1, A1, S1, n, n % 2, n == 0, weight1(n), weight1(n - 1) if n else None,
                        router1 if n == 0 else None)
            moe_low(dve, MOE1, A1, S1, E1, E1 % 2, 3 * MOE1.fc - 1)
            moe_acc(dve, MOE1, S1, E1, 2, weight1(E1))


def moe_buffers(sb, scope, m, name):
    out = {}
    for key, shape, dt in (("s", [P, CHW], F32), ("hf", [P, CHW], F32),
                           ("hh", [P, m.fc, CHW], F32R), ("hl", [P, m.fc, CHW], F32R)):
        out[key] = [sb(f"{name}{key}{b}", shape, dt, scope) for b in range(2)]
    return out


def kernel(**inputs):
    import numpy as np
    import concourse.bacc as bacc
    from concourse.bass_utils import run_bass_kernel_spmd as run

    a = {k: np.asarray(v) for k, v in inputs.items()}

    def two(w):
        return np.concatenate([w[:P], np.concatenate([w[P:], w[P:]], axis=0)], axis=1)

    side = SIDE // PATCH
    x = a["x"].reshape(IMAGES, CHANNELS, side, PATCH, side, PATCH).transpose(0, 1, 2, 4, 3, 5)
    x = x.reshape(TOK, PATCH_K, P).transpose(2, 1, 0)
    x = np.concatenate([x[:, :, j:min(j + 2 * P, TOK)].reshape(P, -1) for j in range(0, TOK, 2 * P)], axis=1)
    tokw = a["L0_tok_W"].T.reshape(PATCH_K, P, D).transpose(1, 0, 2)

    consts = np.zeros((P, NCONST), np.float32)
    consts[:, C_ID:C_ID + P] = np.eye(P)
    i = np.arange(GW)
    same = (i[:, None] // SEQ) == (i[None, :] // SEQ)
    consts[:GW, C_MASK:C_MASK + GW] = np.where(same, 0.0, -1e30)
    consts[:GW, C_TRI:C_TRI + GW] = same & (i[:, None] <= i[None, :])
    inv = np.float32(1.0) / np.float32(10000.0) ** (np.arange(0, HD, 2, dtype=np.float32) / np.float32(HD))
    ang = (i % SEQ).astype(np.float32)[:, None] * inv[None, :]
    consts[:GW, C_COS:C_COS + HD] = np.repeat(np.cos(ang), 2, axis=1)
    consts[:GW, C_SIN:C_SIN + HD] = np.repeat(np.sin(ang), 2, axis=1) * np.where(np.arange(HD) < HD // 2, -1, 1)
    t = (i % SEQ + 1).astype(np.float32)
    consts[:GW, C_T], consts[:GW, C_RT], consts[:GW, C_NRT] = t, 1 / t, -1 / t
    e = np.arange(E0)
    consts[:, C_LOW:C_LOW + E0 * E0] = (e[None, :] < e[:, None]).astype(np.float32).reshape(1, -1)
    p = np.arange(P)
    consts[:, C_BEFORE:C_BEFORE + P] = p[:, None] < p[None, :]
    consts[:, C_ONE:C_ONE + P] = 1.0
    consts[:, C_FULL:C_FULL + FULL] = WT * np.arange(FULL)
    consts[:, C_WORK:C_WORK + WORKS] = np.arange(WORKS)

    vec = np.concatenate([a["L0_tok_b"], a["L0_ffn_gate_bias"], a["L1_ffn_routing_bias"], np.zeros(1, np.float32),
                          a["L1_attn_prior_mu"].reshape(-1), a["L1_attn_prior_log_tau"].reshape(-1)])
    rows = np.broadcast_to(vec[None, :], (P, NROWS))

    wa = two(np.concatenate([a["L0_attn_W_q"], a["L0_attn_W_k"], a["L0_attn_W_v"], a["L0_ffn_gate_w"],
                             a["L1_ffn_router_w"], np.zeros((D, 1), np.float32)], axis=1))
    wg = a["L1_attn_Wg"].reshape(HEADS, 3, D)
    l1w = two(np.concatenate([a["L1_attn_Wq"].T, a["L1_attn_Wk"].T, a["L1_attn_Wu"].T, a["L1_attn_Wv"].T,
                              wg[:, 0].T, wg[:, 1].T], axis=1))
    wo = a["L1_attn_Wo"].T.reshape(2, HALF, D).transpose(1, 0, 2)

    def expert(gate, up, down, m):
        return np.concatenate([two(gate), two(up), down.reshape(m.fc, P, D).transpose(1, 0, 2).reshape(P, -1)], axis=1)

    moe0 = [expert(a["L0_ffn_w1s"], a["L0_ffn_w3s"], a["L0_ffn_w2s"], MOE0)]
    moe0 += [expert(a["L0_ffn_w1"][j], a["L0_ffn_w3"][j], a["L0_ffn_w2"][j], MOE0) for j in range(E0)]
    moe1 = [expert(a["L1_ffn_shared_gate"], a["L1_ffn_shared_up"], a["L1_ffn_shared_down"], MOE1)]
    moe1 += [expert(a["L1_ffn_routed_gate"][j], a["L1_ffn_routed_up"][j], a["L1_ffn_routed_down"][j], MOE1)
             for j in range(E1)]

    arrays = {"patches": x, "tokw": tokw, "consts": consts, "rows": rows, "wa": wa, "l1w": l1w, "wo": wo,
              "moe0w": np.stack(moe0)[:, :, :4 * F0], "moe0d": np.stack(moe0)[:, :, 4 * F0:], "moe1w": np.stack(moe1)}
    arrays = {k: np.ascontiguousarray(v, dtype=np.float32) for k, v in arrays.items()}
    nc = bacc.Bacc("TRN2", target_bir_lowering=False, num_devices=1)
    args = [nc.dram_tensor(k, v.shape, F32, kind="ExternalInput").ap() for k, v in arrays.items()]
    out = nc.dram_tensor("out", (TOK, D), F32, kind="ExternalOutput").ap()
    xs = nc.dram_tensor("slots_in", (SLOTS, D), F32, kind="Internal").ap()
    ys = nc.dram_tensor("slots_out", (WORKS, WT, D), F32, kind="Internal").ap()
    tower(nc, *args, xs, ys, out)
    got = run(nc, [arrays], core_ids=[0]).results[0]["out"]
    return got.reshape(IMAGES, SEQ, D)
```
